# Optimizing a Trainium2 kernel written in Bass

```python
import numpy as np
import jax
import jax.numpy as jnp

def _softmax(x, axis=-1):
    return jax.nn.softmax(x, axis=axis)

def _gelu(x):
    return jax.nn.gelu(x, approximate=True)

def _silu(x):
    return jax.nn.silu(x)

def _sigmoid(x):
    return jax.nn.sigmoid(x)

def _layernorm(x, axis=-1, eps=1e-05):
    m = jnp.mean(x, axis=axis, keepdims=True)
    v = jnp.var(x, axis=axis, keepdims=True)
    return (x - m) / jnp.sqrt(v + eps)

def _scatter_add(tgt, idx, src, axis=0):
    return tgt.at[idx].add(src)

def _segment_sum(src, seg, n):
    return jax.ops.segment_sum(src, seg, n)
kernel_name = 'mk_gnn_resnorm_d4_gnn_r64_6c329b'

def setup_inputs(seed: int=0):
    np.random.seed(seed)
    _w = jnp.asarray

    def _rec_inputs():
        import jax
        import jax.numpy as jnp
        _gk = jax.random.key(seed)
        x = -0.0002117 + 1 * jax.random.normal(jax.random.fold_in(_gk, 1), (100000, 256), jnp.float32)
        src = jax.random.randint(jax.random.fold_in(_gk, 2), (25000,), 0, 100000, jnp.int32)
        dst = jnp.minimum((100000 * jax.random.uniform(jax.random.fold_in(_gk, 3), (25000,)) ** 2.0).astype(jnp.int32), 99999)
        _o = jnp.argsort(dst, stable=True)
        src = src[_o]
        dst = dst[_o]
        edge_weight = jax.random.uniform(jax.random.fold_in(_gk, 13), (25000,), jnp.float32, 0.0, 1)
        return (x, src, dst, edge_weight)
    x, src, dst, edge_weight = _rec_inputs()

    def _L0_gnn_setup():
        import jax, jax.numpy as jnp
        import numpy as np
        N = 100000
        E = 50000
        D_IN = 256
        D_OUT = 256
        key = jax.random.key(seed)
        kx, ke1, ke2, kw = jax.random.split(key, 4)
        X = jax.random.normal(kx, (N, D_IN), dtype=jnp.float32)
        src = jax.random.randint(ke1, (E,), 0, N, dtype=jnp.int64)
        dst = jax.random.randint(ke2, (E,), 0, N, dtype=jnp.int64)
        dst = jnp.where(src == dst, (dst + 1) % N, dst)
        edge_index = jnp.stack([src, dst], axis=0)
        W = jax.random.normal(kw, (D_IN, D_OUT), dtype=jnp.float32) * (1.0 / np.sqrt(D_IN))
        return {'X': X, 'edge_index': edge_index, 'W': W}
    _L0_gnn_all = _L0_gnn_setup()
    _L0_gnn_in = {k: v for k, v in _L0_gnn_all.items() if k in ('W',)}
    del _L0_gnn_all

    def _L1_gnn_setup():
        import jax, jax.numpy as jnp
        import numpy as np
        N_NODES = 100000
        N_EDGES = 50000
        D = 256
        LN_EPS = 1e-05

        def _spmm(edge_row, edge_col, edge_vals, feats):
            msgs = edge_vals[:, None] * feats[edge_col]
            return jax.ops.segment_sum(msgs, edge_row, num_segments=N_NODES)

        def _layernorm(h, gamma, beta):
            mu = jnp.mean(h, axis=-1, keepdims=True)
            var = jnp.mean(jnp.square(h - mu), axis=-1, keepdims=True)
            return (h - mu) * jax.lax.rsqrt(var + LN_EPS) * gamma + beta
        key = jax.random.key(seed)
        ks = jax.random.split(key, 8)
        x = jax.random.normal(ks[0], (N_NODES, D), dtype=jnp.float32)
        edge_row = jax.random.randint(ks[1], (N_EDGES,), 0, N_NODES, dtype=jnp.int32)
        edge_col = jax.random.randint(ks[2], (N_EDGES,), 0, N_NODES, dtype=jnp.int32)
        edge_vals = jax.random.uniform(ks[3], (N_EDGES,), dtype=jnp.float32)
        stdv = 1.0 / np.sqrt(D)
        W = jax.random.uniform(ks[4], (D, D), minval=-stdv, maxval=stdv, dtype=jnp.float32)
        b = jax.random.uniform(ks[5], (D,), minval=-stdv, maxval=stdv, dtype=jnp.float32)
        ln_gamma = jnp.ones((D,), dtype=jnp.float32)
        ln_beta = jnp.zeros((D,), dtype=jnp.float32)
        res_W = jax.random.uniform(ks[6], (D, D), minval=-stdv, maxval=stdv, dtype=jnp.float32)
        res_b = jax.random.uniform(ks[7], (D,), minval=-stdv, maxval=stdv, dtype=jnp.float32)
        return {'x': x, 'edge_row': edge_row, 'edge_col': edge_col, 'edge_vals': edge_vals, 'W': W, 'b': b, 'ln_gamma': ln_gamma, 'ln_beta': ln_beta, 'res_W': res_W, 'res_b': res_b}
    _L1_gnn_all = _L1_gnn_setup()
    _L1_gnn_in = {k: v for k, v in _L1_gnn_all.items() if k in ('W', 'b', 'ln_gamma', 'ln_beta', 'res_W', 'res_b')}
    del _L1_gnn_all

    def _L2_gnn_setup():
        import jax, jax.numpy as jnp
        import numpy as np
        N_NODES = 100000
        N_EDGES = 5000
        DIM = 256
        BN_EPS = 1e-05
        key = jax.random.key(seed)
        k1, k2, k3 = jax.random.split(key, 3)
        x = jax.random.normal(k1, (N_NODES, DIM), dtype=jnp.float32)
        W = jax.random.normal(k2, (DIM, DIM), dtype=jnp.float32) * (1.0 / np.sqrt(DIM))
        b = jnp.zeros((DIM,), dtype=jnp.float32)
        gamma = jnp.ones((DIM,), dtype=jnp.float32)
        beta = jnp.zeros((DIM,), dtype=jnp.float32)
        edge_index = jax.random.randint(k3, (2, N_EDGES), 0, N_NODES, dtype=jnp.int64)
        return {'x': x, 'W': W, 'b': b, 'gamma': gamma, 'beta': beta, 'edge_index': edge_index}
    _L2_gnn_all = _L2_gnn_setup()
    _L2_gnn_in = {k: v for k, v in _L2_gnn_all.items() if k in ('W', 'b', 'gamma', 'beta')}
    del _L2_gnn_all

    def _L3_gnn_setup():
        import jax, jax.numpy as jnp
        import numpy as np
        N_NODES = 50000
        N_EDGES = 25000
        H_SIZE = 256
        HEADS = 8
        HEAD_DIM = H_SIZE // HEADS
        NEG_SLOPE = 0.2
        key = jax.random.key(seed)
        k_x, k_e, k_w, k_as, k_ad, k_b = jax.random.split(key, 6)
        x = jax.random.normal(k_x, (N_NODES, H_SIZE), dtype=jnp.float32)
        edge_index = jax.random.randint(k_e, (2, N_EDGES), 0, N_NODES, dtype=jnp.int64)
        scale = 1.0 / np.sqrt(H_SIZE)
        W = jax.random.normal(k_w, (H_SIZE, HEADS, HEAD_DIM), dtype=jnp.float32) * scale
        att_src = jax.random.normal(k_as, (HEADS, HEAD_DIM), dtype=jnp.float32) * scale
        att_dst = jax.random.normal(k_ad, (HEADS, HEAD_DIM), dtype=jnp.float32) * scale
        bias = jnp.zeros((H_SIZE,), dtype=jnp.float32)
        return {'x': x, 'edge_index': edge_index, 'W': W, 'att_src': att_src, 'att_dst': att_dst, 'bias': bias}
    _L3_gnn_all = _L3_gnn_setup()
    _L3_gnn_in = {k: v for k, v in _L3_gnn_all.items() if k in ('W', 'att_src', 'att_dst', 'bias')}
    del _L3_gnn_all
    return {'x': x, 'src': src, 'dst': dst, 'edge_weight': edge_weight, 'L0_gnn_W': _L0_gnn_in['W'], 'L1_gnn_W': _L1_gnn_in['W'], 'L1_gnn_b': _L1_gnn_in['b'], 'L1_gnn_ln_gamma': _L1_gnn_in['ln_gamma'], 'L1_gnn_ln_beta': _L1_gnn_in['ln_beta'], 'L1_gnn_res_W': _L1_gnn_in['res_W'], 'L1_gnn_res_b': _L1_gnn_in['res_b'], 'L2_gnn_W': _L2_gnn_in['W'], 'L2_gnn_b': _L2_gnn_in['b'], 'L2_gnn_gamma': _L2_gnn_in['gamma'], 'L2_gnn_beta': _L2_gnn_in['beta'], 'L3_gnn_W': _L3_gnn_in['W'], 'L3_gnn_att_src': _L3_gnn_in['att_src'], 'L3_gnn_att_dst': _L3_gnn_in['att_dst'], 'L3_gnn_bias': _L3_gnn_in['bias']}

def reference(x, src, dst, edge_weight, L0_gnn_W, L1_gnn_W, L1_gnn_b, L1_gnn_ln_gamma, L1_gnn_ln_beta, L1_gnn_res_W, L1_gnn_res_b, L2_gnn_W, L2_gnn_b, L2_gnn_gamma, L2_gnn_beta, L3_gnn_W, L3_gnn_att_src, L3_gnn_att_dst, L3_gnn_bias):
    import jax
    import jax.numpy as jnp

    def _L0_gnn_ref(X, edge_index, W):
        import jax, jax.numpy as jnp
        import numpy as np
        N = 100000
        E = 50000
        D_IN = 256
        D_OUT = 256
        loop = jnp.arange(N, dtype=edge_index.dtype)
        row = jnp.concatenate([edge_index[0], loop])
        col = jnp.concatenate([edge_index[1], loop])
        vals = jnp.ones(row.shape[0], dtype=X.dtype)
        deg = jax.ops.segment_sum(vals, row, num_segments=N)
        dinv = jnp.where(deg > 0, deg ** (-0.5), 0.0)
        norm = vals * dinv[col] * dinv[col]
        agg = jax.ops.segment_sum(norm[:, None] * X[col], row, num_segments=N)
        return agg @ W

    def _L1_gnn_ref(x, edge_row, edge_col, edge_vals, W, b, ln_gamma, ln_beta, res_W, res_b):
        import jax, jax.numpy as jnp
        import numpy as np
        N_NODES = 100000
        N_EDGES = 50000
        D = 256
        LN_EPS = 1e-05

        def _spmm(edge_row, edge_col, edge_vals, feats):
            msgs = edge_vals[:, None] * feats[edge_col]
            return jax.ops.segment_sum(msgs, edge_row, num_segments=N_NODES)

        def _layernorm(h, gamma, beta):
            mu = jnp.mean(h, axis=-1, keepdims=True)
            var = jnp.mean(jnp.square(h - mu), axis=-1, keepdims=True)
            return (h - mu) * jax.lax.rsqrt(var + LN_EPS) * gamma + beta
        support = x @ W.T + b
        out = _spmm(edge_row, edge_col, edge_vals, support)
        out = _layernorm(out, ln_gamma, ln_beta)
        out = jax.nn.relu(out)
        out = out + (x @ res_W.T + res_b)
        return out

    def _L2_gnn_ref(x, W, b, gamma, beta, edge_index):
        import jax, jax.numpy as jnp
        import numpy as np
        N_NODES = 100000
        N_EDGES = 5000
        DIM = 256
        BN_EPS = 1e-05
        N = x.shape[0]
        loop = jnp.arange(N, dtype=edge_index.dtype)
        row = jnp.concatenate([edge_index[0], loop])
        col = jnp.concatenate([edge_index[1], loop])
        deg = jax.ops.segment_sum(jnp.ones_like(col, dtype=x.dtype), col, num_segments=N)
        dinv = jax.lax.rsqrt(deg)
        norm = dinv[row] * dinv[col]
        h = x @ W
        msg = h[row] * norm[:, None]
        out = jax.ops.segment_sum(msg, col, num_segments=N) + b
        mean = jnp.mean(out, axis=0)
        var = jnp.var(out, axis=0)
        out = (out - mean) * jax.lax.rsqrt(var + BN_EPS) * gamma + beta
        return jnp.tanh(out)

    def _L3_gnn_ref(x, edge_index, W, att_src, att_dst, bias):
        import jax, jax.numpy as jnp
        import numpy as np
        N_NODES = 50000
        N_EDGES = 25000
        H_SIZE = 256
        HEADS = 8
        HEAD_DIM = H_SIZE // HEADS
        NEG_SLOPE = 0.2
        'GATConv (concat heads) -> relu -> dropout(eval=identity).\n\n            x: [N, F]; edge_index: [2, E] with (src=row0, dst=row1) meaning message j->i.\n            '
        N = x.shape[0]
        h = jnp.einsum('nf,fhd->nhd', x, W)
        a_src = jnp.sum(h * att_src, axis=-1)
        a_dst = jnp.sum(h * att_dst, axis=-1)
        src = edge_index[0]
        dst = edge_index[1]
        e = jax.nn.leaky_relu(a_src[src] + a_dst[dst], NEG_SLOPE)
        e_max = jax.ops.segment_max(e, dst, num_segments=N)
        e_exp = jnp.exp(e - e_max[dst])
        denom = jax.ops.segment_sum(e_exp, dst, num_segments=N)
        alpha = e_exp / (denom[dst] + 1e-16)
        msg = h[src] * alpha[:, :, None]
        out = jax.ops.segment_sum(msg, dst, num_segments=N)
        out = out.reshape(N, -1) + bias
        return jax.nn.relu(out)
    edge_index = jnp.stack([src, dst])
    x = _layernorm(x + _L0_gnn_ref(x, edge_index, L0_gnn_W), axis=-1)
    x = _layernorm(x + _L1_gnn_ref(x, src, dst, edge_weight, L1_gnn_W, L1_gnn_b, L1_gnn_ln_gamma, L1_gnn_ln_beta, L1_gnn_res_W, L1_gnn_res_b), axis=-1)
    x = _layernorm(x + _L2_gnn_ref(x, L2_gnn_W, L2_gnn_b, L2_gnn_gamma, L2_gnn_beta, edge_index), axis=-1)
    x = _layernorm(x + _L3_gnn_ref(x, edge_index, L3_gnn_W, L3_gnn_att_src, L3_gnn_att_dst, L3_gnn_bias), axis=-1)
    return x

_drawn_inputs = setup_inputs


def setup_inputs(seed=0):
    import zlib

    import numpy as np

    out = dict(_drawn_inputs(seed))
    spreads = {'L1_gnn_ln_gamma': (1.0, 0.2),
     'L1_gnn_ln_beta': (0.0, 0.1),
     'L2_gnn_b': (0.0, 0.8),
     'L2_gnn_gamma': (1.0, 0.2),
     'L2_gnn_beta': (0.0, 0.1),
     'L3_gnn_bias': (0.0, 0.1)}
    factors = {'L1_gnn_b': 2.696, 'L3_gnn_att_src': 8.0, 'L3_gnn_att_dst': 8.0}
    for name, (base, spread) in spreads.items():
        noise = np.random.default_rng([zlib.crc32(name.encode()), seed]).standard_normal(out[name].shape)
        drawn = base * np.exp(spread * noise) if base else spread * noise
        out[name] = jnp.asarray(drawn.astype(out[name].dtype))
    for name, factor in factors.items():
        out[name] = (out[name] * factor).astype(out[name].dtype)
    return out
```

```python
from contextlib import ExitStack, contextmanager

import concourse.bass as bass
from concourse import mybir

F32 = mybir.dt.float32
BF16 = mybir.dt.bfloat16
I32 = mybir.dt.int32
ALU = mybir.AluOpType
ACT = mybir.ActivationFunctionType
AX_X = mybir.AxisListType.X

P = 128
D = 256
KB = D // P
EPS = 1e-5

N = 100000
QT = 4
NPP = N // (P * QT) * QT
NQ = NPP // QT
TAIL = (N - P * NPP) // QT
RING = 3
ITERS = NQ // RING

E = 25000
EC = -(-E // P)
EP = P * EC
GT = 7
GI = EC // (2 * GT)
PADKEY = (1 << 17) - 1
SKIP = 1 << 18
DIGITS = ((0, 6), (6, 6), (12, 5))
ND = 64


def ev(q, mul=1, add=0):
    i, c, u = q
    return c * mul + add if i is None else i * (u * mul) + (c * mul + add)


def sh(q, k):
    return (q[0], q[1] + k, q[2])


def slot(q):
    return q[1] % q[2]


def nth(q, mul=1, add=0):
    i, c, u = q
    return c // u * mul + add if i is None else i * mul + (c // u * mul + add)


def inside(q, lo, hi):
    return q[0] is not None or lo <= q[1] <= hi


def wait(eng, sem, value):
    if type(value) is not int or value > 0:
        eng.wait_ge(sem, value)


def rows(q):
    return TAIL if q[0] is None and q[1] == NQ else P


def value(eng, v):
    return v if type(v) is int else eng.snap(v)


def quad_of(table, q, at=None):
    if rows(q) == TAIL:
        return table[P * NPP:N, :].rearrange("(p j) d -> p (j d)", j=QT)
    return table[0:P * NPP, :].rearrange("(p n) d -> p (n d)", n=NPP)[:, bass.ds(ev(q, QT * D) if at is None else at, QT * D)]


def steps(eng, step, first, last, cuts=(), at_cut=None, ring=RING):
    iters = NQ // ring
    for c in range(first, 2 * ring):
        step((None, c, ring))
    edges = [2] + list(cuts) + [iters - 1]
    for n in range(len(edges) - 1):
        if n >= 1:
            at_cut(n - 1, edges[n])
        with eng.Fori(edges[n], edges[n + 1]) as i:
            for u in range(ring):
                step((i, u, ring))
    for c in range(ring * (iters - 1), last + 1):
        step((None, c, ring))


FIX = 4 * GI


def tile0(q):
    i, c, _ = q
    at = c // 4 * 2 * GT + c % 4 // 2 * GT + c % 2 * 4
    return at if i is None else i * (2 * GT) + at


def ntiles(q):
    if q[0] is None and q[1] >= FIX:
        return 1
    return 4 - q[1] % 2


def half(q):
    return q[1] % 4 // 2


def landed(q, per):
    if q[0] is None and q[1] >= FIX:
        return 16 * per * (GI * GT + 1)
    c = 16 * per * GT * (q[1] // 4 + 1)
    return c if q[0] is None else q[0] * (16 * per * GT) + c


def loads(q):
    c = 16 * (q[1] // 4 + 1)
    return c if q[0] is None else q[0] * 16 + c


def chunks(eng, step, last):
    for c in range(8):
        step((None, c, 4))
    with eng.Fori(2, GI) as i:
        for u in range(4):
            step((i, u, 4))
    for c in range(FIX, last + 1):
        step((None, c, 4))


def groups(eng, step, last):
    for g in range(4):
        step((None, g, 2))
    with eng.Fori(2, GI) as i:
        for u in range(2):
            step((i, u, 2))
    for g in range(2 * GI, last + 1):
        step((None, g, 2))


def group_tiles(q):
    return 1 if q[0] is None and q[1] >= 2 * GI else GT


def build(nc, x, src, dst, ew, w0, w1, b1, g1, be1, wr, br, w2, b2, g2, be2, w3, as3, ad3, b3, out):
    ctx = ExitStack()
    with ctx:
        def sb(name, shape, dt=F32, scope=ctx):
            return scope.enter_context(nc.sbuf_tensor(name, shape, dt))

        def pb(name, shape, dt=F32, scope=ctx):
            return scope.enter_context(nc.psum_tensor(name, shape, dt))

        taken = []

        def sem(name):
            taken.append(nc.alloc_semaphore(name=name))
            return taken[-1]

        @contextmanager
        def phase():
            with ExitStack() as scope:
                yield scope
            nc.clear_and_free_semaphores(list(taken))
            nc.all_engine_barrier()
            taken.clear()

        def dram(name, shape, dt=F32):
            return nc.dram_tensor(name, shape, dt, kind="Internal").ap()

        x1 = dram("x1", [N, D])
        x2 = dram("x2", [N, D])
        x3 = dram("x3", [N, D])
        sorted_src = dram("sorted_src", [EP + 2, 4], I32)
        sorted_dst = dram("sorted_dst", [EP + 2, 4], I32)
        rec_dram = (sorted_src, sorted_dst)

        ident = sb("ident", [P, P])
        ones = sb("ones", [P, P])
        before = sb("before", [P, P])
        eps = sb("eps", [P, 1])
        W0 = sb("W0", [P, KB, D])
        WrT = sb("WrT", [P, KB, D])
        W1T = sb("W1T", [P, KB, D])
        W2 = sb("W2", [P, KB, D])
        c1 = sb("c1", [P, D])
        vec = sb("vec", [P, 8, D])
        B1, G1, BE1, BR, B2, G2, BE2, B3 = (vec[:, k, :] for k in range(8))
        c3 = sb("c3", [P, D])
        rec = [sb(f"rec{k}", [P, EC, 4], I32) for k in range(2)]

        with phase() as scope:
            raw = sb("raw", [P, 2, KB, D], F32, scope)
            srow = sb("srow", [1, 2, 4], I32, scope)
            cols = sb("cols", [P, 3, EC], I32, scope)
            psw = [pb(f"psw{k}", [P, KB, D], F32, scope) for k in range(2)]
            s_const, s_ld, s_raw, s_fill, s_tw, s_sent, s_cols, s_id = map(sem, (
                "s_const", "s_ld", "s_raw", "s_fill", "s_tw", "s_sent", "s_cols", "s_id"))
            block = scope.enter_context(nc.Block())

            @block.sync
            def _(sp):
                sp.dma_start(raw[:, 0, :, :], wr.rearrange("(k p) d -> p k d", p=P)).then_inc(s_raw, 16)
                sp.dma_start(raw[:, 1, :, :], w1.rearrange("(k p) d -> p k d", p=P)).then_inc(s_raw, 16)
                sp.dma_start(W0[:, :, :], w0.rearrange("(k p) d -> p k d", p=P)).then_inc(s_ld, 16)
                sp.dma_start(W2[:, :, :], w2.rearrange("(k p) d -> p k d", p=P)).then_inc(s_ld, 16)
                sp.wait_ge(s_fill, 3)
                for k, a in enumerate((src, dst, ew.bitcast(I32))):
                    full = E // EC
                    sp.dma_start(cols[0:full, k, :], a[0:full * EC].rearrange("(p c) -> p c", c=EC)).then_inc(s_cols, 16)
                    sp.dma_start(cols[full:full + 1, k, 0:E - full * EC],
                                 a[full * EC:E].rearrange("(p c) -> p c", p=1)).then_inc(s_cols, 16)
                for k, a in enumerate((b1, g1, be1, br, b2, g2, be2, b3)):
                    sp.dma_start(vec[:, k, :], a.partition_broadcast(P)).then_inc(s_ld, 16)
                sp.wait_ge(s_fill, 5)
                for table in rec_dram:
                    for end in (0, 1):
                        at = end * (EP + 1)
                        sp.dma_start(table[at:at + 1, :], srow[0:1, end, :]).then_inc(s_sent, 16)
                sp.wait_ge(s_sent, 64)
                sp.wait_ge(s_ld, 160)

            @block.gpsimd
            def _(pool):
                for k, fill in ((0, PADKEY), (1, PADKEY), (2, 0)):
                    pool.memset(cols[:, k, :], fill).then_inc(s_fill, 1)
                pool.memset(srow[:, 0, :], -1).then_inc(s_fill, 1)
                pool.memset(srow[:, 1, :], -2).then_inc(s_fill, 1)
                pool.memset(ident[:, :], 0.0).then_inc(s_id, 1)
                pool.memset(before[:, :], 0.0).then_inc(s_id, 1)
                pool.memset(ones[:, :], 1.0).then_inc(s_const, 1)
                pool.memset(eps[:, :], EPS).then_inc(s_const, 1)
                pool.wait_ge(s_id, 2)
                pool.affine_select(out=ident[:, :], in_=ident[:, :], compare_op=ALU.not_equal, fill=1.0, base=0,
                                   pattern=[[-1, P]], channel_multiplier=1).then_inc(s_id, 1)
                pool.affine_select(out=before[:, :], in_=before[:, :], compare_op=ALU.is_ge, fill=1.0, base=0,
                                   pattern=[[-1, P]], channel_multiplier=1).then_inc(s_id, 1)
                pool.wait_ge(s_id, 4)

            @block.tensor
            def _(pe):
                pe.wait_ge(s_raw, 32)
                pe.wait_ge(s_id, 4)
                for m in range(2):
                    for a in range(KB):
                        for b in range(KB):
                            last = nc.tensor.transpose(psw[m][:, b, a * P:(a + 1) * P],
                                                       raw[:, m, a, b * P:(b + 1) * P], ident[:, :])
                    last.then_inc(s_tw, 1)

            @block.vector
            def _(dve):
                for m, to in ((0, WrT), (1, W1T)):
                    dve.wait_ge(s_tw, m + 1)
                    nc.vector.tensor_copy(to[:, :, :], psw[m][:, :, :])
                dve.wait_ge(s_ld, 160)
                nc.vector.scalar_tensor_tensor(out=c1[:, :], in0=BE1, scalar=0.0, in1=BR, op0=ALU.max, op1=ALU.add)
                nc.vector.tensor_scalar(c3[:, :], B3, 0.0, None, ALU.max)
                dve.wait_ge(s_cols, 96)
                for k, order in ((0, (0, 1, 2)), (1, (1, 0, 2))):
                    for f in range(3):
                        nc.vector.tensor_copy(rec[k][:, :, f], cols[:, order[f], :])
                for k in range(2):
                    nc.vector.memset(rec[k][:, :, 3], 0)

        with phase() as scope:
            xin = sb("xin", [P, RING, QT, D], F32, scope)
            xT = sb("xT", [P, RING, KB, QT, P], F32, scope)
            y1 = sb("y1", [P, RING, QT, D], F32, scope)
            y1T = sb("y1T", [P, RING, KB, QT, P], F32, scope)
            y2 = sb("y2", [P, RING, QT, D], F32, scope)
            small = sb("small", [P, 2, RING, 4, QT], F32, scope)
            st = sb("st", [P, 2, RING, QT, 6], F32, scope)
            mv = sb("mv", [P, 2, RING, QT, 2], F32, scope)
            digit = sb("digit", [P, EC], I32, scope)
            digit_f = sb("digit_f", [P, EC], BF16, scope)
            iota_i = sb("iota_i", [P, ND], I32, scope)
            iota_d = sb("iota_d", [P, ND], BF16, scope)
            hot = sb("hot", [P, ND, EC], BF16, scope)
            cum = sb("cum", [P, ND, EC], F32, scope)
            below = sb("below", [P, ND], F32, scope)
            count = sb("count", [P, ND], F32, scope)
            offset = sb("offset", [P, ND], F32, scope)
            rank_f = sb("rank_f", [P, EC], F32, scope)
            rank = [sb(f"rank{k}", [P, EC], I32, scope) for k in range(2)]
            rank_slot = sb("rank_slot", [P, 2, GT], I32, scope)
            rec_slot = sb("rec_slot", [P, 2, GT, 4], I32, scope)
            psT1 = pb("psT1", [P, KB, QT, P], F32, scope)
            psY1 = pb("psY1", [P, QT, D], F32, scope)
            psT2 = pb("psT2", [P, KB, QT, P], F32, scope)
            psY2 = pb("psY2", [P, QT, D], F32, scope)

            s_x = [sem(f"s_x{k}") for k in range(RING)]
            s_st1 = [sem(f"s_st1{k}") for k in range(RING)]
            s_st2 = [sem(f"s_st2{k}") for k in range(RING)]
            s_t = [sem(f"s_t{k}") for k in range(2)]
            s_tc = [sem(f"s_tc{k}") for k in range(2)]
            s_y = [sem(f"s_y{k}") for k in range(2)]
            s_add = [sem(f"s_add{k}") for k in range(2)]
            s_bn = [sem(f"s_bn{k}") for k in range(2)]
            s_mv = [sem(f"s_mv{k}") for k in range(2)]
            s_sd = [sem(f"s_sd{k}") for k in range(2)]
            s_rs = [sem(f"s_rs{k}") for k in range(2)]
            s_nm = [sem(f"s_nm{k}") for k in range(2)]
            s_norm = [sem(f"s_norm{k}") for k in range(2)]
            s_dpass = sem("s_dpass")
            s_spass = sem("s_spass")
            s_res = sem("s_res")
            s_rec = [sem(f"s_rec{k}") for k in range(2)]
            s_iota, s_chain, s_cnt, s_off, s_offr, s_rank, s_slotc, s_pass = map(sem, (
                "s_iota", "s_chain", "s_cnt", "s_off", "s_offr", "s_rank", "s_slotc", "s_pass"))
            s_scat = [sem(f"s_scat{k}") for k in range(2)]
            block = scope.enter_context(nc.Block())
            CUTS = [3, 12, 22, 32, 42, 52]
            LAST = NQ + 2
            buf = (y1, y2)

            @block.sync
            def _(sp):
                def load(q):
                    at, used = value(sp, ev(q, QT * D)), value(sp, ev(q, 1, 1 - RING))
                    wait(sp, s_t[0], used)
                    wait(sp, s_add[0], used)
                    sp.sem_inc(s_spass, 1)
                    sp.dma_start(xin[0:rows(q), slot(q), :, :].rearrange("p j d -> p (j d)"),
                                 quad_of(x, q, at)).then_inc(s_x[slot(q)], 16)

                def store(l, table, q, s_st):
                    at, done = value(sp, ev(q, QT * D)), value(sp, ev(q, 1, 1))
                    sp.wait_ge(s_norm[l], done)
                    sp.sem_inc(s_spass, 1)
                    sp.dma_start(quad_of(table, q, at),
                                 buf[l][0:rows(q), slot(q), :, :].rearrange("p j d -> p (j d)")).then_inc(s_st[slot(q)], 16)

                def step(q):
                    if inside(sh(q, 2), 0, NQ):
                        load(sh(q, 2))
                    if inside(sh(q, -1), 0, NQ):
                        store(0, x1, sh(q, -1), s_st1)
                    if inside(sh(q, -3), 0, NQ):
                        store(1, x2, sh(q, -3), s_st2)

                load((None, 0, RING))
                load((None, 1, RING))
                steps(sp, step, 0, LAST + 1)
                for c in range(RING):
                    sp.wait_ge(s_st1[c], 16 * len(range(c, NQ + 1, RING)))
                    sp.wait_ge(s_st2[c], 16 * len(range(c, NQ + 1, RING)))

            @block.tensor
            def _(pe):
                def transposes(l, of, to, q):
                    for j in range(QT):
                        for k in range(KB):
                            last = nc.tensor.transpose(to[:, k, j, 0:rows(q)], of[0:rows(q), slot(q), j, k * P:(k + 1) * P],
                                                       ident[0:rows(q), 0:rows(q)])
                    last.then_inc(s_t[l], 1)

                def product(l, of, weights, to, q):
                    for j in range(QT):
                        for k in range(KB):
                            last = nc.tensor.matmul(to[0:rows(q), j, :], of[:, slot(q), k, j, 0:rows(q)], weights[:, k, :],
                                                    start=(k == 0), stop=(k == KB - 1))
                    last.then_inc(s_y[l], 1)

                def step(q):
                    nxt, lag = sh(q, 1), sh(q, -2)
                    if inside(nxt, 0, NQ):
                        pe.wait_ge(s_x[slot(nxt)], nth(nxt, 16, 16))
                        wait(pe, s_tc[0], ev(nxt))
                        transposes(0, xin, psT1, nxt)
                    if inside(lag, 0, NQ):
                        pe.wait_ge(s_norm[0], ev(lag, 1, 1))
                        wait(pe, s_tc[1], ev(lag))
                        transposes(1, y1, psT2, lag)
                    if inside(q, 0, NQ):
                        pe.wait_ge(s_tc[0], ev(q, 1, 1))
                        wait(pe, s_add[0], ev(q))
                        product(0, xT, W0, psY1, q)
                    if inside(lag, 0, NQ):
                        pe.wait_ge(s_tc[1], ev(lag, 1, 1))
                        wait(pe, s_res, ev(lag))
                        product(1, y1T, WrT, psY2, lag)

                def sort_offsets(k, i):
                    pe.wait_ge(s_add[0], RING * i)
                    pe.wait_ge(s_cnt, k + 1)
                    nc.tensor.matmul(psY1[:, 0, 0:ND], ones[:, :], below[:, :], start=True, stop=False)
                    nc.tensor.matmul(psY1[:, 0, 0:ND], before[:, :], count[:, :], start=False, stop=True).then_inc(s_off, 1)
                    pe.wait_ge(s_offr, k + 1)

                step((None, -1, RING))
                steps(pe, step, 0, LAST, CUTS, sort_offsets)

            @block.scalar
            def _(act):
                def copy_transposed(l, of, to, q):
                    act.wait_ge(s_t[l], ev(q, 1, 1))
                    wait(act, s_y[l], ev(q, 1, 1 - RING))
                    nc.scalar.activation(to[:, slot(q), :, :, 0:rows(q)], of[:, :, :, 0:rows(q)],
                                         ACT.Copy).then_inc(s_tc[l], 1)

                def deviation(l, q):
                    r, s = rows(q), slot(q)
                    act.wait_ge(s_mv[l], ev(q, 1, 1))
                    nc.scalar.activation(small[0:r, l, s, 0, :], mv[0:r, l, s, :, 1], ACT.Sqrt,
                                         bias=eps[0:r, :]).then_inc(s_sd[l], 1)

                def normalise(l, q):
                    r, s = rows(q), slot(q)
                    act.wait_ge(s_nm[l], ev(q, 1, 1))
                    for j in range(QT):
                        last = nc.scalar.activation(buf[l][0:r, s, j, :], buf[l][0:r, s, j, :], ACT.Identity,
                                                    bias=small[0:r, l, s, 2, j:j + 1], scale=small[0:r, l, s, 1, j:j + 1])
                    last.then_inc(s_norm[l], 1)

                def step(q):
                    nxt, lag = sh(q, 1), sh(q, -2)
                    if inside(nxt, 0, NQ):
                        copy_transposed(0, psT1, xT, nxt)
                    if inside(lag, 0, NQ):
                        copy_transposed(1, psT2, y1T, lag)
                    if inside(q, 0, NQ):
                        deviation(0, q)
                    if inside(lag, 0, NQ):
                        deviation(1, lag)
                    if inside(q, 0, NQ):
                        normalise(0, q)
                    if inside(lag, 0, NQ):
                        normalise(1, lag)

                step((None, -1, RING))
                steps(act, step, 0, LAST)

            @block.vector
            def _(dve):
                def statistics(l, q):
                    r, s = rows(q), slot(q)
                    dve.wait_ge(s_add[l], ev(q, 1, 1))
                    for j in range(QT):
                        last = nc.vector.bn_stats(st[0:r, l, s, j, :], buf[l][0:r, s, j, :])
                    last.then_inc(s_bn[l], 1)
                    dve.wait_ge(s_bn[l], ev(q, 1, 1))
                    dve.sem_inc(s_dpass, 1)
                    for j in range(QT):
                        last = nc.vector.bn_aggr(mv[0:r, l, s, j, :], st[0:r, l, s, j, :])
                    last.then_inc(s_mv[l], 1)

                def reciprocals(l, q):
                    r, s = rows(q), slot(q)
                    dve.wait_ge(s_sd[l], ev(q, 1, 1))
                    nc.vector.reciprocal(small[0:r, l, s, 1, :], small[0:r, l, s, 0, :]).then_inc(s_rs[l], 1)
                    dve.wait_ge(s_rs[l], ev(q, 1, 1))
                    nc.vector.scalar_tensor_tensor(out=small[0:r, l, s, 2, :], in0=mv[0:r, l, s, :, 0], scalar=-1.0,
                                                   in1=small[0:r, l, s, 1, :], op0=ALU.mult, op1=ALU.mult).then_inc(s_nm[l], 1)

                def step(q):
                    lag = sh(q, -2)
                    if inside(q, 0, NQ):
                        r, s = rows(q), slot(q)
                        dve.wait_ge(s_y[0], ev(q, 1, 1))
                        wait(dve, s_st1[s], nth(q, 16))
                        wait(dve, s_t[1], ev(q, 1, 1 - RING))
                        nc.vector.tensor_tensor(y1[0:r, s, :, :], psY1[0:r, :, :], xin[0:r, s, :, :],
                                                ALU.add).then_inc(s_add[0], 1)
                        statistics(0, q)
                    if inside(lag, 0, NQ):
                        r, s = rows(lag), slot(lag)
                        dve.wait_ge(s_y[1], ev(lag, 1, 1))
                        wait(dve, s_st2[s], nth(lag, 16))
                        nc.vector.tensor_tensor(y2[0:r, s, :, :], psY2[0:r, :, :], y1[0:r, s, :, :],
                                                ALU.add).then_inc(s_res, 1)
                        dve.wait_ge(s_res, ev(lag, 1, 1))
                        nc.vector.tensor_tensor(y2[0:r, s, :, :], y2[0:r, s, :, :],
                                                c1[0:r, :].unsqueeze(1).broadcast_to([r, QT, D]), ALU.add).then_inc(s_add[1], 1)
                        statistics(1, lag)
                    if inside(q, 0, NQ):
                        reciprocals(0, q)
                    if inside(lag, 0, NQ):
                        reciprocals(1, lag)

                chain = [0]

                def link(ins):
                    chain[0] += 1
                    ins.then_inc(s_chain, 1)
                    dve.wait_ge(s_chain, chain[0])

                def rank_pass(k, _):
                    o, r = k % 2, k // 2
                    shift, bits = DIGITS[r]
                    nd = 1 << bits
                    if r:
                        dve.wait_ge(s_rec[o], 16 * r)
                    link(nc.vector.tensor_scalar(digit[:, :], rec[o][:, :, 0], shift, nd - 1,
                                                 ALU.logical_shift_right, ALU.bitwise_and))
                    link(nc.vector.tensor_copy(digit_f[:, :], digit[:, :]))
                    link(nc.vector.tensor_tensor(hot[:, 0:nd, :], digit_f[:, :].unsqueeze(1).broadcast_to([P, nd, EC]),
                                                 iota_d[:, 0:nd].unsqueeze(2).broadcast_to([P, nd, EC]), ALU.is_equal))
                    hot_v = hot[:, 0:nd, :].rearrange("p d c -> p (d c)")
                    cum_v = cum[:, 0:nd, :].rearrange("p d c -> p (d c)")
                    link(nc.vector.tensor_tensor_scan(cum_v, hot_v, hot_v, 0.0, ALU.add, ALU.max))
                    link(nc.vector.memset(below[:, :], 0.0))
                    link(nc.vector.memset(count[:, :], 0.0))
                    link(nc.vector.tensor_copy(below[:, 1:nd], cum[:, 0:nd - 1, EC - 1]))
                    nc.vector.tensor_tensor(count[:, 0:nd], cum[:, 0:nd, EC - 1], below[:, 0:nd],
                                            ALU.subtract).then_inc(s_cnt, 1)
                    dve.wait_ge(s_off, k + 1)
                    nc.vector.tensor_tensor(offset[:, :], psY1[:, 0, 0:ND], below[:, :], ALU.subtract).then_inc(s_offr, 1)
                    dve.wait_ge(s_offr, k + 1)
                    link(nc.vector.tensor_tensor(cum[:, 0:nd, :], cum[:, 0:nd, :],
                                                 offset[:, 0:nd].unsqueeze(2).broadcast_to([P, nd, EC]), ALU.add))
                    link(nc.vector.tensor_tensor(cum[:, 0:nd, :], cum[:, 0:nd, :], hot[:, 0:nd, :], ALU.mult))
                    link(nc.vector.tensor_reduce(rank_f[:, :], cum[:, 0:nd, :].rearrange("p d c -> p c d"), AX_X, ALU.add))
                    nc.vector.tensor_copy(rank[o][:, :], rank_f[:, :]).then_inc(s_rank, 1)

                dve.wait_ge(s_iota, 1)
                link(nc.vector.tensor_copy(iota_d[:, :], iota_i[:, :]))
                steps(dve, step, 0, LAST, CUTS, rank_pass)

            @block.gpsimd
            def _(pool):
                pool.iota(iota_i[:, :], pattern=[[1, ND]], base=0, channel_multiplier=0).then_inc(s_iota, 1)
                copies = 0
                for k in range(2 * len(DIGITS)):
                    o, r = k % 2, k // 2

                    def body(i, first):
                        for h in range(2):
                            if not (first and k == 0):
                                pool.wait_ge(s_scat[h], i * (16 * GT) + k * GI * 16 * GT)
                            pool.tensor_copy(rank_slot[:, h, :], rank[o][:, bass.ds(i * (2 * GT) + h * GT, GT)])
                            pool.tensor_copy(rec_slot[:, h, :, :], rec[o][:, bass.ds(i * (2 * GT) + h * GT, GT), :]).then_inc(s_slotc, 1)
                            pool.wait_ge(s_slotc, i * 2 + (k * GI * 2 + h + 1))
                            pool.sem_inc(s_pass, 1)
                            for u in range(GT):
                                pool.indirect_dma_start(
                                    out=rec_dram[o][:, :], out_offset=bass.IndirectOffsetOnAxis(ap=rank_slot[:, h, u:u + 1], axis=0),
                                    in_=rec_slot[:, h, u, :], in_offset=None, bounds_check=EP + 1,
                                    oob_is_err=False).then_inc(s_scat[h], 16)

                    pool.wait_ge(s_rank, k + 1)
                    body(0, True)
                    with pool.Fori(1, GI) as i:
                        body(i, False)
                    for h in range(2):
                        pool.wait_ge(s_scat[h], (k + 1) * GI * 16 * GT)
                    pool.dma_start(rec[o][:, :, :].rearrange("p c w -> p (c w)"),
                                   rec_dram[o][1:EP + 1, :].rearrange("(p c) w -> p (c w)", c=EC)).then_inc(s_rec[o], 16)
                for o in range(2):
                    pool.wait_ge(s_rec[o], 16 * len(DIGITS))

        inv_deg_src = dram("inv_deg_src", [N, 1])
        dinv_dst = dram("dinv_dst", [N, 1])
        deg_table = (inv_deg_src, dinv_dst)
        go_on = [sb(f"go_on{o}", [P, EC]) for o in range(2)]
        whole = [sb(f"whole{o}", [P, EC]) for o in range(2)]
        leadend = [sb(f"leadend{o}", [P, EC]) for o in range(2)]
        pack = [sb(f"pack{o}", [P, EC + 1, 3], I32) for o in range(2)]
        scale = [sb(f"scale{o}", [P, EC + 1]) for o in range(2)]
        feeds = [sb(f"feeds{o}", [P, P]) for o in range(2)]
        inv_deg_dst = sb("inv_deg_dst", [P, EC + 1])
        weight = sb("weight", [P, EC])
        wsum = sb("wsum", [P, EC + 1])
        valid = sb("valid", [P, EC + 1])
        on_next = sb("on_next", [P, EC])
        pen_f = sb("pen_f", [P, P])
        pen_b = sb("pen_b", [P, P])
        TOTAL = EC + 1
        W3 = sb("W3", [P, KB, D])
        Was = sb("Was", [P, KB, 8])
        Wad = sb("Wad", [P, KB, 8])
        HEADS, HD = as3.shape

        with phase() as scope:
            recp = [sb(f"recp{o}", [P, EC, 4], I32, scope) for o in range(2)]
            recn = [sb(f"recn{o}", [P, EC, 4], I32, scope) for o in range(2)]
            att = sb("att", [P, 2, HEADS, HD], F32, scope)
            prod = sb("prod", [P, HEADS, HD], F32, scope)
            keyf = sb("keyf", [P, EC], F32, scope)
            keyp = sb("keyp", [P, EC], F32, scope)
            keyn = sb("keyn", [P, EC], F32, scope)
            last_e = sb("last_e", [P, EC], F32, scope)
            lead = sb("lead", [P, EC], F32, scope)
            fin = sb("fin", [P, EC + 1], F32, scope)
            idxf = sb("idxf", [P, EC + 1], F32, scope)
            ones_e = sb("ones_e", [P, EC], F32, scope)
            cnt = sb("cnt", [P, EC + 1], F32, scope)
            tmp = sb("tmp", [P, EC + 1], F32, scope)
            start = sb("start", [P, 2], F32, scope)
            diag = sb("diag", [P, 2, P], F32, scope)
            after = sb("after", [P, P], F32, scope)
            before_t = sb("before_t", [P, P], F32, scope)
            full1 = sb("full1", [P, N // P], F32, scope)
            idx_slot = sb("idx_slot", [P, 2, GT], I32, scope)
            val_slot = sb("val_slot", [P, 2, GT], F32, scope)
            ps = pb("ps", [P, 2, P], F32, scope)
            psc = pb("psc", [P, 512], F32, scope)
            (s_in, s_w3, s_one, s_init, s_v, s_dg, s_row, s_tails, s_st0, s_cnt1, s_sq, s_deg, s_slot, s_pass2, s_m) = map(sem, (
                "s_in", "s_w3", "s_one", "s_init", "s_v", "s_dg", "s_row", "s_tails", "s_st0", "s_cnt1", "s_sq", "s_deg",
                "s_slot", "s_pass2", "s_m"))
            s_dsc = [sem(f"s_dsc{k}") for k in range(2)]
            block = scope.enter_context(nc.Block())

            @block.sync
            def _(sp):
                for o in range(2):
                    for t, at in ((recp[o], 0), (recn[o], 2)):
                        sp.dma_start(t[:, :, :].rearrange("p c w -> p (c w)"),
                                     rec_dram[o][at:at + EP, :].rearrange("(p c) w -> p (c w)", c=EC)).then_inc(s_in, 16)
                sp.dma_start(W3[:, :, :], w3.rearrange("(k p) h d -> p k (h d)", p=P)).then_inc(s_w3, 16)
                for k, a in enumerate((as3, ad3)):
                    sp.dma_start(att[:, k, :, :], a.partition_broadcast(P)).then_inc(s_w3, 16)
                sp.wait_ge(s_one, 1)
                for table in deg_table:
                    sp.dma_start(table[0:P * (N // P), 0].rearrange("(p c) -> p c", p=P), full1[:, :]).then_inc(s_init, 16)
                    sp.dma_start(table[P * (N // P):N, 0].rearrange("(p c) -> p c", p=1),
                                 full1[0:1, 0:N % P]).then_inc(s_init, 16)

            @block.gpsimd
            def _(pool):
                pool.memset(full1[:, :], 1.0).then_inc(s_one, 1)
                pool.memset(ones_e[:, :], 1.0).then_inc(s_m, 1)
                pool.memset(after[:, :], 0.0).then_inc(s_m, 1)
                pool.wait_ge(s_m, 2)
                pool.affine_select(out=after[:, :], in_=after[:, :], compare_op=ALU.is_ge, fill=1.0, base=0,
                                   pattern=[[-1, P]], channel_multiplier=1).then_inc(s_m, 1)
                pool.memset(before_t[:, :], 0.0).then_inc(s_m, 1)
                pool.wait_ge(s_m, 4)
                pool.affine_select(out=before_t[:, :], in_=before_t[:, :], compare_op=ALU.is_ge, fill=1.0, base=0,
                                   pattern=[[1, P]], channel_multiplier=-1).then_inc(s_m, 1)
                pool.wait_ge(s_init, 64)
                for o in range(2):
                    pool.wait_ge(s_deg, o + 1)

                    def body(i, first, n=GT, halves=2):
                        for h in range(halves):
                            if not first:
                                pool.wait_ge(s_dsc[h], i * (16 * GT) + (o * (GI * GT + 1) if h == 0 else o * GI * GT) * 16)
                            t = i * (2 * GT) + h * GT
                            pool.tensor_copy(idx_slot[:, h, 0:n], pack[o][:, bass.ds(t, n), 2])
                            pool.tensor_copy(val_slot[:, h, 0:n], scale[o][:, bass.ds(t, n)]).then_inc(s_slot, 1)
                            pool.wait_ge(s_slot, i * 2 + (o * (2 * GI + 1) + h + 1))
                            pool.sem_inc(s_pass2, 1)
                            for u in range(n):
                                pool.indirect_dma_start(
                                    out=deg_table[o][:, :], out_offset=bass.IndirectOffsetOnAxis(ap=idx_slot[:, h, u:u + 1], axis=0),
                                    in_=val_slot[:, h, u:u + 1], in_offset=None, bounds_check=N - 1,
                                    oob_is_err=False).then_inc(s_dsc[h], 16)

                    body(0, o == 0)
                    with pool.Fori(1, GI) as i:
                        body(i, False)
                    body(GI, False, 1, 1)
                pool.wait_ge(s_dsc[0], 2 * (GI * GT + 1) * 16)
                pool.wait_ge(s_dsc[1], 2 * GI * GT * 16)

            @block.tensor
            def _(pe):
                for o in range(2):
                    pe.wait_ge(s_dg, o + 1)
                    for k in range(2):
                        last = nc.tensor.matmul(ps[:, k, :], ones[:, :], diag[:, k, :], start=True, stop=True)
                    last.then_inc(s_row, 1)
                    pe.wait_ge(s_tails, o + 1)
                    nc.tensor.matmul(psc[:, 0:2], feeds[o][:, :], tmp[:, 0:2], start=True, stop=True).then_inc(s_st0, 1)

            @block.scalar
            def _(act):
                act.wait_ge(s_cnt1, 2)
                nc.scalar.activation(scale[1][:, :], cnt[:, :], ACT.Sqrt).then_inc(s_sq, 1)

            @block.vector
            def _(dve):
                chain = [0]

                def link(ins):
                    chain[0] += 1
                    ins.then_inc(s_v, 1)
                    dve.wait_ge(s_v, chain[0])

                V = nc.vector
                dve.wait_ge(s_in, 64)
                dve.wait_ge(s_m, 5)
                for o in range(2):
                    col0 = lambda a: a[:, 0:1]
                    link(V.tensor_copy(keyf[:, :], rec[o][:, :, 0]))
                    link(V.tensor_copy(keyp[:, :], recp[o][:, :, 0]))
                    link(V.tensor_copy(keyn[:, :], recn[o][:, :, 0]))
                    link(V.tensor_tensor(whole[o][:, :], keyf[:, :], keyp[:, :], ALU.is_equal))
                    link(V.tensor_copy(go_on[o][:, :], whole[o][:, :]))
                    link(V.memset(go_on[o][:, 0:1], 0.0))
                    link(V.tensor_tensor(last_e[:, :], keyf[:, :], keyn[:, :], ALU.not_equal))
                    if o == 1:
                        link(V.tensor_tensor(on_next[:, :], keyf[:, :], keyn[:, :], ALU.is_equal))
                    link(V.tensor_scalar(lead[:, :], keyf[:, :], keyf[:, 0:1], whole[o][:, 0:1], ALU.is_equal, ALU.mult))
                    link(V.tensor_tensor(leadend[o][:, :], last_e[:, :], lead[:, :], ALU.mult))
                    link(V.tensor_tensor(fin[:, 0:EC], last_e[:, :], leadend[o][:, :], ALU.subtract))
                    link(V.tensor_reduce(fin[:, EC:EC + 1], leadend[o][:, :], AX_X, ALU.add))
                    link(V.tensor_scalar(idxf[:, :], fin[:, :], -float(SKIP), float(SKIP), ALU.mult, ALU.add))
                    link(V.tensor_tensor(idxf[:, 0:EC], idxf[:, 0:EC], keyf[:, :], ALU.add))
                    link(V.tensor_tensor(idxf[:, EC:EC + 1], idxf[:, EC:EC + 1], keyf[:, 0:1], ALU.add))
                    link(V.tensor_copy(pack[o][:, :, 2], idxf[:, :]))
                    if o == 1:
                        link(V.tensor_scalar(valid[:, :], idxf[:, :], float(N), None, ALU.is_lt))
                    link(V.tensor_scalar(pack[o][:, 0:EC, 1], keyf[:, :], float(N - 1), None, ALU.min))
                    link(V.tensor_scalar(pack[o][:, EC:EC + 1, 1], keyf[:, 0:1], float(N - 1), None, ALU.min))
                    link(V.tensor_copy(keyp[:, :], rec[o][:, :, 1]))
                    link(V.tensor_scalar(pack[o][:, 0:EC, 0], keyp[:, :], float(N - 1), None, ALU.min))
                    link(V.memset(pack[o][:, EC:EC + 1, 0], 0))
                    link(V.tensor_scalar(diag[:, 0, :], ident[:, :], keyf[:, 0:1], None, ALU.mult))
                    V.tensor_scalar(diag[:, 1, :], ident[:, :], keyf[:, EC - 1:EC], None, ALU.mult).then_inc(s_dg, 1)
                    dve.wait_ge(s_row, o + 1)
                    link(V.scalar_tensor_tensor(out=feeds[o][:, :], in0=ps[:, 0, :], scalar=keyf[:, EC - 1:EC],
                                                in1=before[:, :], op0=ALU.is_equal, op1=ALU.mult))
                    if o == 1:
                        for pen, k, key, where in ((pen_f, 1, keyf[:, 0:1], before_t), (pen_b, 0, keyf[:, EC - 1:EC], after)):
                            link(V.scalar_tensor_tensor(out=pen[:, :], in0=ps[:, k, :], scalar=key, in1=where[:, :],
                                                        op0=ALU.is_equal, op1=ALU.mult))
                            link(V.tensor_scalar(pen[:, :], pen[:, :], 1.0, 1e30, ALU.subtract, ALU.mult))
                    else:
                        link(V.tensor_copy(weight[:, :], rec[0][:, :, 2].bitcast(F32)))
                    link(V.tensor_tensor_scan(cnt[:, 0:EC], go_on[o][:, :], ones_e[:, :], 0.0, ALU.mult, ALU.add))
                    link(V.tensor_copy(tmp[:, 0:1], cnt[:, EC - 1:EC]))
                    if o == 0:
                        link(V.tensor_tensor_scan(wsum[:, 0:EC], go_on[0][:, :], weight[:, :], 0.0, ALU.mult, ALU.add))
                        V.tensor_copy(tmp[:, 1:2], wsum[:, EC - 1:EC]).then_inc(s_tails, 1)
                    else:
                        V.tensor_copy(tmp[:, 1:2], cnt[:, EC - 1:EC]).then_inc(s_tails, 1)
                    dve.wait_ge(s_st0, o + 1)
                    link(V.tensor_copy(start[:, :], psc[:, 0:2]))
                    link(V.tensor_tensor_scan(cnt[:, 0:EC], whole[o][:, :], ones_e[:, :], start[:, 0:1], ALU.mult, ALU.add))
                    link(V.tensor_tensor(tmp[:, 0:EC], cnt[:, 0:EC], leadend[o][:, :], ALU.mult))
                    link(V.tensor_reduce(cnt[:, EC:EC + 1], tmp[:, 0:EC], AX_X, ALU.add))
                    if o == 0:
                        link(V.tensor_tensor_scan(wsum[:, 0:EC], whole[0][:, :], weight[:, :], start[:, 1:2], ALU.mult, ALU.add))
                        link(V.tensor_tensor(tmp[:, 0:EC], wsum[:, 0:EC], leadend[0][:, :], ALU.mult))
                        link(V.tensor_reduce(wsum[:, EC:EC + 1], tmp[:, 0:EC], AX_X, ALU.add))
                    link(V.tensor_scalar(cnt[:, :], cnt[:, :], 1.0, None, ALU.add))
                    if o == 0:
                        V.reciprocal(scale[0][:, :], cnt[:, :]).then_inc(s_deg, 1)
                        dve.wait_ge(s_deg, 1)
                        V.tensor_copy(start[:, 0:1], cnt[:, 0:1]).then_inc(s_cnt1, 1)
                    else:
                        link(V.reciprocal(inv_deg_dst[:, :], cnt[:, :]))
                        V.tensor_copy(start[:, 0:1], cnt[:, 0:1]).then_inc(s_cnt1, 1)
                        dve.wait_ge(s_sq, 1)
                        V.reciprocal(scale[1][:, :], scale[1][:, :]).then_inc(s_deg, 1)
                dve.wait_ge(s_w3, 48)
                for k, to in ((0, Was), (1, Wad)):
                    for b in range(KB):
                        link(V.tensor_tensor(prod[:, :, :], W3[:, b, :].rearrange("p (h d) -> p h d", d=HD),
                                             att[:, k, :, :], ALU.mult))
                        link(V.tensor_reduce(to[:, b, :], prod[:, :, :], AX_X, ALU.add))

        x1e = dram("x1e", [P, TOTAL * D])
        x2e = dram("x2e", [P, TOTAL * D])
        x3e = dram("x3e", [P, TOTAL * D])
        agg2 = dram("agg2", [P, TOTAL * D])
        h3 = dram("h3", [P, TOTAL * D])

        msg = sb("msg", [P, 2, GT, D])
        own = sb("own", [P, 2, GT, D])
        pk = sb("pk", [P, 2, GT, 3], I32)
        lr = sb("lr", [P, D])
        tot = sb("tot", [P, 2, GT, D])
        tT = sb("tT", [P, 2, 2, KB, QT, P])
        o4 = sb("o4", [P, 2, QT, D])
        est = sb("est", [P, 2, 4, QT, 6])
        emv = sb("emv", [P, 2, 4, QT, 2])
        esm = sb("esm", [P, 2, 4, 3, QT])
        wslot = sb("wslot", [P, 2, GT])
        V, A, T = nc.vector, nc.scalar, nc.tensor

        def gather(pool, table, to, h, u, f, s):
            pool.indirect_dma_start(out=to, out_offset=None, in_=table[:, :],
                                    in_offset=bass.IndirectOffsetOnAxis(ap=pk[:, h, u, f:f + 1], axis=0),
                                    bounds_check=N - 1, oob_is_err=False).then_inc(s, 16)

        def scatter_rows(pool, table, h, n, s):
            for u in range(n):
                pool.indirect_dma_start(out=table[:, :], out_offset=bass.IndirectOffsetOnAxis(ap=pk[:, h, u, 2:3], axis=0),
                                        in_=own[:, h, u, :], in_offset=None, bounds_check=N - 1,
                                        oob_is_err=False).then_inc(s, 16)

        def indices(pool, o, g, s_pk, s_go):
            i, c, _ = g
            t = c * GT if i is None else i * (2 * GT) + c * GT
            n = group_tiles(g)
            pool.tensor_copy(pk[:, slot(g), 0:n, :], pack[o][:, bass.ds(t, n), :]).then_inc(s_pk, 1)
            pool.wait_ge(s_pk, ev(g, 1, 1))
            pool.sem_inc(s_go, 1)

        def transposed(q, k, of, to, s):
            for j in range(ntiles(q)):
                for b in range(KB):
                    last = T.transpose(to[:, b, j, :], of[:, half(q), q[1] % 2 * 4 + j, b * P:(b + 1) * P], ident[:, :])
            last.then_inc(s, 1)

        def product(q, k, weights, to, s):
            for j in range(ntiles(q)):
                for b in range(KB):
                    last = T.matmul(to[:, j, :], tT[:, q[1] % 2, k, b, j, :], weights[:, b, :],
                                    start=(b == 0), stop=(b == KB - 1))
            last.then_inc(s, 1)

        def accumulate(q, o, s_ready, ready, s_acc, s_lr, s_fix):
            n, h, j0, t0 = ntiles(q), half(q), q[1] % 2 * 4, tile0(q)
            if q[0] is None and q[1] >= FIX:
                V.wait_ge(s_fix, 1)
                V.wait_ge(s_lr, EC)
                V.tensor_tensor(msg[:, 0, 0, :], psF, lr[:, :], ALU.add).then_inc(s_acc, 1)
                return
            V.wait_ge(s_ready, ready)
            for j in range(n):
                if q[0] is None and t0 + j == 0:
                    continue
                before_it = msg[:, h, j0 + j - 1, :] if j0 + j else msg[:, 1 - h, GT - 1, :]
                wait(V, s_acc, t0 + (j - 1))
                V.scalar_tensor_tensor(out=msg[:, h, j0 + j, :], in0=before_it, scalar=go_on[o][:, bass.ds(t0 + j, 1)],
                                       in1=msg[:, h, j0 + j, :], op0=ALU.mult, op1=ALU.add).then_inc(s_acc, 1)
            V.wait_ge(s_acc, t0 + (n - 1))
            for j in range(n):
                V.wait_ge(s_lr, t0 + (j + 1))
                V.scalar_tensor_tensor(out=lr[:, :], in0=msg[:, h, j0 + j, :], scalar=leadend[o][:, bass.ds(t0 + j, 1)],
                                       in1=lr[:, :], op0=ALU.mult, op1=ALU.add).then_inc(s_lr, 1)

        def statistics(l, q, of, s_sum, s_bn, s_go, s_mv):
            n, k = ntiles(q), slot(q)
            V.wait_ge(s_sum, ev(q, 1, 1))
            for j in range(n):
                last = V.bn_stats(est[:, l, k, j, :], of(q, j))
            last.then_inc(s_bn, 1)
            V.wait_ge(s_bn, ev(q, 1, 1))
            V.sem_inc(s_go, 1)
            for j in range(n):
                last = V.bn_aggr(emv[:, l, k, j, :], est[:, l, k, j, :])
            last.then_inc(s_mv, 1)

        def deviation(l, q, s_mv, s_sd):
            n, k = ntiles(q), slot(q)
            A.wait_ge(s_mv, ev(q, 1, 1))
            A.activation(esm[:, l, k, 0, 0:n], emv[:, l, k, 0:n, 1], ACT.Sqrt, bias=eps[:, :]).then_inc(s_sd, 1)

        def reciprocals(l, q, s_sd, s_rs, s_nm):
            n, k = ntiles(q), slot(q)
            V.wait_ge(s_sd, ev(q, 1, 1))
            V.reciprocal(esm[:, l, k, 1, 0:n], esm[:, l, k, 0, 0:n]).then_inc(s_rs, 1)
            V.wait_ge(s_rs, ev(q, 1, 1))
            V.scalar_tensor_tensor(out=esm[:, l, k, 2, 0:n], in0=emv[:, l, k, 0:n, 0], scalar=-1.0,
                                   in1=esm[:, l, k, 1, 0:n], op0=ALU.mult, op1=ALU.mult).then_inc(s_nm, 1)

        def normalise(l, q, of, s_nm, s_norm):
            k = slot(q)
            A.wait_ge(s_nm, ev(q, 1, 1))
            for j in range(ntiles(q)):
                last = A.activation(of(q, j), of(q, j), ACT.Identity, bias=esm[:, l, k, 2, j:j + 1],
                                    scale=esm[:, l, k, 1, j:j + 1])
            last.then_inc(s_norm, 1)

        def own_row(q, j):
            return own[:, half(q), q[1] % 2 * 4 + j, :]

        def o4_row(q, j):
            return o4[:, q[1] % 2, j, :]

        def chunk_of(a, q):
            j0 = q[1] % 2 * 4
            return a[:, half(q), j0:j0 + ntiles(q), :]

        def tiles_of(table, q, n=None):
            t = tile0(q)
            n = n or ntiles(q)
            return table[:, bass.ds(t * D, n * D)]

        def store(sp, table, of, q, s_from, s_go, s_to):
            sp.wait_ge(s_from, ev(q, 1, 1))
            sp.sem_inc(s_go, 1)
            sp.dma_start(tiles_of(table, q), chunk_of(of, q).rearrange("p n d -> p (n d)")).then_inc(s_to, 16)

        def stored(q):
            return 32 * (q[1] // 4) if q[0] is None else q[0] * 32 + q[1] // 4 * 32

        def over(v, n):
            return v.unsqueeze(1).broadcast_to([P, n, D])

        with phase() as scope:
            psT = pb("psT", [P, KB, QT, P], F32, scope)
            psY = pb("psY", [P, QT, D], F32, scope)
            psF = psT[:, 0, 0:2, :].rearrange("p a b -> p (a b)")
            (s_pk, s_go, s_vgo, s_spgo, s_scaled, s_acc, s_lr, s_fix, s_tot, s_t, s_tc, s_y, s_add, s_bn, s_mv, s_sd, s_rs,
             s_nm, s_norm) = (sem(f"e0_{n}") for n in (
                "pk", "go", "vgo", "spgo", "scaled", "acc", "lr", "fix", "tot", "t", "tc", "y", "add", "bn", "mv", "sd",
                "rs", "nm", "norm"))
            s_g = [sem(f"e0_g{k}") for k in range(2)]
            s_sc = [sem(f"e0_sc{k}") for k in range(2)]
            s_lin = [sem(f"e0_lin{k}") for k in range(2)]
            block = scope.enter_context(nc.Block())

            @block.gpsimd
            def _(pool):
                def step(g):
                    n, h = group_tiles(g), slot(g)
                    if inside(g, 0, 2 * GI):
                        wait(pool, s_sc[h], nth(g, 16 * GT))
                        wait(pool, s_lin[h], nth(g, 32))
                        wait(pool, s_acc, ev(g, GT, 1 - GT))
                        indices(pool, 0, g, s_pk, s_go)
                        for u in range(n):
                            if n == GT:
                                gather(pool, x, msg[:, h, u, :], h, u, 0, s_g[h])
                                gather(pool, inv_deg_src, wslot[:, h, u:u + 1], h, u, 0, s_g[h])
                            gather(pool, x, own[:, h, u, :], h, u, 1, s_g[h])
                    b = sh(g, -1)
                    if inside(b, 0, 2 * GI):
                        pool.wait_ge(s_norm, FIX + 1 if group_tiles(b) == 1 else ev(b, 2, 2))
                        pool.sem_inc(s_go, 1)
                        scatter_rows(pool, x1, slot(b), group_tiles(b), s_sc[slot(b)])

                groups(pool, step, 2 * GI + 1)
                pool.wait_ge(s_sc[0], 16 * (GI * GT + 1))
                pool.wait_ge(s_sc[1], 16 * GI * GT)

            def arrived(q):
                return 16 * 3 * GI * GT + 16 if q[0] is None and q[1] >= FIX else landed(q, 3)

            @block.scalar
            def _(act):
                def step(q):
                    if inside(q, 0, FIX - 1):
                        act.wait_ge(s_g[half(q)], arrived(q))
                        for j in range(ntiles(q)):
                            jj = q[1] % 2 * 4 + j
                            last = A.activation(msg[:, half(q), jj, :], msg[:, half(q), jj, :], ACT.Copy,
                                                scale=wslot[:, half(q), jj:jj + 1])
                        last.then_inc(s_scaled, 1)
                    if inside(q, 0, FIX):
                        n = ntiles(q)
                        act.wait_ge(s_t, ev(q, 1, 1))
                        wait(act, s_y, ev(q, 1, -1))
                        A.activation(tT[:, q[1] % 2, 0, :, 0:n, :], psT[:, :, 0:n, :], ACT.Copy).then_inc(s_tc, 1)
                    b = sh(q, -1)
                    if inside(b, 0, FIX):
                        deviation(0, b, s_mv, s_sd)
                        normalise(0, b, own_row, s_nm, s_norm)

                chunks(act, step, FIX + 1)

            @block.tensor
            def _(pe):
                def step(q):
                    if q[0] is None and q[1] == FIX:
                        pe.wait_ge(s_acc, EC - 1)
                        pe.wait_ge(s_tc, FIX)
                        T.matmul(psF, feeds[0][:, :], msg[:, 1, GT - 1, :], start=True, stop=True).then_inc(s_fix, 1)
                    pe.wait_ge(s_tot, ev(q, 1, 1))
                    wait(pe, s_tc, ev(q))
                    transposed(q, 0, tot, psT, s_t)
                    pe.wait_ge(s_tc, ev(q, 1, 1))
                    wait(pe, s_add, ev(q))
                    product(q, 0, W0, psY, s_y)

                chunks(pe, step, FIX)

            @block.vector
            def _(dve):
                def step(q):
                    if inside(q, 0, FIX):
                        n, h, j0, t0 = ntiles(q), half(q), q[1] % 2 * 4, tile0(q)
                        accumulate(q, 0, s_scaled, ev(q, 1, 1), s_acc, s_lr, s_fix)
                        if n == 1:
                            dve.wait_ge(s_g[0], arrived(q))
                        wait(dve, s_acc, t0 + (n - 1))
                        wait(dve, s_t, ev(q, 1, -3))
                        for j in range(n):
                            last = V.scalar_tensor_tensor(out=tot[:, h, j0 + j, :], in0=own[:, h, j0 + j, :],
                                                          scalar=scale[0][:, bass.ds(t0 + j, 1)], in1=msg[:, h, j0 + j, :],
                                                          op0=ALU.mult, op1=ALU.add)
                        last.then_inc(s_tot, 1)
                    b = sh(q, -1)
                    if inside(b, 0, FIX):
                        n = ntiles(b)
                        dve.wait_ge(s_y, ev(b, 1, 1))
                        V.tensor_tensor(chunk_of(own, b), psY[:, 0:n, :], chunk_of(own, b), ALU.add).then_inc(s_add, 1)
                        statistics(0, b, own_row, s_add, s_bn, s_vgo, s_mv)
                        reciprocals(0, b, s_sd, s_rs, s_nm)

                V.memset(lr[:, :], 0.0).then_inc(s_lr, 1)
                chunks(dve, step, FIX + 1)

            @block.sync
            def _(sp):
                chunks(sp, lambda q: store(sp, x1e, own, q, s_norm, s_spgo, s_lin[half(q)]), FIX)
                sp.wait_ge(s_lin[0], 32 * GI + 16)
                sp.wait_ge(s_lin[1], 32 * GI)

        with phase() as scope:
            psT = [pb(f"psT{k}", [P, KB, QT, P], F32, scope) for k in "AB"]
            psY = [pb(f"psY{k}", [P, QT, D], F32, scope) for k in "AB"]
            psF = psT[0][:, 0, 0:2, :].rearrange("p a b -> p (a b)")
            (s_pk, s_go, s_vgo, s_spgo, s_scaled, s_acc, s_lr, s_fix, s_t, s_tc, s_y, s_oa, s_take, s_sum, s_plus) = (
                sem(f"e1_{n}") for n in ("pk", "go", "vgo", "spgo", "scaled", "acc", "lr", "fix", "t", "tc", "y", "oa",
                                         "take", "sum", "plus"))
            s_gb = [sem(f"e1_gb{k}") for k in range(3)]
            s_bn, s_mv, s_sd, s_rs, s_nm, s_norm = ([sem(f"e1_{n}{l}") for l in range(2)] for n in (
                "bn", "mv", "sd", "rs", "nm", "norm"))
            s_g = [sem(f"e1_g{k}") for k in range(2)]
            s_own = [sem(f"e1_own{k}") for k in range(2)]
            s_sc = [sem(f"e1_sc{k}") for k in range(2)]
            block = scope.enter_context(nc.Block())

            @block.sync
            def _(sp):
                def step(g):
                    n, h = group_tiles(g), slot(g)
                    i, c, _ = g
                    t = c * GT if i is None else i * (2 * GT) + c * GT
                    wait(sp, s_sc[h], nth(g, 16 * GT))
                    sp.sem_inc(s_spgo, 1)
                    sp.dma_start(own[:, h, 0:n, :].rearrange("p n d -> p (n d)"),
                                 x1e[:, bass.ds(t * D, n * D)]).then_inc(s_own[h], 16)

                groups(sp, step, 2 * GI)

            @block.gpsimd
            def _(pool):
                def step(g):
                    n, h = group_tiles(g), slot(g)
                    if inside(g, 0, 2 * GI):
                        wait(pool, s_sc[h], nth(g, 16 * GT))
                        wait(pool, s_acc, ev(g, GT, 1 - GT))
                        wait(pool, s_t, ev(g, 2, -2))
                        indices(pool, 0, g, s_pk, s_go)
                        if n == GT:
                            for u in range(n):
                                gather(pool, x1, msg[:, h, u, :], h, u, 0, s_g[h])
                    b = sh(g, -1)
                    if inside(b, 0, 2 * GI):
                        pool.wait_ge(s_norm[1], FIX + 1 if group_tiles(b) == 1 else ev(b, 2, 2))
                        pool.sem_inc(s_go, 1)
                        scatter_rows(pool, x2, slot(b), group_tiles(b), s_sc[slot(b)])

                groups(pool, step, 2 * GI + 1)
                pool.wait_ge(s_sc[0], 16 * (GI * GT + 1))
                pool.wait_ge(s_sc[1], 16 * GI * GT)

            @block.scalar
            def _(act):
                def step(q):
                    if inside(q, 0, FIX - 1):
                        act.wait_ge(s_g[half(q)], landed(q, 1))
                        t0 = tile0(q)
                        for j in range(ntiles(q)):
                            jj = q[1] % 2 * 4 + j
                            last = A.activation(msg[:, half(q), jj, :], msg[:, half(q), jj, :], ACT.Copy,
                                                scale=weight[:, bass.ds(t0 + j, 1)])
                        last.then_inc(s_scaled, 1)
                    if inside(q, 0, FIX):
                        n = ntiles(q)
                        act.wait_ge(s_t, ev(q, 1, 1))
                        wait(act, s_y, ev(q, 1, -1))
                        for k in range(2):
                            last = A.activation(tT[:, q[1] % 2, k, :, 0:n, :], psT[k][:, :, 0:n, :], ACT.Copy)
                        last.then_inc(s_tc, 1)
                    b, c = sh(q, -1), sh(q, -2)
                    if inside(b, 0, FIX):
                        deviation(0, b, s_mv[0], s_sd[0])
                        normalise(0, b, o4_row, s_nm[0], s_norm[0])
                    if inside(c, 0, FIX):
                        deviation(1, c, s_mv[1], s_sd[1])
                        normalise(1, c, own_row, s_nm[1], s_norm[1])

                chunks(act, step, FIX + 2)

            @block.tensor
            def _(pe):
                def step(q):
                    if q[0] is None and q[1] == FIX:
                        pe.wait_ge(s_acc, EC - 1)
                        pe.wait_ge(s_tc, FIX)
                        T.matmul(psF, feeds[0][:, :], msg[:, 1, GT - 1, :], start=True, stop=True).then_inc(s_fix, 1)
                    pe.wait_ge(s_acc, tile0(q) + (ntiles(q) - 1))
                    pe.wait_ge(s_own[half(q)], loads(q))
                    wait(pe, s_tc, ev(q))
                    transposed(q, 0, msg, psT[0], s_gb[0])
                    transposed(q, 1, own, psT[1], s_t)
                    pe.wait_ge(s_tc, ev(q, 1, 1))
                    wait(pe, s_take, ev(q))
                    product(q, 0, W1T, psY[0], s_gb[1])
                    product(q, 1, WrT, psY[1], s_y)

                chunks(pe, step, FIX)

            @block.vector
            def _(dve):
                def step(q):
                    if inside(q, 0, FIX):
                        accumulate(q, 0, s_scaled, ev(q, 1, 1), s_acc, s_lr, s_fix)
                    b, c = sh(q, -1), sh(q, -2)
                    if inside(b, 0, FIX):
                        n, t0 = ntiles(b), tile0(b)
                        dve.wait_ge(s_y, ev(b, 1, 1))
                        wait(dve, s_sum, ev(b, 1, -1))
                        for j in range(n):
                            last = V.scalar_tensor_tensor(out=o4[:, b[1] % 2, j, :], in0=B1, scalar=wsum[:, bass.ds(t0 + j, 1)],
                                                          in1=psY[0][:, j, :], op0=ALU.mult, op1=ALU.add)
                        last.then_inc(s_oa, 1)
                        V.tensor_tensor(chunk_of(own, b), psY[1][:, 0:n, :], chunk_of(own, b), ALU.add).then_inc(s_take, 1)
                        statistics(0, b, o4_row, s_oa, s_bn[0], s_vgo, s_mv[0])
                    if inside(c, 0, FIX):
                        n = ntiles(c)
                        oc = o4[:, c[1] % 2, 0:n, :]
                        dve.wait_ge(s_norm[0], ev(c, 1, 1))
                        V.tensor_tensor(oc, oc, over(G1, n), ALU.mult).then_inc(s_plus, 1)
                        dve.wait_ge(s_plus, ev(c, 3, 1))
                        V.tensor_tensor(oc, oc, over(BE1, n), ALU.add).then_inc(s_plus, 1)
                        dve.wait_ge(s_plus, ev(c, 3, 2))
                        V.scalar_tensor_tensor(out=oc, in0=oc, scalar=0.0, in1=over(BR, n), op0=ALU.max,
                                               op1=ALU.add).then_inc(s_plus, 1)
                        dve.wait_ge(s_plus, ev(c, 3, 3))
                        V.tensor_tensor(chunk_of(own, c), chunk_of(own, c), oc, ALU.add).then_inc(s_sum, 1)
                        statistics(1, c, own_row, s_sum, s_bn[1], s_vgo, s_mv[1])
                    if inside(b, 0, FIX):
                        reciprocals(0, b, s_sd[0], s_rs[0], s_nm[0])
                    if inside(c, 0, FIX):
                        reciprocals(1, c, s_sd[1], s_rs[1], s_nm[1])

                V.memset(lr[:, :], 0.0).then_inc(s_lr, 1)
                chunks(dve, step, FIX + 2)

        DG = D + 4
        gram_scope = ctx.enter_context(ExitStack())
        psG = pb("psG", [P, KB, 512], F32, gram_scope)

        with phase() as scope:
            xg = sb("xg", [P, RING, QT, DG], F32, scope)
            xm = sb("xm", [P, RING, QT, D], F32, scope)
            free = sb("free", [P, NPP + QT], F32, scope)
            s_fr, s_one2, s_mask, s_mul, s_gram, s_pgo = (sem(f"g_{n}") for n in ("fr", "one", "mask", "mul", "gram", "pgo"))
            s_x = [sem(f"g_x{k}") for k in range(RING)]
            block = scope.enter_context(nc.Block())

            @block.sync
            def _(sp):
                sp.dma_start(free[:, 0:NPP], dinv_dst[0:P * NPP, 0].rearrange("(p c) -> p c", p=P)).then_inc(s_fr, 16)
                sp.dma_start(free[0:TAIL, NPP:NPP + QT], dinv_dst[P * NPP:N, 0].rearrange("(p c) -> p c", p=TAIL)).then_inc(s_fr, 16)

                def step(q):
                    wait(sp, s_gram, ev(q, 1, 1 - RING))
                    sp.sem_inc(s_pgo, 1)
                    sp.dma_start(xg[0:rows(q), slot(q), :, 0:D],
                                 quad_of(x2, q).rearrange("p (j d) -> p j d", d=D)).then_inc(s_x[slot(q)], 16)

                steps(sp, step, 0, NQ)

            @block.vector
            def _(dve):
                V.memset(xg[:, :, :, D:DG], 1.0).then_inc(s_one2, 1)
                dve.wait_ge(s_fr, 32)
                V.tensor_scalar(free[:, 0:NPP], free[:, 0:NPP], 1.0, None, ALU.is_equal).then_inc(s_mask, 1)
                V.tensor_scalar(free[0:TAIL, NPP:NPP + QT], free[0:TAIL, NPP:NPP + QT], 1.0, None, ALU.is_equal).then_inc(s_mask, 1)
                dve.wait_ge(s_mask, 2)

                def step(q):
                    r, s = rows(q), slot(q)
                    dve.wait_ge(s_x[s], nth(q, 16, 16))
                    wait(dve, s_gram, ev(q, 1, 1 - RING))
                    V.tensor_tensor(xm[0:r, s, :, :], xg[0:r, s, :, 0:D],
                                    free[0:r, bass.ds(ev(q, QT), QT)].unsqueeze(2).broadcast_to([r, QT, D]),
                                    ALU.mult).then_inc(s_mul, 1)

                steps(dve, step, 0, NQ)

            @block.tensor
            def _(pe):
                pe.wait_ge(s_one2, 1)

                def step(q):
                    r, s = rows(q), slot(q)
                    pe.wait_ge(s_mul, ev(q, 1, 1))
                    for j in range(QT):
                        for b in range(KB):
                            last = T.matmul(psG[:, b, 0:D + 1], xm[0:r, s, j, b * P:(b + 1) * P], xg[0:r, s, j, 0:D + 1],
                                            start=q[0] is None and q[1] == 0 and j == 0, stop=False)
                    last.then_inc(s_gram, 1)

                steps(pe, step, 0, NQ)

        with phase() as scope:
            tw = sb("tw", [P, 2, GT, D], F32, scope)
            tot1 = sb("tot1", [P, 2, GT, DG], F32, scope)
            psF = pb("psF2", [P, D], F32, scope)[:, :]
            s_pk, s_go, s_spgo, s_scaled, s_acc, s_lr, s_fix, s_one2, s_part, s_tot, s_val, s_gram, s_own, s_agg = (
                sem(f"e2_{n}") for n in ("pk", "go", "spgo", "scaled", "acc", "lr", "fix", "one", "part", "tot", "val", "gram",
                                         "own", "agg"))
            s_g = [sem(f"e2_g{k}") for k in range(2)]
            s_lin = [sem(f"e2_lin{k}") for k in range(2)]
            block = scope.enter_context(nc.Block())

            def stored_pair(q):
                return 64 * (q[1] // 4) if q[0] is None else q[0] * 64 + q[1] // 4 * 64

            def arrived2(q):
                return 16 * 3 * GI * GT + 16 if q[0] is None and q[1] >= FIX else landed(q, 3)

            @block.gpsimd
            def _(pool):
                def step(g):
                    n, h = group_tiles(g), slot(g)
                    wait(pool, s_lin[h], nth(g, 64))
                    wait(pool, s_acc, ev(g, GT, 1 - GT))
                    wait(pool, s_tot, ev(g, 2, -2))
                    indices(pool, 1, g, s_pk, s_go)
                    for u in range(n):
                        if n == GT:
                            gather(pool, x2, msg[:, h, u, :], h, u, 0, s_g[h])
                            gather(pool, dinv_dst, wslot[:, h, u:u + 1], h, u, 0, s_g[h])
                        gather(pool, x2, own[:, h, u, :], h, u, 1, s_g[h])

                groups(pool, step, 2 * GI)

            @block.scalar
            def _(act):
                def step(q):
                    n, h, j0, t0 = ntiles(q), half(q), q[1] % 2 * 4, tile0(q)
                    if inside(q, 0, FIX):
                        act.wait_ge(s_g[h], arrived2(q))
                        if not (q[0] is None and q[1] == FIX):
                            for j in range(n):
                                last = A.activation(msg[:, h, j0 + j, :], msg[:, h, j0 + j, :], ACT.Copy,
                                                    scale=wslot[:, h, j0 + j:j0 + j + 1])
                            last.then_inc(s_scaled, 1)
                        wait(act, s_val, ev(q, 1, -3))
                        wait(act, s_gram, ev(q, 1, -3))
                        for j in range(n):
                            last = A.activation(tw[:, h, j0 + j, :], own[:, h, j0 + j, :], ACT.Copy,
                                                scale=inv_deg_dst[:, bass.ds(t0 + j, 1)])
                        last.then_inc(s_part, 1)
                    b = sh(q, -1)
                    if inside(b, 0, FIX):
                        n, h, j0, t0 = ntiles(b), half(b), b[1] % 2 * 4, tile0(b)
                        act.wait_ge(s_tot, ev(b, 1, 1))
                        for j in range(n):
                            last = A.activation(tw[:, h, j0 + j, :], tot1[:, h, j0 + j, 0:D], ACT.Copy,
                                                scale=valid[:, bass.ds(t0 + j, 1)])
                        last.then_inc(s_val, 1)

                chunks(act, step, FIX + 1)

            @block.vector
            def _(dve):
                def step(q):
                    n, h, j0, t0 = ntiles(q), half(q), q[1] % 2 * 4, tile0(q)
                    accumulate(q, 1, s_scaled, ev(q, 1, 1), s_acc, s_lr, s_fix)
                    wait(dve, s_acc, t0 + (n - 1))
                    dve.wait_ge(s_part, ev(q, 1, 1))
                    wait(dve, s_gram, ev(q, 1, -3))
                    wait(dve, s_lin[h], stored_pair(q))
                    for j in range(n):
                        last = V.scalar_tensor_tensor(out=tot1[:, h, j0 + j, 0:D], in0=msg[:, h, j0 + j, :],
                                                      scalar=scale[1][:, bass.ds(t0 + j, 1)], in1=tw[:, h, j0 + j, :],
                                                      op0=ALU.mult, op1=ALU.add)
                    last.then_inc(s_tot, 1)

                V.memset(tot1[:, :, :, D:DG], 1.0).then_inc(s_one2, 1)
                V.memset(lr[:, :], 0.0).then_inc(s_lr, 1)
                chunks(dve, step, FIX)

            @block.tensor
            def _(pe):
                pe.wait_ge(s_one2, 1)

                def step(q):
                    n, h, j0 = ntiles(q), half(q), q[1] % 2 * 4
                    fix = q[0] is None and q[1] == FIX
                    if fix:
                        pe.wait_ge(s_acc, EC - 1)
                        T.matmul(psF, feeds[1][:, :], msg[:, 1, GT - 1, :], start=True, stop=True).then_inc(s_fix, 1)
                    pe.wait_ge(s_val, ev(q, 1, 1))
                    for j in range(n):
                        for b in range(KB):
                            last = T.matmul(psG[:, b, 0:D + 1], tw[:, h, j0 + j, b * P:(b + 1) * P],
                                            tot1[:, h, j0 + j, 0:D + 1], start=False, stop=fix)
                    last.then_inc(s_gram, 1)

                chunks(pe, step, FIX)

            @block.sync
            def _(sp):
                def step(q):
                    n, h, j0 = ntiles(q), half(q), q[1] % 2 * 4
                    sp.wait_ge(s_tot, ev(q, 1, 1))
                    sp.sem_inc(s_spgo, 1)
                    sp.dma_start(tiles_of(agg2, q).rearrange("p (n d) -> p n d", d=D), tot1[:, h, j0:j0 + n, 0:D]).then_inc(s_lin[h], 16)
                    sp.dma_start(tiles_of(x2e, q), chunk_of(own, q).rearrange("p n d -> p (n d)")).then_inc(s_lin[h], 16)

                chunks(sp, step, FIX)
                sp.wait_ge(s_lin[0], 64 * GI + 32)
                sp.wait_ge(s_lin[1], 64 * GI)

        W2s = sb("W2s", [P, KB, D])
        shift = sb("shift", [P, D])
        with phase() as scope:
            gram = sb("gram", [P, KB, D + 1], F32, scope)
            wv = sb("wv", [P, KB, D], F32, scope)
            ws = sb("ws", [P, KB, D], F32, scope)
            mean = sb("mean", [P, D], F32, scope)
            var = sb("var", [P, D], F32, scope)
            tmp2 = sb("tmp2", [P, D], F32, scope)
            psV = pb("psV", [P, KB, D], F32, scope)
            psM = pb("psM", [P, 2, D], F32, scope)
            s_c, s_gr, s_v1, s_wv, s_mo, s_sd2, s_vr = (sem(f"s2_{n}") for n in ("c", "gr", "v", "wv", "mo", "sd", "vr"))
            block = scope.enter_context(nc.Block())

            @block.tensor
            def _(pe):
                pe.wait_ge(s_gr, 1)
                for b in range(KB):
                    for a in range(KB):
                        last = T.matmul(psV[:, b, :], gram[:, a, b * P:(b + 1) * P], W2[:, a, :], start=(a == 0), stop=(a == KB - 1))
                last.then_inc(s_v1, 1)
                pe.wait_ge(s_wv, 1)
                for k, of in enumerate((wv, ws)):
                    for b in range(KB):
                        last = T.matmul(psM[:, k, :], ones[:, :], of[:, b, :], start=(b == 0), stop=(b == KB - 1))
                last.then_inc(s_mo, 1)

            @block.scalar
            def _(act):
                act.wait_ge(s_vr, 1)
                A.activation(var[:, :], var[:, :], ACT.Sqrt, bias=eps[:, :]).then_inc(s_sd2, 1)

            @block.vector
            def _(dve):
                chain = [0]

                def link(ins):
                    chain[0] += 1
                    ins.then_inc(s_c, 1)
                    dve.wait_ge(s_c, chain[0])

                V.tensor_copy(gram[:, :, :], psG[:, :, 0:D + 1]).then_inc(s_gr, 1)
                dve.wait_ge(s_gr, 1)
                for b in range(KB):
                    link(V.tensor_scalar(ws[:, b, :], W2[:, b, :], gram[:, b, D:D + 1], None, ALU.mult))
                dve.wait_ge(s_v1, 1)
                V.tensor_tensor(wv[:, :, :], psV[:, :, :], W2[:, :, :], ALU.mult).then_inc(s_wv, 1)
                dve.wait_ge(s_mo, 1)
                link(V.tensor_scalar(mean[:, :], psM[:, 1, :], 1.0 / N, None, ALU.mult))
                link(V.tensor_tensor(tmp2[:, :], mean[:, :], mean[:, :], ALU.mult))
                V.scalar_tensor_tensor(out=var[:, :], in0=psM[:, 0, :], scalar=1.0 / N, in1=tmp2[:, :],
                                       op0=ALU.mult, op1=ALU.subtract).then_inc(s_vr, 1)
                link(V.tensor_tensor(mean[:, :], mean[:, :], B2, ALU.add))
                dve.wait_ge(s_sd2, 1)
                link(V.reciprocal(var[:, :], var[:, :]))
                link(V.tensor_tensor(var[:, :], var[:, :], G2, ALU.mult))
                link(V.tensor_tensor(tmp2[:, :], B2, mean[:, :], ALU.subtract))
                link(V.tensor_tensor(tmp2[:, :], tmp2[:, :], var[:, :], ALU.mult))
                link(V.tensor_tensor(shift[:, :], tmp2[:, :], BE2, ALU.add))
                link(V.tensor_tensor(W2s[:, :, :], W2[:, :, :], over(var[:, :], KB), ALU.mult))
        gram_scope.close()

        half_neg = sb("half_neg", [P, QT])
        R3 = 5
        with phase() as scope:
            xin = sb("p3_xin", [P, R3, QT, D], F32, scope)
            xT = sb("p3_xT", [P, 2, KB, QT, P], F32, scope)
            yo = sb("p3_yo", [P, R3, QT, D], F32, scope)
            y3 = sb("p3_y3", [P, R3, QT, D], F32, scope)
            small = sb("p3_small", [P, 2, R3, 3, QT], F32, scope)
            st = sb("p3_st", [P, 2, R3, QT, 6], F32, scope)
            mv = sb("p3_mv", [P, 2, R3, QT, 2], F32, scope)
            psT = [pb(f"p3_psT{k}", [P, KB, QT, P], F32, scope) for k in range(2)]
            psY = [pb(f"p3_psY{k}", [P, QT, D], F32, scope) for k in range(2)]
            s_t, s_tc, s_y, s_o, s_th, s_half, s_dp, s_spg = (sem(f"p3_{n}") for n in ("t", "tc", "y", "o", "th", "half", "dp", "sp"))
            s_add, s_bn, s_mv, s_ve, s_rs, s_nm, s_norm = ([sem(f"p3_{n}{l}") for l in range(2)] for n in (
                "add", "bn", "mv", "ve", "rs", "nm", "norm"))
            s_x = [sem(f"p3_x{k}") for k in range(R3)]
            s_st3 = [sem(f"p3_st3{k}") for k in range(R3)]
            s_st4 = [sem(f"p3_st4{k}") for k in range(R3)]
            block = scope.enter_context(nc.Block())
            LAST3 = NQ + 2
            buf3 = (xin, y3)

            @block.sync
            def _(sp):
                def load(q):
                    wait(sp, s_st3[slot(q)], nth(q, 16))
                    wait(sp, s_add[1], ev(q, 1, 1 - R3))
                    sp.sem_inc(s_spg, 1)
                    sp.dma_start(xin[0:rows(q), slot(q), :, :].rearrange("p j d -> p (j d)"),
                                 quad_of(x2, q)).then_inc(s_x[slot(q)], 16)

                def store_quad(l, table, q, s_st):
                    sp.wait_ge(s_norm[l], ev(q, 1, 1))
                    sp.sem_inc(s_spg, 1)
                    sp.dma_start(quad_of(table, q),
                                 buf3[l][0:rows(q), slot(q), :, :].rearrange("p j d -> p (j d)")).then_inc(s_st[slot(q)], 16)

                def step(q):
                    if inside(sh(q, 2), 0, NQ):
                        load(sh(q, 2))
                    if inside(sh(q, -2), 0, NQ):
                        store_quad(0, x3, sh(q, -2), s_st3)
                    if inside(sh(q, -3), 0, NQ):
                        store_quad(1, out, sh(q, -3), s_st4)

                load((None, 0, R3))
                load((None, 1, R3))
                steps(sp, step, 0, LAST3 + 1, ring=R3)
                for c in range(R3):
                    sp.wait_ge(s_st3[c], 16 * len(range(c, NQ + 1, R3)))
                    sp.wait_ge(s_st4[c], 16 * len(range(c, NQ + 1, R3)))

            @block.tensor
            def _(pe):
                def step(c):
                    q, k = sh(c, 1), 0
                    if inside(q, 0, NQ):
                        r, s = rows(q), slot(q)
                        pe.wait_ge(s_x[s], nth(q, 16, 16))
                        wait(pe, s_tc, ev(q))
                        for j in range(QT):
                            for b in range(KB):
                                last = T.transpose(psT[0][:, b, j, 0:r], xin[0:r, s, j, b * P:(b + 1) * P], ident[0:r, 0:r])
                        last.then_inc(s_t, 1)
                    q = c
                    if inside(q, 0, NQ):
                        r = rows(q)
                        pe.wait_ge(s_tc, ev(q, 1, 1))
                        wait(pe, s_o, ev(q))
                        for j in range(QT):
                            for b in range(KB):
                                last = T.matmul(psY[0][0:r, j, :], xT[:, 0, b, j, 0:r], W2s[:, b, :],
                                                start=(b == 0), stop=(b == KB - 1))
                        last.then_inc(s_y, 1)

                step((None, -1, R3))
                steps(pe, step, 0, NQ, ring=R3)

            @block.scalar
            def _(act):
                def norm(l, q):
                    r, s = rows(q), slot(q)
                    act.wait_ge(s_nm[l], ev(q, 1, 1))
                    for j in range(QT):
                        last = A.activation(buf3[l][0:r, s, j, :], buf3[l][0:r, s, j, :], ACT.Identity,
                                            bias=small[0:r, l, s, 2, j:j + 1], scale=small[0:r, l, s, 1, j:j + 1])
                    last.then_inc(s_norm[l], 1)

                def step(q):
                    nxt = sh(q, 1)
                    if inside(nxt, 0, NQ):
                        r = rows(nxt)
                        act.wait_ge(s_t, ev(nxt, 1, 1))
                        wait(act, s_y, ev(nxt))
                        A.activation(xT[:, 0, :, :, 0:r], psT[0][:, :, :, 0:r], ACT.Copy).then_inc(s_tc, 1)
                    if inside(q, 0, NQ):
                        r, s = rows(q), slot(q)
                        act.wait_ge(s_o, ev(q, 1, 1))
                        A.activation(yo[0:r, s, :, :], yo[0:r, s, :, :], ACT.Tanh).then_inc(s_th, 1)
                    if inside(sh(q, -1), 0, NQ):
                        norm(0, sh(q, -1))
                    if inside(sh(q, -2), 0, NQ):
                        norm(1, sh(q, -2))

                step((None, -1, R3))
                steps(act, step, 0, LAST3, ring=R3)

            @block.gpsimd
            def _(pool):
                def rsqrt(l, q):
                    r, s = rows(q), slot(q)
                    pool.wait_ge(s_ve[l], ev(q, 1, 1))
                    pool.sem_inc(s_dp, 1)
                    pool.tensor_tensor(small[0:r, l, s, 1, :], small[0:r, l, s, 0, :], half_neg[0:r, :],
                                       ALU.pow).then_inc(s_rs[l], 1)

                def step(q):
                    if inside(sh(q, -1), 0, NQ):
                        rsqrt(0, sh(q, -1))
                    if inside(sh(q, -2), 0, NQ):
                        rsqrt(1, sh(q, -2))

                pool.memset(half_neg[:, :], -0.5).then_inc(s_half, 1)
                pool.wait_ge(s_half, 1)
                steps(pool, step, 0, LAST3, ring=R3)

            @block.vector
            def _(dve):
                s_vp = sem("p3_vp")

                def stats(l, q):
                    r, s = rows(q), slot(q)
                    dve.wait_ge(s_add[l], ev(q, 1, 1))
                    for j in range(QT):
                        last = V.bn_stats(st[0:r, l, s, j, :], buf3[l][0:r, s, j, :])
                    last.then_inc(s_bn[l], 1)
                    dve.wait_ge(s_bn[l], ev(q, 1, 1))
                    dve.sem_inc(s_vp, 1)
                    for j in range(QT):
                        last = V.bn_aggr(mv[0:r, l, s, j, :], st[0:r, l, s, j, :])
                    last.then_inc(s_mv[l], 1)
                    dve.wait_ge(s_mv[l], ev(q, 1, 1))
                    V.tensor_scalar(small[0:r, l, s, 0, :], mv[0:r, l, s, :, 1], EPS, None, ALU.add).then_inc(s_ve[l], 1)

                def neg_mean(l, q):
                    r, s = rows(q), slot(q)
                    dve.wait_ge(s_rs[l], ev(q, 1, 1))
                    V.scalar_tensor_tensor(out=small[0:r, l, s, 2, :], in0=mv[0:r, l, s, :, 0], scalar=-1.0,
                                           in1=small[0:r, l, s, 1, :], op0=ALU.mult, op1=ALU.mult).then_inc(s_nm[l], 1)

                def step(q):
                    b, c = sh(q, -1), sh(q, -2)
                    if inside(q, 0, NQ):
                        r, s = rows(q), slot(q)
                        dve.wait_ge(s_y, ev(q, 1, 1))
                        V.tensor_tensor(yo[0:r, s, :, :], psY[0][0:r, :, :],
                                        shift[0:r, :].unsqueeze(1).broadcast_to([r, QT, D]), ALU.add).then_inc(s_o, 1)
                    if inside(b, 0, NQ):
                        r, s = rows(b), slot(b)
                        dve.wait_ge(s_th, ev(b, 1, 1))
                        V.tensor_tensor(xin[0:r, s, :, :], xin[0:r, s, :, :], yo[0:r, s, :, :], ALU.add).then_inc(s_add[0], 1)
                        stats(0, b)
                    if inside(c, 0, NQ):
                        r, s = rows(c), slot(c)
                        dve.wait_ge(s_norm[0], ev(c, 1, 1))
                        wait(dve, s_st4[s], nth(c, 16))
                        V.tensor_tensor(y3[0:r, s, :, :], xin[0:r, s, :, :],
                                        c3[0:r, :].unsqueeze(1).broadcast_to([r, QT, D]), ALU.add).then_inc(s_add[1], 1)
                        stats(1, c)
                    if inside(b, 0, NQ):
                        neg_mean(0, b)
                    if inside(c, 0, NQ):
                        neg_mean(1, c)

                steps(dve, step, 0, LAST3, ring=R3)

        def store_of(table_rows, q, of):
            return chunk_of(of, q).rearrange("p n d -> p (n d)")

        def load_group(sp, g, pairs, s_to, s_go, frees):
            n, h = group_tiles(g), slot(g)
            i, c, _ = g
            t = c * GT if i is None else i * (2 * GT) + c * GT
            for s, v in frees:
                wait(sp, s, v)
                sp.sem_inc(s_go, 1)
            for table, to in pairs:
                sp.dma_start(to[:, h, 0:n, :].rearrange("p n d -> p (n d)"),
                             table[:, bass.ds(t * D, n * D)]).then_inc(s_to[h], 16)

        with phase() as scope:
            psT = pb("e2b_psT", [P, KB, QT, P], F32, scope)
            psY = pb("e2b_psY", [P, QT, D], F32, scope)
            (s_pk, s_go, s_vgo, s_spgo, s_t, s_tc, s_y, s_o, s_th, s_add, s_bn, s_mv, s_sd, s_rs, s_nm, s_norm) = (
                sem(f"e2b_{n}") for n in ("pk", "go", "vgo", "spgo", "t", "tc", "y", "o", "th", "add", "bn", "mv", "sd",
                                          "rs", "nm", "norm"))
            s_in2 = [sem(f"e2b_in{k}") for k in range(2)]
            s_sc = [sem(f"e2b_sc{k}") for k in range(2)]
            s_lin = [sem(f"e2b_lin{k}") for k in range(2)]
            block = scope.enter_context(nc.Block())

            @block.sync
            def _(sp):
                def step(g):
                    if inside(g, 0, 2 * GI):
                        h = slot(g)
                        load_group(sp, g, ((agg2, msg), (x2e, own)), s_in2, s_spgo,
                                   ((s_sc[h], nth(g, 16 * GT)), (s_t, ev(g, 2, -2)), (s_lin[h], nth(g, 32))))
                    b = sh(g, -1)
                    if inside(b, 0, 2 * GI):
                        i, c, _ = b
                        for k in range(2 if group_tiles(b) == GT else 1):
                            store(sp, x3e, own, (i, 2 * c + k, 4), s_norm, s_spgo, s_lin[slot(b)])

                groups(sp, step, 2 * GI + 1)
                sp.wait_ge(s_lin[0], 32 * GI + 16)
                sp.wait_ge(s_lin[1], 32 * GI)

            @block.gpsimd
            def _(pool):
                def step(g):
                    wait(pool, s_sc[slot(g)], nth(g, 16 * GT))
                    indices(pool, 1, g, s_pk, s_go)
                    pool.wait_ge(s_norm, FIX + 1 if group_tiles(g) == 1 else ev(g, 2, 2))
                    pool.sem_inc(s_go, 1)
                    scatter_rows(pool, x3, slot(g), group_tiles(g), s_sc[slot(g)])

                groups(pool, step, 2 * GI)
                pool.wait_ge(s_sc[0], 16 * (GI * GT + 1))
                pool.wait_ge(s_sc[1], 16 * GI * GT)

            @block.tensor
            def _(pe):
                def step(q):
                    pe.wait_ge(s_in2[half(q)], two_loads(q))
                    wait(pe, s_tc, ev(q))
                    transposed(q, 0, msg, psT, s_t)
                    pe.wait_ge(s_tc, ev(q, 1, 1))
                    wait(pe, s_o, ev(q))
                    product(q, 0, W2s, psY, s_y)

                def two_loads(q):
                    c = 32 * (q[1] // 4 + 1)
                    return c if q[0] is None else q[0] * 32 + c

                chunks(pe, step, FIX)

            @block.scalar
            def _(act):
                def step(q):
                    if inside(q, 0, FIX):
                        n = ntiles(q)
                        act.wait_ge(s_t, ev(q, 1, 1))
                        wait(act, s_y, ev(q, 1, -1))
                        A.activation(tT[:, q[1] % 2, 0, :, 0:n, :], psT[:, :, 0:n, :], ACT.Copy).then_inc(s_tc, 1)
                        act.wait_ge(s_o, ev(q, 1, 1))
                        A.activation(o4[:, q[1] % 2, 0:n, :], o4[:, q[1] % 2, 0:n, :], ACT.Tanh).then_inc(s_th, 1)
                    b = sh(q, -1)
                    if inside(b, 0, FIX):
                        deviation(0, b, s_mv, s_sd)
                        normalise(0, b, own_row, s_nm, s_norm)

                chunks(act, step, FIX + 1)

            @block.vector
            def _(dve):
                def step(q):
                    if inside(q, 0, FIX):
                        n = ntiles(q)
                        dve.wait_ge(s_y, ev(q, 1, 1))
                        wait(dve, s_add, ev(q, 1, -1))
                        V.tensor_tensor(o4[:, q[1] % 2, 0:n, :], psY[:, 0:n, :], over(shift[:, :], n), ALU.add).then_inc(s_o, 1)
                    b = sh(q, -1)
                    if inside(b, 0, FIX):
                        n = ntiles(b)
                        dve.wait_ge(s_th, ev(b, 1, 1))
                        V.tensor_tensor(chunk_of(own, b), o4[:, b[1] % 2, 0:n, :], chunk_of(own, b), ALU.add).then_inc(s_add, 1)
                        statistics(0, b, own_row, s_add, s_bn, s_vgo, s_mv)
                        reciprocals(0, b, s_sd, s_rs, s_nm)

                chunks(dve, step, FIX + 1)

        score = sb("score", [P, EC, HEADS])
        with phase() as scope:
            psT = [pb(f"e3_psT{k}", [P, KB, QT, P], F32, scope) for k in "AB"]
            psY = pb("e3_psY", [P, QT, D], F32, scope)
            psE = pb("e3_psE", [P, QT, HEADS], F32, scope)
            s_pk, s_go, s_spgo, s_ta, s_t, s_tc, s_ya, s_y, s_h = (sem(f"e3_{n}") for n in (
                "pk", "go", "spgo", "ta", "t", "tc", "ya", "y", "h"))
            s_g = [sem(f"e3_g{k}") for k in range(2)]
            s_lin = [sem(f"e3_lin{k}") for k in range(2)]
            block = scope.enter_context(nc.Block())

            @block.gpsimd
            def _(pool):
                def step(g):
                    wait(pool, s_t, ev(g, 2, -2))
                    indices(pool, 1, g, s_pk, s_go)
                    for u in range(GT):
                        gather(pool, x3, msg[:, slot(g), u, :], slot(g), u, 0, s_g[slot(g)])
                        gather(pool, x3, own[:, slot(g), u, :], slot(g), u, 1, s_g[slot(g)])

                groups(pool, step, 2 * GI - 1)

            @block.tensor
            def _(pe):
                def step(q):
                    pe.wait_ge(s_g[half(q)], landed(q, 2))
                    wait(pe, s_tc, ev(q))
                    transposed(q, 0, msg, psT[0], s_ta)
                    transposed(q, 1, own, psT[1], s_t)
                    pe.wait_ge(s_tc, ev(q, 1, 1))
                    wait(pe, s_h, ev(q))
                    product(q, 0, W3, psY, s_ya)
                    for j in range(ntiles(q)):
                        for k, weights in enumerate((Was, Wad)):
                            for b in range(KB):
                                last = T.matmul(psE[:, j, :], tT[:, q[1] % 2, k, b, j, :], weights[:, b, :],
                                                start=(k == 0 and b == 0), stop=(k == 1 and b == KB - 1))
                    last.then_inc(s_y, 1)

                chunks(pe, step, FIX - 1)

            @block.scalar
            def _(act):
                def step(q):
                    n = ntiles(q)
                    act.wait_ge(s_t, ev(q, 1, 1))
                    wait(act, s_y, ev(q, 1, -1))
                    for k in range(2):
                        last = A.activation(tT[:, q[1] % 2, k, :, 0:n, :], psT[k][:, :, 0:n, :], ACT.Copy)
                    last.then_inc(s_tc, 1)

                chunks(act, step, FIX - 1)

            @block.vector
            def _(dve):
                def step(q):
                    n, h, j0 = ntiles(q), half(q), q[1] % 2 * 4
                    dve.wait_ge(s_y, ev(q, 1, 1))
                    wait(dve, s_lin[h], stored(q))
                    V.tensor_copy(tot[:, h, j0:j0 + n, :], psY[:, 0:n, :])
                    V.tensor_copy(score[:, bass.ds(tile0(q), n), :], psE[:, 0:n, :]).then_inc(s_h, 1)

                chunks(dve, step, FIX - 1)

            @block.sync
            def _(sp):
                chunks(sp, lambda q: store(sp, h3, tot, q, s_h, s_spgo, s_lin[half(q)]), FIX - 1)
                sp.wait_ge(s_lin[0], 32 * GI)
                sp.wait_ge(s_lin[1], 32 * GI)

        attend = sb("attend", [P, EC, HEADS])
        rden = sb("rden", [P, TOTAL, HEADS])
        with phase() as scope:
            eh = sb("eh", [P, HEADS, EC], F32, scope)
            fwd = sb("fwd", [P, HEADS, TOTAL], F32, scope)
            bwd = sb("bwd", [P, HEADS, EC], F32, scope)
            pf = sb("pf", [P, 2, EC], F32, scope)
            pbk = sb("pbk", [P, 2, EC], F32, scope)
            dg = sb("dg", [P, 2, HEADS, P], F32, scope)
            cr = sb("cr", [P, 2, HEADS, P], F32, scope)
            edge_in = sb("edge_in", [P, 2, HEADS], F32, scope)
            ends = sb("ends", [P, HEADS], F32, scope)
            psC = [pb(f"s3_psC{k}", [P, HEADS, P], F32, scope) for k in range(2)]
            psD = pb("s3_psD", [P, HEADS], F32, scope)
            s_c, s_dg3, s_cr, s_sub, s_ex, s_tl, s_dn = (sem(f"s3_{n}") for n in ("c", "dg", "cr", "sub", "ex", "tl", "dn"))
            block = scope.enter_context(nc.Block())

            @block.tensor
            def _(pe):
                pe.wait_ge(s_dg3, 1)
                for k in range(2):
                    for a in range(2):
                        last = T.matmul(psC[k][:, 4 * a:4 * a + 4, :], ones[:, :], dg[:, k, 4 * a:4 * a + 4, :], start=True, stop=True)
                last.then_inc(s_cr, 1)
                pe.wait_ge(s_tl, 1)
                T.matmul(psD[:, :], feeds[1][:, :], ends[:, :], start=True, stop=True).then_inc(s_dn, 1)

            @block.scalar
            def _(act):
                act.wait_ge(s_sub, 1)
                A.activation(eh[:, :, :], eh[:, :, :], ACT.Exp).then_inc(s_ex, 1)

            @block.vector
            def _(dve):
                chain = [0]

                def link(ins):
                    chain[0] += 1
                    ins.then_inc(s_c, 1)
                    dve.wait_ge(s_c, chain[0])

                link(V.scalar_tensor_tensor(out=eh[:, :, :], in0=score[:, :, :].rearrange("p t h -> p h t"), scalar=0.2,
                                            in1=score[:, :, :].rearrange("p t h -> p h t"), op0=ALU.mult, op1=ALU.max))
                for k, of in ((0, go_on[1]), (1, whole[1])):
                    link(V.tensor_scalar(pf[:, k, :], of[:, :], 1.0, 1e30, ALU.subtract, ALU.mult))
                link(V.tensor_scalar(pbk[:, 1, :], on_next[:, :], 1.0, 1e30, ALU.subtract, ALU.mult))
                link(V.tensor_copy(pbk[:, 0, :], pbk[:, 1, :]))
                link(V.memset(pbk[:, 0, EC - 1:EC], -1e30))
                for hd in range(HEADS):
                    V.tensor_tensor_scan(fwd[:, hd, 0:EC], pf[:, 0, :], eh[:, hd, :], -1e30, ALU.add, ALU.max)
                    last = V.tensor_tensor_scan(bwd[:, hd, ::-1], pbk[:, 0, ::-1], eh[:, hd, ::-1], -1e30, ALU.add, ALU.max)
                link(last)
                for hd in range(HEADS):
                    V.tensor_scalar(dg[:, 0, hd, :], ident[:, :], fwd[:, hd, EC - 1:EC], None, ALU.mult)
                    last = V.tensor_scalar(dg[:, 1, hd, :], ident[:, :], bwd[:, hd, 0:1], None, ALU.mult)
                last.then_inc(s_dg3, 1)
                dve.wait_ge(s_cr, 1)
                for k, pen in ((0, pen_f), (1, pen_b)):
                    link(V.tensor_tensor(cr[:, k, :, :], psC[k][:, :, :], pen[:, :].unsqueeze(1).broadcast_to([P, HEADS, P]), ALU.add))
                    link(V.tensor_reduce(edge_in[:, k, :], cr[:, k, :, :], AX_X, ALU.max))
                for hd in range(HEADS):
                    V.tensor_tensor_scan(fwd[:, hd, 0:EC], pf[:, 1, :], eh[:, hd, :], edge_in[:, 0, hd:hd + 1], ALU.add, ALU.max)
                    last = V.tensor_tensor_scan(bwd[:, hd, ::-1], pbk[:, 1, ::-1], eh[:, hd, ::-1], edge_in[:, 1, hd:hd + 1],
                                                ALU.add, ALU.max)
                link(last)
                link(V.tensor_tensor(bwd[:, :, :], fwd[:, :, 0:EC], bwd[:, :, :], ALU.max))
                V.tensor_tensor(eh[:, :, :], eh[:, :, :], bwd[:, :, :], ALU.subtract).then_inc(s_sub, 1)
                dve.wait_ge(s_ex, 1)
                link(V.tensor_copy(attend[:, :, :], eh[:, :, :].rearrange("p h t -> p t h")))
                for hd in range(HEADS):
                    last = V.tensor_tensor_scan(fwd[:, hd, 0:EC], go_on[1][:, :], eh[:, hd, :], 0.0, ALU.mult, ALU.add)
                link(last)
                V.tensor_copy(ends[:, :], fwd[:, :, EC - 1]).then_inc(s_tl, 1)
                dve.wait_ge(s_dn, 1)
                link(V.tensor_copy(edge_in[:, 0, :], psD[:, :]))
                for hd in range(HEADS):
                    last = V.tensor_tensor_scan(fwd[:, hd, 0:EC], whole[1][:, :], eh[:, hd, :], edge_in[:, 0, hd:hd + 1],
                                                ALU.mult, ALU.add)
                link(last)
                link(V.tensor_tensor(bwd[:, :, :], fwd[:, :, 0:EC], leadend[1][:, :].unsqueeze(1).broadcast_to([P, HEADS, EC]), ALU.mult))
                link(V.tensor_reduce(fwd[:, :, EC], bwd[:, :, :], AX_X, ALU.add))
                link(V.tensor_scalar(fwd[:, :, :], fwd[:, :, :], 1e-16, None, ALU.add))
                link(V.reciprocal(fwd[:, :, :], fwd[:, :, :]))
                link(V.tensor_copy(rden[:, :, :], fwd[:, :, :].rearrange("p h t -> p t h")))

        with phase() as scope:
            psF = pb("e3b_psF", [P, D], F32, scope)[:, :]
            (s_pk, s_go, s_vgo, s_spgo, s_scaled, s_acc, s_lr, s_fix, s_o, s_add, s_bn, s_mv, s_sd, s_rs, s_nm, s_norm) = (
                sem(f"e3b_{n}") for n in ("pk", "go", "vgo", "spgo", "scaled", "acc", "lr", "fix", "o", "add", "bn", "mv",
                                          "sd", "rs", "nm", "norm"))
            s_hin = [sem(f"e3b_h{k}") for k in range(2)]
            s_own = [sem(f"e3b_own{k}") for k in range(2)]
            s_sc = [sem(f"e3b_sc{k}") for k in range(2)]
            block = scope.enter_context(nc.Block())

            @block.sync
            def _(sp):
                def step(g):
                    h = slot(g)
                    frees = ((s_sc[h], nth(g, 16 * GT)), (s_acc, ev(g, GT, 1 - GT)), (s_o, ev(g, 4, -4)))
                    if group_tiles(g) == GT:
                        load_group(sp, g, ((h3, msg),), s_hin, s_spgo, frees)
                    load_group(sp, g, ((x3e, own),), s_own, s_spgo, frees)

                groups(sp, step, 2 * GI)

            @block.gpsimd
            def _(pool):
                def step(g):
                    wait(pool, s_sc[slot(g)], nth(g, 16 * GT))
                    indices(pool, 1, g, s_pk, s_go)
                    pool.wait_ge(s_norm, FIX + 1 if group_tiles(g) == 1 else ev(g, 2, 2))
                    pool.sem_inc(s_go, 1)
                    scatter_rows(pool, out, slot(g), group_tiles(g), s_sc[slot(g)])

                groups(pool, step, 2 * GI)
                pool.wait_ge(s_sc[0], 16 * (GI * GT + 1))
                pool.wait_ge(s_sc[1], 16 * GI * GT)

            @block.tensor
            def _(pe):
                pe.wait_ge(s_acc, EC - 1)
                T.matmul(psF, feeds[1][:, :], msg[:, 1, GT - 1, :], start=True, stop=True).then_inc(s_fix, 1)

            @block.scalar
            def _(act):
                def step(q):
                    deviation(0, q, s_mv, s_sd)
                    normalise(0, q, own_row, s_nm, s_norm)

                chunks(act, step, FIX)

            @block.vector
            def _(dve):
                def by_head(a):
                    return a.rearrange("p n (h d) -> p n h d", d=HD)

                def step(q):
                    if inside(q, 0, FIX):
                        n, h, t0 = ntiles(q), half(q), tile0(q)
                        if not (q[0] is None and q[1] == FIX):
                            dve.wait_ge(s_hin[h], loads(q))
                            m = by_head(chunk_of(msg, q))
                            V.tensor_tensor(m, m, attend[:, bass.ds(t0, n), :].unsqueeze(3).broadcast_to([P, n, HEADS, HD]),
                                            ALU.mult).then_inc(s_scaled, 1)
                        accumulate(q, 1, s_scaled, ev(q, 1, 1), s_acc, s_lr, s_fix)
                        wait(dve, s_acc, t0 + (n - 1))
                        oq = o4[:, q[1] % 2, 0:n, :]
                        V.tensor_tensor(by_head(oq), by_head(chunk_of(msg, q)),
                                        rden[:, bass.ds(t0, n), :].unsqueeze(3).broadcast_to([P, n, HEADS, HD]),
                                        ALU.mult).then_inc(s_o, 1)
                        dve.wait_ge(s_o, ev(q, 2, 1))
                        V.tensor_tensor(oq, oq, over(B3, n), ALU.add).then_inc(s_o, 1)
                        dve.wait_ge(s_o, ev(q, 2, 2))
                        dve.wait_ge(s_own[h], loads(q))
                        V.scalar_tensor_tensor(out=chunk_of(own, q), in0=oq, scalar=0.0, in1=chunk_of(own, q),
                                               op0=ALU.max, op1=ALU.add).then_inc(s_add, 1)
                        statistics(0, q, own_row, s_add, s_bn, s_vgo, s_mv)
                    b = sh(q, -1)
                    if inside(b, 0, FIX):
                        reciprocals(0, b, s_sd, s_rs, s_nm)

                V.memset(lr[:, :], 0.0).then_inc(s_lr, 1)
                chunks(dve, step, FIX + 1)


_INS = ["x", "src", "dst", "edge_weight", "L0_gnn_W", "L1_gnn_W", "L1_gnn_b", "L1_gnn_ln_gamma", "L1_gnn_ln_beta",
        "L1_gnn_res_W", "L1_gnn_res_b", "L2_gnn_W", "L2_gnn_b", "L2_gnn_gamma", "L2_gnn_beta", "L3_gnn_W",
        "L3_gnn_att_src", "L3_gnn_att_dst", "L3_gnn_bias"]


def kernel(**inputs):
    import numpy as np
    import concourse.bacc as bacc
    from concourse.bass_utils import run_bass_kernel_spmd

    nc = bacc.Bacc("TRN2", target_bir_lowering=False, num_devices=1)
    arrays, args = {}, []
    for name in _INS:
        a = np.ascontiguousarray(inputs[name])
        arrays[f"in_{name}"] = a
        args.append(nc.dram_tensor(f"in_{name}", a.shape, mybir.dt.from_np(a.dtype), kind="ExternalInput").ap())
    args.append(nc.dram_tensor("out_0", (N, D), F32, kind="ExternalOutput").ap())
    build(nc, *args)
    r = run_bass_kernel_spmd(nc, [arrays], core_ids=[0])
    return r.results[0]["out_0"]
```

```python
from contextlib import ExitStack, contextmanager

import concourse.bass as bass
from concourse import mybir

F32 = mybir.dt.float32
BF16 = mybir.dt.bfloat16
I32 = mybir.dt.int32
ALU = mybir.AluOpType
ACT = mybir.ActivationFunctionType
AX_X = mybir.AxisListType.X

P = 128
D = 256
KB = D // P
EPS = 1e-5

N = 100000
QT = 4
NPP = N // (P * QT) * QT
NQ = NPP // QT
TAIL = (N - P * NPP) // QT
RING = 3
ITERS = NQ // RING

E = 25000
EC = -(-E // P)
EP = P * EC
GT = 7
GI = EC // (2 * GT)
PADKEY = (1 << 17) - 1
SKIP = 1 << 18
DIGITS = ((0, 5), (5, 4), (9, 4), (13, 4))
ND = max(1 << bits for _, bits in DIGITS)


def ev(q, mul=1, add=0):
    i, c, u = q
    return c * mul + add if i is None else i * (u * mul) + (c * mul + add)


def sh(q, k):
    return (q[0], q[1] + k, q[2])


def slot(q):
    return q[1] % q[2]


def nth(q, mul=1, add=0):
    i, c, u = q
    return c // u * mul + add if i is None else i * mul + (c // u * mul + add)


def inside(q, lo, hi):
    return q[0] is not None or lo <= q[1] <= hi


def wait(eng, sem, value):
    if type(value) is not int or value > 0:
        eng.wait_ge(sem, value)


def rows(q):
    return TAIL if q[0] is None and q[1] == NQ else P


def value(eng, v):
    return v if type(v) is int else eng.snap(v)


def quad_of(table, q, at=None):
    if rows(q) == TAIL:
        return table[P * NPP:N, :].rearrange("(p j) d -> p (j d)", j=QT)
    return table[0:P * NPP, :].rearrange("(p n) d -> p (n d)", n=NPP)[:, bass.ds(ev(q, QT * D) if at is None else at, QT * D)]


def steps(eng, step, first, last, cuts=(), at_cut=None, ring=RING):
    iters = NQ // ring
    for c in range(first, 2 * ring):
        step((None, c, ring))
    edges = [2] + list(cuts) + [iters - 1]
    for n in range(len(edges) - 1):
        if n >= 1:
            at_cut(n - 1, edges[n])
        with eng.Fori(edges[n], edges[n + 1]) as i:
            for u in range(ring):
                step((i, u, ring))
    for c in range(ring * (iters - 1), last + 1):
        step((None, c, ring))


FIX = 4 * GI


def tile0(q):
    i, c, _ = q
    at = c // 4 * 2 * GT + c % 4 // 2 * GT + c % 2 * 4
    return at if i is None else i * (2 * GT) + at


def ntiles(q):
    if q[0] is None and q[1] >= FIX:
        return 1
    return 4 - q[1] % 2


def half(q):
    return q[1] % 4 // 2


def landed(q, per):
    if q[0] is None and q[1] >= FIX:
        return 16 * per * (GI * GT + 1)
    c = 16 * per * GT * (q[1] // 4 + 1)
    return c if q[0] is None else q[0] * (16 * per * GT) + c


def loads(q):
    c = 16 * (q[1] // 4 + 1)
    return c if q[0] is None else q[0] * 16 + c


def chunks(eng, step, last):
    for c in range(8):
        step((None, c, 4))
    with eng.Fori(2, GI) as i:
        for u in range(4):
            step((i, u, 4))
    for c in range(FIX, last + 1):
        step((None, c, 4))


def groups(eng, step, last):
    for g in range(4):
        step((None, g, 2))
    with eng.Fori(2, GI) as i:
        for u in range(2):
            step((i, u, 2))
    for g in range(2 * GI, last + 1):
        step((None, g, 2))


def group_tiles(q):
    return 1 if q[0] is None and q[1] >= 2 * GI else GT


def build(nc, x, src, dst, ew, w0, w1, b1, g1, be1, wr, br, w2, b2, g2, be2, w3, as3, ad3, b3, out):
    ctx = ExitStack()
    with ctx:
        def sb(name, shape, dt=F32, scope=ctx):
            return scope.enter_context(nc.sbuf_tensor(name, shape, dt))

        def pb(name, shape, dt=F32, scope=ctx):
            return scope.enter_context(nc.psum_tensor(name, shape, dt))

        taken = []

        def sem(name):
            taken.append(nc.alloc_semaphore(name=name))
            return taken[-1]

        @contextmanager
        def phase():
            with ExitStack() as scope:
                yield scope
            nc.clear_and_free_semaphores(list(taken))
            nc.all_engine_barrier()
            taken.clear()

        def dram(name, shape, dt=F32):
            return nc.dram_tensor(name, shape, dt, kind="Internal").ap()

        x1 = dram("x1", [N, D])
        x2 = dram("x2", [N, D])
        x3 = dram("x3", [N, D])
        sorted_src = dram("sorted_src", [EP + 2, 4], I32)
        sorted_dst = dram("sorted_dst", [EP + 2, 4], I32)
        rec_dram = (sorted_src, sorted_dst)

        ident = sb("ident", [P, P])
        ones = sb("ones", [P, P])
        before = sb("before", [P, P])
        eps = sb("eps", [P, 1])
        W0 = sb("W0", [P, KB, D])
        WrI = sb("WrI", [P, KB, D])
        WZ = sb("WZ", [P, KB, 2 * D])
        W1T = sb("W1T", [P, KB, D])
        W2 = sb("W2", [P, KB, D])
        c1 = sb("c1", [P, D])
        vec = sb("vec", [P, 8, D])
        B1, G1, BE1, BR, B2, G2, BE2, B3 = (vec[:, k, :] for k in range(8))
        c3 = sb("c3", [P, D])
        rec = [sb(f"rec{k}", [P, EC, 4], I32) for k in range(2)]

        with phase() as scope:
            raw = sb("raw", [P, 2, KB, D], F32, scope)
            srow = sb("srow", [1, 2, 4], I32, scope)
            cols = sb("cols", [P, 3, EC], I32, scope)
            psw = [pb(f"psw{k}", [P, KB, D], F32, scope) for k in range(4)]
            AC = sb("AC", [P, KB, D], F32, scope)
            ACT_T = sb("ACT_T", [P, KB, D], F32, scope)
            row_mean = sb("row_mean", [P, KB], F32, scope)
            s_const, s_ld, s_raw, s_fill, s_tw, s_sent, s_cols, s_id, s_link, s_ac, s_w0 = map(sem, (
                "s_const", "s_ld", "s_raw", "s_fill", "s_tw", "s_sent", "s_cols", "s_id", "s_link", "s_ac", "s_w0"))
            block = scope.enter_context(nc.Block())

            @block.sync
            def _(sp):
                sp.dma_start(raw[:, 0, :, :], wr.rearrange("(k p) d -> p k d", p=P)).then_inc(s_raw, 16)
                sp.dma_start(raw[:, 1, :, :], w1.rearrange("(k p) d -> p k d", p=P)).then_inc(s_raw, 16)
                sp.dma_start(W0[:, :, :], w0.rearrange("(k p) d -> p k d", p=P)).then_inc(s_w0, 16)
                sp.dma_start(W2[:, :, :], w2.rearrange("(k p) d -> p k d", p=P)).then_inc(s_ld, 16)
                sp.wait_ge(s_fill, 3)
                for k, a in enumerate((src, dst, ew.bitcast(I32))):
                    full = E // EC
                    sp.dma_start(cols[0:full, k, :], a[0:full * EC].rearrange("(p c) -> p c", c=EC)).then_inc(s_cols, 16)
                    sp.dma_start(cols[full:full + 1, k, 0:E - full * EC],
                                 a[full * EC:E].rearrange("(p c) -> p c", p=1)).then_inc(s_cols, 16)
                for k, a in enumerate((b1, g1, be1, br, b2, g2, be2, b3)):
                    sp.dma_start(vec[:, k, :], a.partition_broadcast(P)).then_inc(s_ld, 16)
                sp.wait_ge(s_fill, 5)
                for table in rec_dram:
                    for end in (0, 1):
                        at = end * (EP + 1)
                        sp.dma_start(table[at:at + 1, :], srow[0:1, end, :]).then_inc(s_sent, 16)
                sp.wait_ge(s_sent, 64)
                sp.wait_ge(s_ld, 144)

            @block.gpsimd
            def _(pool):
                for k, fill in ((0, PADKEY), (1, PADKEY), (2, 0)):
                    pool.memset(cols[:, k, :], fill).then_inc(s_fill, 1)
                pool.memset(srow[:, 0, :], -1).then_inc(s_fill, 1)
                pool.memset(srow[:, 1, :], -2).then_inc(s_fill, 1)
                pool.memset(ident[:, :], 0.0).then_inc(s_id, 1)
                pool.memset(before[:, :], 0.0).then_inc(s_id, 1)
                pool.memset(ones[:, :], 1.0).then_inc(s_const, 1)
                pool.memset(eps[:, :], EPS).then_inc(s_const, 1)
                pool.wait_ge(s_id, 2)
                pool.affine_select(out=ident[:, :], in_=ident[:, :], compare_op=ALU.not_equal, fill=1.0, base=0,
                                   pattern=[[-1, P]], channel_multiplier=1).then_inc(s_id, 1)
                pool.affine_select(out=before[:, :], in_=before[:, :], compare_op=ALU.is_ge, fill=1.0, base=0,
                                   pattern=[[-1, P]], channel_multiplier=1).then_inc(s_id, 1)
                pool.wait_ge(s_id, 4)

            @block.tensor
            def _(pe):
                pe.wait_ge(s_raw, 32)
                pe.wait_ge(s_id, 4)
                for m in range(2):
                    for a in range(KB):
                        for b in range(KB):
                            last = nc.tensor.transpose(psw[m][:, b, a * P:(a + 1) * P],
                                                       raw[:, m, a, b * P:(b + 1) * P], ident[:, :])
                    last.then_inc(s_tw, 1)
                pe.wait_ge(s_ac, 1)
                for a in range(KB):
                    for b in range(KB):
                        last = nc.tensor.transpose(psw[2][:, a, b * P:(b + 1) * P], AC[:, b, a * P:(a + 1) * P], ident[:, :])
                last.then_inc(s_tw, 1)
                pe.wait_ge(s_ac, 2)
                for b in range(KB):
                    for a in range(KB):
                        last = nc.tensor.matmul(psw[3][:, b, :], ACT_T[:, a, b * P:(b + 1) * P], WrI[:, a, :],
                                                start=(a == 0), stop=(a == KB - 1))
                last.then_inc(s_tw, 1)

            @block.vector
            def _(dve):
                chain = [0]

                def link(ins):
                    chain[0] += 1
                    ins.then_inc(s_link, 1)
                    dve.wait_ge(s_link, chain[0])

                dve.wait_ge(s_w0, 16)
                dve.wait_ge(s_id, 4)
                link(nc.vector.tensor_copy(AC[:, :, :], W0[:, :, :]))
                for b in range(KB):
                    at = AC[:, b, b * P:(b + 1) * P]
                    link(nc.vector.tensor_tensor(at, at, ident[:, :], ALU.add))
                link(nc.vector.tensor_reduce(row_mean[:, :], AC[:, :, :], AX_X, ALU.add))
                link(nc.vector.tensor_scalar(row_mean[:, :], row_mean[:, :], 1.0 / D, None, ALU.mult))
                for b in range(KB):
                    last = nc.vector.tensor_scalar(AC[:, b, :], AC[:, b, :], row_mean[:, b:b + 1], None, ALU.subtract)
                last.then_inc(s_ac, 1)
                dve.wait_ge(s_ac, 1)
                nc.vector.tensor_copy(WZ[:, :, 0:D], AC[:, :, :])
                for m, to in ((0, WrI), (1, W1T)):
                    dve.wait_ge(s_tw, m + 1)
                    link(nc.vector.tensor_copy(to[:, :, :], psw[m][:, :, :]))
                for b in range(KB):
                    at = WrI[:, b, b * P:(b + 1) * P]
                    link(nc.vector.tensor_tensor(at, at, ident[:, :], ALU.add))
                dve.wait_ge(s_tw, 3)
                nc.vector.tensor_copy(ACT_T[:, :, :], psw[2][:, :, :]).then_inc(s_ac, 1)
                dve.wait_ge(s_tw, 4)
                nc.vector.tensor_copy(WZ[:, :, D:2 * D], psw[3][:, :, :])
                dve.wait_ge(s_ld, 144)
                nc.vector.scalar_tensor_tensor(out=c1[:, :], in0=BE1, scalar=0.0, in1=BR, op0=ALU.max, op1=ALU.add)
                nc.vector.tensor_scalar(c3[:, :], B3, 0.0, None, ALU.max)
                dve.wait_ge(s_cols, 96)
                for k, order in ((0, (0, 1, 2)), (1, (1, 0, 2))):
                    for f in range(3):
                        nc.vector.tensor_copy(rec[k][:, :, f], cols[:, order[f], :])
                for k in range(2):
                    nc.vector.memset(rec[k][:, :, 3], 0)

        with phase() as scope:
            xin = sb("xin", [P, RING, QT, D], F32, scope)
            xT = sb("xT", [P, RING, KB, QT, P], F32, scope)
            y1 = sb("y1", [P, RING, QT, D], F32, scope)
            y2 = sb("y2", [P, RING, QT, D], F32, scope)
            small = sb("small", [P, 2, RING, 3, QT], F32, scope)
            st = sb("st", [P, 2, RING, QT, 6], F32, scope)
            mv = sb("mv", [P, 2, RING, QT, 2], F32, scope)
            digit = sb("digit", [P, EC], I32, scope)
            digit_f = sb("digit_f", [P, EC], BF16, scope)
            iota_i = sb("iota_i", [P, ND], I32, scope)
            iota_d = sb("iota_d", [P, ND], BF16, scope)
            hot = sb("hot", [P, ND, EC], BF16, scope)
            cum = sb("cum", [P, ND, EC], F32, scope)
            below = sb("below", [P, ND], F32, scope)
            count = sb("count", [P, ND], F32, scope)
            offset = sb("offset", [P, ND], F32, scope)
            rank_f = sb("rank_f", [P, EC], F32, scope)
            rank = [sb(f"rank{k}", [P, EC], I32, scope) for k in range(2)]
            rank_slot = sb("rank_slot", [P, 2, GT], I32, scope)
            rec_slot = sb("rec_slot", [P, 2, GT, 4], I32, scope)
            psT = pb("p1_psT", [P, KB, QT, P], F32, scope)
            psZ = [pb(f"psZ{k}", [P, 2, 2, D], F32, scope) for k in range(3)]

            s_x = [sem(f"s_x{k}") for k in range(RING)]
            s_st1 = [sem(f"s_st1{k}") for k in range(RING)]
            s_st2 = [sem(f"s_st2{k}") for k in range(RING)]
            s_t = sem("s_t")
            s_tc = sem("s_tc")
            s_z = sem("s_z")
            s_bn0 = sem("s_bn0")
            s_mv0 = sem("s_mv0")
            s_sd0 = sem("s_sd0")
            s_rs0 = sem("s_rs0")
            s_rows1 = sem("s_rows1")
            s_y2 = sem("s_y2")
            s_bn1, s_mv1, s_sd1, s_rs1, s_nm1 = map(sem, ("s_bn1", "s_mv1", "s_sd1", "s_rs1", "s_nm1"))
            s_rows2 = sem("s_rows2")
            s_dpass = sem("s_dpass")
            s_spass = sem("s_spass")
            s_rec = [sem(f"s_rec{k}") for k in range(2)]
            s_iota, s_chain, s_cnt, s_off, s_offr, s_rank, s_slotc, s_pass = map(sem, (
                "s_iota", "s_chain", "s_cnt", "s_off", "s_offr", "s_rank", "s_slotc", "s_pass"))
            s_scat = [sem(f"s_scat{k}") for k in range(2)]
            block = scope.enter_context(nc.Block())
            CUTS = [3, 9, 16, 23, 30, 37, 44, 51]
            LAST = NQ + 3

            def psz(q, k):
                return psZ[(2 * q[1] + k) % 3]

            def tiles(k):
                return range(2 * k, 2 * k + 2)

            @block.sync
            def _(sp):
                def load(q):
                    at, used = value(sp, ev(q, QT * D)), value(sp, ev(q, 1, 1 - RING))
                    wait(sp, s_t, used)
                    sp.sem_inc(s_spass, 1)
                    sp.dma_start(xin[0:rows(q), slot(q), :, :].rearrange("p j d -> p (j d)"),
                                 quad_of(x, q, at)).then_inc(s_x[slot(q)], 16)

                def store(of, table, q, s_from, done, s_st):
                    at, done = value(sp, ev(q, QT * D)), value(sp, done)
                    sp.wait_ge(s_from, done)
                    sp.sem_inc(s_spass, 1)
                    sp.dma_start(quad_of(table, q, at),
                                 of[0:rows(q), slot(q), :, :].rearrange("p j d -> p (j d)")).then_inc(s_st[slot(q)], 16)

                def step(q):
                    if inside(sh(q, 2), 0, NQ):
                        load(sh(q, 2))
                    b, d = sh(q, -1), sh(q, -3)
                    if inside(b, 0, NQ):
                        store(y1, x1, b, s_rows1, ev(b, 2, 2), s_st1)
                    if inside(d, 0, NQ):
                        store(y2, x2, d, s_rows2, ev(d, 1, 1), s_st2)

                load((None, 0, RING))
                load((None, 1, RING))
                steps(sp, step, 0, LAST)
                for c in range(RING):
                    sp.wait_ge(s_st1[c], 16 * len(range(c, NQ + 1, RING)))
                    sp.wait_ge(s_st2[c], 16 * len(range(c, NQ + 1, RING)))

            @block.tensor
            def _(pe):
                def transposes(q):
                    pe.wait_ge(s_x[slot(q)], nth(q, 16, 16))
                    wait(pe, s_tc, ev(q))
                    for j in range(QT):
                        for k in range(KB):
                            last = nc.tensor.transpose(psT[:, k, j, 0:rows(q)], xin[0:rows(q), slot(q), j, k * P:(k + 1) * P],
                                                       ident[0:rows(q), 0:rows(q)])
                    last.then_inc(s_t, 1)

                def products(q, k):
                    wait(pe, s_rows1, ev(q, 2, k - 2))
                    wait(pe, s_y2, ev(q, 2, k - 2))
                    for j in tiles(k):
                        for l in range(2):
                            for b in range(KB):
                                last = nc.tensor.matmul(psz(q, k)[0:rows(q), l, j % 2, :], xT[:, slot(q), b, j, 0:rows(q)],
                                                        WZ[:, b, l * D:(l + 1) * D], start=(b == 0), stop=(b == KB - 1))
                    last.then_inc(s_z, 1)

                def step(q):
                    if inside(sh(q, 1), 0, NQ):
                        transposes(sh(q, 1))
                    if inside(q, 0, NQ):
                        pe.wait_ge(s_tc, ev(q, 1, 1))
                        products(q, 0)
                        products(q, 1)

                def sort_offsets(k, i):
                    pe.wait_ge(s_rows1, 2 * RING * i - 2)
                    pe.wait_ge(s_y2, 2 * RING * i - 2)
                    pe.wait_ge(s_cnt, k + 1)
                    nc.tensor.matmul(psZ[0][:, 0, 0, 0:ND], ones[:, :], below[:, :], start=True, stop=False)
                    nc.tensor.matmul(psZ[0][:, 0, 0, 0:ND], before[:, :], count[:, :], start=False, stop=True).then_inc(s_off, 1)
                    pe.wait_ge(s_offr, k + 1)

                step((None, -1, RING))
                steps(pe, step, 0, NQ, CUTS, sort_offsets)

            @block.scalar
            def _(act):
                def copy_transposed(q):
                    act.wait_ge(s_t, ev(q, 1, 1))
                    wait(act, s_z, ev(q, 2, 2 - 2 * RING))
                    nc.scalar.activation(xT[:, slot(q), :, :, 0:rows(q)], psT[:, :, :, 0:rows(q)], ACT.Copy).then_inc(s_tc, 1)

                def deviation(l, q, lo, hi, s_mv, s_sd, count):
                    act.wait_ge(s_mv, count)
                    r, s = rows(q), slot(q)
                    nc.scalar.activation(small[0:r, l, s, 0, lo:hi], mv[0:r, l, s, lo:hi, 1], ACT.Sqrt,
                                         bias=eps[0:r, :]).then_inc(s_sd, 1)

                def scale_x1(q, k):
                    r, s = rows(q), slot(q)
                    act.wait_ge(s_rs0, ev(q, 2, k + 1))
                    wait(act, s_st1[s], nth(q, 16))
                    for j in tiles(k):
                        last = nc.scalar.activation(y1[0:r, s, j, :], psz(q, k)[0:r, 0, j % 2, :], ACT.Copy,
                                                    scale=small[0:r, 0, s, 1, j:j + 1])
                    last.then_inc(s_rows1, 1)

                def normalise_x2(q):
                    r, s = rows(q), slot(q)
                    act.wait_ge(s_nm1, ev(q, 1, 1))
                    for j in range(QT):
                        last = nc.scalar.activation(y2[0:r, s, j, :], y2[0:r, s, j, :], ACT.Identity,
                                                    bias=small[0:r, 1, s, 2, j:j + 1], scale=small[0:r, 1, s, 1, j:j + 1])
                    last.then_inc(s_rows2, 1)

                def step(q):
                    nxt, b, c = sh(q, 1), sh(q, -1), sh(q, -2)
                    here = inside(q, 0, NQ)
                    if inside(nxt, 0, NQ):
                        copy_transposed(nxt)
                    if here:
                        deviation(0, q, 0, 2, s_mv0, s_sd0, ev(q, 2, 1))
                    if inside(c, 0, NQ):
                        normalise_x2(c)
                    if here:
                        scale_x1(q, 0)
                        deviation(0, q, 2, 4, s_mv0, s_sd0, ev(q, 2, 2))
                    if inside(b, 0, NQ):
                        deviation(1, b, 0, QT, s_mv1, s_sd1, ev(b, 1, 1))
                    if here:
                        scale_x1(q, 1)

                step((None, -1, RING))
                steps(act, step, 0, NQ + 2)

            @block.vector
            def _(dve):
                def partial0(q, k):
                    r, s = rows(q), slot(q)
                    dve.wait_ge(s_z, ev(q, 2, k + 1))
                    for j in tiles(k):
                        last = nc.vector.bn_stats(st[0:r, 0, s, j, :], psz(q, k)[0:r, 0, j % 2, :])
                    last.then_inc(s_bn0, 1)

                def total0(q, k):
                    r, s = rows(q), slot(q)
                    dve.wait_ge(s_bn0, ev(q, 2, k + 1))
                    dve.sem_inc(s_dpass, 1)
                    for j in tiles(k):
                        last = nc.vector.bn_aggr(mv[0:r, 0, s, j, :], st[0:r, 0, s, j, :])
                    last.then_inc(s_mv0, 1)

                def reciprocal0(q, k):
                    r, s = rows(q), slot(q)
                    dve.wait_ge(s_sd0, ev(q, 2, k + 1))
                    nc.vector.reciprocal(small[0:r, 0, s, 1, 2 * k:2 * k + 2], small[0:r, 0, s, 0, 2 * k:2 * k + 2]).then_inc(s_rs0, 1)

                def layer1(q, k):
                    r, s = rows(q), slot(q)
                    dve.wait_ge(s_rs0, ev(q, 2, k + 1))
                    wait(dve, s_st2[s], nth(q, 16))
                    for j in tiles(k):
                        last = nc.vector.scalar_tensor_tensor(out=y2[0:r, s, j, :], in0=psz(q, k)[0:r, 1, j % 2, :],
                                                              scalar=small[0:r, 0, s, 1, j:j + 1], in1=c1[0:r, :],
                                                              op0=ALU.mult, op1=ALU.add)
                    last.then_inc(s_y2, 1)

                def partial1(q):
                    r, s = rows(q), slot(q)
                    dve.wait_ge(s_y2, ev(q, 2, 2))
                    for j in range(QT):
                        last = nc.vector.bn_stats(st[0:r, 1, s, j, :], y2[0:r, s, j, :])
                    last.then_inc(s_bn1, 1)

                def total1(q):
                    r, s = rows(q), slot(q)
                    dve.wait_ge(s_bn1, ev(q, 1, 1))
                    dve.sem_inc(s_dpass, 1)
                    for j in range(QT):
                        last = nc.vector.bn_aggr(mv[0:r, 1, s, j, :], st[0:r, 1, s, j, :])
                    last.then_inc(s_mv1, 1)

                def reciprocal1(q):
                    r, s = rows(q), slot(q)
                    dve.wait_ge(s_sd1, ev(q, 1, 1))
                    nc.vector.reciprocal(small[0:r, 1, s, 1, :], small[0:r, 1, s, 0, :]).then_inc(s_rs1, 1)

                def neg_mean1(q):
                    r, s = rows(q), slot(q)
                    dve.wait_ge(s_rs1, ev(q, 1, 1))
                    nc.vector.scalar_tensor_tensor(out=small[0:r, 1, s, 2, :], in0=mv[0:r, 1, s, :, 0], scalar=-1.0,
                                                   in1=small[0:r, 1, s, 1, :], op0=ALU.mult, op1=ALU.mult).then_inc(s_nm1, 1)

                def step(q):
                    b = sh(q, -1)
                    here, behind = inside(q, 0, NQ), inside(b, 0, NQ)
                    if here:
                        partial0(q, 0)
                    if behind:
                        layer1(b, 1)
                    if here:
                        total0(q, 0)
                    if behind:
                        partial1(b)
                    if here:
                        reciprocal0(q, 0)
                        partial0(q, 1)
                    if behind:
                        total1(b)
                    if here:
                        total0(q, 1)
                        layer1(q, 0)
                        reciprocal0(q, 1)
                    if behind:
                        reciprocal1(b)
                        neg_mean1(b)

                chain = [0]

                def link(ins):
                    chain[0] += 1
                    ins.then_inc(s_chain, 1)
                    dve.wait_ge(s_chain, chain[0])

                def rank_pass(k, _):
                    o, r = k % 2, k // 2
                    shift, bits = DIGITS[r]
                    nd = 1 << bits
                    if r:
                        dve.wait_ge(s_rec[o], 16 * r)
                    link(nc.vector.tensor_scalar(digit[:, :], rec[o][:, :, 0], shift, nd - 1,
                                                 ALU.logical_shift_right, ALU.bitwise_and))
                    link(nc.vector.tensor_copy(digit_f[:, :], digit[:, :]))
                    link(nc.vector.tensor_tensor(hot[:, 0:nd, :], digit_f[:, :].unsqueeze(1).broadcast_to([P, nd, EC]),
                                                 iota_d[:, 0:nd].unsqueeze(2).broadcast_to([P, nd, EC]), ALU.is_equal))
                    hot_v = hot[:, 0:nd, :].rearrange("p d c -> p (d c)")
                    cum_v = cum[:, 0:nd, :].rearrange("p d c -> p (d c)")
                    link(nc.vector.tensor_tensor_scan(cum_v, hot_v, hot_v, 0.0, ALU.add, ALU.max))
                    link(nc.vector.memset(below[:, :], 0.0))
                    link(nc.vector.memset(count[:, :], 0.0))
                    link(nc.vector.tensor_copy(below[:, 1:nd], cum[:, 0:nd - 1, EC - 1]))
                    nc.vector.tensor_tensor(count[:, 0:nd], cum[:, 0:nd, EC - 1], below[:, 0:nd],
                                            ALU.subtract).then_inc(s_cnt, 1)
                    dve.wait_ge(s_off, k + 1)
                    nc.vector.tensor_tensor(offset[:, :], psZ[0][:, 0, 0, 0:ND], below[:, :], ALU.subtract).then_inc(s_offr, 1)
                    dve.wait_ge(s_offr, k + 1)
                    link(nc.vector.tensor_tensor(cum[:, 0:nd, :], cum[:, 0:nd, :],
                                                 offset[:, 0:nd].unsqueeze(2).broadcast_to([P, nd, EC]), ALU.add))
                    link(nc.vector.tensor_tensor(cum[:, 0:nd, :], cum[:, 0:nd, :], hot[:, 0:nd, :], ALU.mult))
                    link(nc.vector.tensor_reduce(rank_f[:, :], cum[:, 0:nd, :].rearrange("p d c -> p c d"), AX_X, ALU.add))
                    nc.vector.tensor_copy(rank[o][:, :], rank_f[:, :]).then_inc(s_rank, 1)

                dve.wait_ge(s_iota, 1)
                link(nc.vector.tensor_copy(iota_d[:, :], iota_i[:, :]))
                steps(dve, step, 0, NQ + 1, CUTS, rank_pass)

            @block.gpsimd
            def _(pool):
                pool.iota(iota_i[:, :], pattern=[[1, ND]], base=0, channel_multiplier=0).then_inc(s_iota, 1)
                copies = 0
                for k in range(2 * len(DIGITS)):
                    o, r = k % 2, k // 2

                    def body(i, first):
                        for h in range(2):
                            if not (first and k == 0):
                                pool.wait_ge(s_scat[h], i * (16 * GT) + k * GI * 16 * GT)
                            pool.tensor_copy(rank_slot[:, h, :], rank[o][:, bass.ds(i * (2 * GT) + h * GT, GT)])
                            pool.tensor_copy(rec_slot[:, h, :, :], rec[o][:, bass.ds(i * (2 * GT) + h * GT, GT), :]).then_inc(s_slotc, 1)
                            pool.wait_ge(s_slotc, i * 2 + (k * GI * 2 + h + 1))
                            pool.sem_inc(s_pass, 1)
                            for u in range(GT):
                                pool.indirect_dma_start(
                                    out=rec_dram[o][:, :], out_offset=bass.IndirectOffsetOnAxis(ap=rank_slot[:, h, u:u + 1], axis=0),
                                    in_=rec_slot[:, h, u, :], in_offset=None, bounds_check=EP + 1,
                                    oob_is_err=False).then_inc(s_scat[h], 16)

                    pool.wait_ge(s_rank, k + 1)
                    body(0, True)
                    with pool.Fori(1, GI) as i:
                        body(i, False)
                    for h in range(2):
                        pool.wait_ge(s_scat[h], (k + 1) * GI * 16 * GT)
                    pool.dma_start(rec[o][:, :, :].rearrange("p c w -> p (c w)"),
                                   rec_dram[o][1:EP + 1, :].rearrange("(p c) w -> p (c w)", c=EC)).then_inc(s_rec[o], 16)
                for o in range(2):
                    pool.wait_ge(s_rec[o], 16 * len(DIGITS))

        inv_deg_src = dram("inv_deg_src", [N, 1])
        dinv_dst = dram("dinv_dst", [N, 1])
        deg_table = (inv_deg_src, dinv_dst)
        go_on = [sb(f"go_on{o}", [P, EC]) for o in range(2)]
        whole = [sb(f"whole{o}", [P, EC]) for o in range(2)]
        leadend = [sb(f"leadend{o}", [P, EC]) for o in range(2)]
        pack = [sb(f"pack{o}", [P, EC + 1, 3], I32) for o in range(2)]
        scale = [sb(f"scale{o}", [P, EC + 1]) for o in range(2)]
        feeds = [sb(f"feeds{o}", [P, P]) for o in range(2)]
        inv_deg_dst = sb("inv_deg_dst", [P, EC + 1])
        weight = sb("weight", [P, EC])
        wsum = sb("wsum", [P, EC + 1])
        valid = sb("valid", [P, EC + 1])
        on_next = sb("on_next", [P, EC])
        pen_f = sb("pen_f", [P, P])
        pen_b = sb("pen_b", [P, P])
        TOTAL = EC + 1
        W3 = sb("W3", [P, KB, D])
        Was = sb("Was", [P, KB, 8])
        Wad = sb("Wad", [P, KB, 8])
        HEADS, HD = as3.shape

        with phase() as scope:
            recp = [sb(f"recp{o}", [P, EC, 4], I32, scope) for o in range(2)]
            recn = [sb(f"recn{o}", [P, EC, 4], I32, scope) for o in range(2)]
            att = sb("att", [P, 2, HEADS, HD], F32, scope)
            prod = sb("prod", [P, HEADS, HD], F32, scope)
            keyf = sb("keyf", [P, EC], F32, scope)
            keyp = sb("keyp", [P, EC], F32, scope)
            keyn = sb("keyn", [P, EC], F32, scope)
            last_e = sb("last_e", [P, EC], F32, scope)
            lead = sb("lead", [P, EC], F32, scope)
            fin = sb("fin", [P, EC + 1], F32, scope)
            idxf = sb("idxf", [P, EC + 1], F32, scope)
            ones_e = sb("ones_e", [P, EC], F32, scope)
            cnt = sb("cnt", [P, EC + 1], F32, scope)
            tmp = sb("tmp", [P, EC + 1], F32, scope)
            start = sb("start", [P, 2], F32, scope)
            diag = sb("diag", [P, 2, P], F32, scope)
            after = sb("after", [P, P], F32, scope)
            before_t = sb("before_t", [P, P], F32, scope)
            full1 = sb("full1", [P, N // P], F32, scope)
            idx_slot = sb("idx_slot", [P, 2, GT], I32, scope)
            val_slot = sb("val_slot", [P, 2, GT], F32, scope)
            ps = pb("ps", [P, 2, P], F32, scope)
            psc = pb("psc", [P, 512], F32, scope)
            (s_in, s_w3, s_one, s_init, s_v, s_dg, s_row, s_tails, s_st0, s_cnt1, s_sq, s_deg, s_slot, s_pass2, s_m) = map(sem, (
                "s_in", "s_w3", "s_one", "s_init", "s_v", "s_dg", "s_row", "s_tails", "s_st0", "s_cnt1", "s_sq", "s_deg",
                "s_slot", "s_pass2", "s_m"))
            s_dsc = [sem(f"s_dsc{k}") for k in range(2)]
            block = scope.enter_context(nc.Block())

            @block.sync
            def _(sp):
                for o in range(2):
                    for t, at in ((recp[o], 0), (recn[o], 2)):
                        sp.dma_start(t[:, :, :].rearrange("p c w -> p (c w)"),
                                     rec_dram[o][at:at + EP, :].rearrange("(p c) w -> p (c w)", c=EC)).then_inc(s_in, 16)
                sp.dma_start(W3[:, :, :], w3.rearrange("(k p) h d -> p k (h d)", p=P)).then_inc(s_w3, 16)
                for k, a in enumerate((as3, ad3)):
                    sp.dma_start(att[:, k, :, :], a.partition_broadcast(P)).then_inc(s_w3, 16)
                sp.wait_ge(s_one, 1)
                for table in deg_table:
                    sp.dma_start(table[0:P * (N // P), 0].rearrange("(p c) -> p c", p=P), full1[:, :]).then_inc(s_init, 16)
                    sp.dma_start(table[P * (N // P):N, 0].rearrange("(p c) -> p c", p=1),
                                 full1[0:1, 0:N % P]).then_inc(s_init, 16)

            @block.gpsimd
            def _(pool):
                pool.memset(full1[:, :], 1.0).then_inc(s_one, 1)
                pool.memset(ones_e[:, :], 1.0).then_inc(s_m, 1)
                pool.memset(after[:, :], 0.0).then_inc(s_m, 1)
                pool.wait_ge(s_m, 2)
                pool.affine_select(out=after[:, :], in_=after[:, :], compare_op=ALU.is_ge, fill=1.0, base=0,
                                   pattern=[[-1, P]], channel_multiplier=1).then_inc(s_m, 1)
                pool.memset(before_t[:, :], 0.0).then_inc(s_m, 1)
                pool.wait_ge(s_m, 4)
                pool.affine_select(out=before_t[:, :], in_=before_t[:, :], compare_op=ALU.is_ge, fill=1.0, base=0,
                                   pattern=[[1, P]], channel_multiplier=-1).then_inc(s_m, 1)
                pool.wait_ge(s_init, 64)
                for o in range(2):
                    pool.wait_ge(s_deg, o + 1)

                    def body(i, first, n=GT, halves=2):
                        for h in range(halves):
                            if not first:
                                pool.wait_ge(s_dsc[h], i * (16 * GT) + (o * (GI * GT + 1) if h == 0 else o * GI * GT) * 16)
                            t = i * (2 * GT) + h * GT
                            pool.tensor_copy(idx_slot[:, h, 0:n], pack[o][:, bass.ds(t, n), 2])
                            pool.tensor_copy(val_slot[:, h, 0:n], scale[o][:, bass.ds(t, n)]).then_inc(s_slot, 1)
                            pool.wait_ge(s_slot, i * 2 + (o * (2 * GI + 1) + h + 1))
                            pool.sem_inc(s_pass2, 1)
                            for u in range(n):
                                pool.indirect_dma_start(
                                    out=deg_table[o][:, :], out_offset=bass.IndirectOffsetOnAxis(ap=idx_slot[:, h, u:u + 1], axis=0),
                                    in_=val_slot[:, h, u:u + 1], in_offset=None, bounds_check=N - 1,
                                    oob_is_err=False).then_inc(s_dsc[h], 16)

                    body(0, o == 0)
                    with pool.Fori(1, GI) as i:
                        body(i, False)
                    body(GI, False, 1, 1)
                pool.wait_ge(s_dsc[0], 2 * (GI * GT + 1) * 16)
                pool.wait_ge(s_dsc[1], 2 * GI * GT * 16)

            @block.tensor
            def _(pe):
                for o in range(2):
                    pe.wait_ge(s_dg, o + 1)
                    for k in range(2):
                        last = nc.tensor.matmul(ps[:, k, :], ones[:, :], diag[:, k, :], start=True, stop=True)
                    last.then_inc(s_row, 1)
                    pe.wait_ge(s_tails, o + 1)
                    nc.tensor.matmul(psc[:, 0:2], feeds[o][:, :], tmp[:, 0:2], start=True, stop=True).then_inc(s_st0, 1)

            @block.scalar
            def _(act):
                act.wait_ge(s_cnt1, 2)
                nc.scalar.activation(scale[1][:, :], cnt[:, :], ACT.Sqrt).then_inc(s_sq, 1)

            @block.vector
            def _(dve):
                chain = [0]

                def link(ins):
                    chain[0] += 1
                    ins.then_inc(s_v, 1)
                    dve.wait_ge(s_v, chain[0])

                V = nc.vector
                dve.wait_ge(s_in, 64)
                dve.wait_ge(s_m, 5)
                for o in range(2):
                    col0 = lambda a: a[:, 0:1]
                    link(V.tensor_copy(keyf[:, :], rec[o][:, :, 0]))
                    link(V.tensor_copy(keyp[:, :], recp[o][:, :, 0]))
                    link(V.tensor_copy(keyn[:, :], recn[o][:, :, 0]))
                    link(V.tensor_tensor(whole[o][:, :], keyf[:, :], keyp[:, :], ALU.is_equal))
                    link(V.tensor_copy(go_on[o][:, :], whole[o][:, :]))
                    link(V.memset(go_on[o][:, 0:1], 0.0))
                    link(V.tensor_tensor(last_e[:, :], keyf[:, :], keyn[:, :], ALU.not_equal))
                    if o == 1:
                        link(V.tensor_tensor(on_next[:, :], keyf[:, :], keyn[:, :], ALU.is_equal))
                    link(V.tensor_scalar(lead[:, :], keyf[:, :], keyf[:, 0:1], whole[o][:, 0:1], ALU.is_equal, ALU.mult))
                    link(V.tensor_tensor(leadend[o][:, :], last_e[:, :], lead[:, :], ALU.mult))
                    link(V.tensor_tensor(fin[:, 0:EC], last_e[:, :], leadend[o][:, :], ALU.subtract))
                    link(V.tensor_reduce(fin[:, EC:EC + 1], leadend[o][:, :], AX_X, ALU.add))
                    link(V.tensor_scalar(idxf[:, :], fin[:, :], -float(SKIP), float(SKIP), ALU.mult, ALU.add))
                    link(V.tensor_tensor(idxf[:, 0:EC], idxf[:, 0:EC], keyf[:, :], ALU.add))
                    link(V.tensor_tensor(idxf[:, EC:EC + 1], idxf[:, EC:EC + 1], keyf[:, 0:1], ALU.add))
                    link(V.tensor_copy(pack[o][:, :, 2], idxf[:, :]))
                    if o == 1:
                        link(V.tensor_scalar(valid[:, :], idxf[:, :], float(N), None, ALU.is_lt))
                    link(V.tensor_scalar(pack[o][:, 0:EC, 1], keyf[:, :], float(N - 1), None, ALU.min))
                    link(V.tensor_scalar(pack[o][:, EC:EC + 1, 1], keyf[:, 0:1], float(N - 1), None, ALU.min))
                    link(V.tensor_copy(keyp[:, :], rec[o][:, :, 1]))
                    link(V.tensor_scalar(pack[o][:, 0:EC, 0], keyp[:, :], float(N - 1), None, ALU.min))
                    link(V.memset(pack[o][:, EC:EC + 1, 0], 0))
                    link(V.tensor_scalar(diag[:, 0, :], ident[:, :], keyf[:, 0:1], None, ALU.mult))
                    V.tensor_scalar(diag[:, 1, :], ident[:, :], keyf[:, EC - 1:EC], None, ALU.mult).then_inc(s_dg, 1)
                    dve.wait_ge(s_row, o + 1)
                    link(V.scalar_tensor_tensor(out=feeds[o][:, :], in0=ps[:, 0, :], scalar=keyf[:, EC - 1:EC],
                                                in1=before[:, :], op0=ALU.is_equal, op1=ALU.mult))
                    if o == 1:
                        for pen, k, key, where in ((pen_f, 1, keyf[:, 0:1], before_t), (pen_b, 0, keyf[:, EC - 1:EC], after)):
                            link(V.scalar_tensor_tensor(out=pen[:, :], in0=ps[:, k, :], scalar=key, in1=where[:, :],
                                                        op0=ALU.is_equal, op1=ALU.mult))
                            link(V.tensor_scalar(pen[:, :], pen[:, :], 1.0, 1e30, ALU.subtract, ALU.mult))
                    else:
                        link(V.tensor_copy(weight[:, :], rec[0][:, :, 2].bitcast(F32)))
                    link(V.tensor_tensor_scan(cnt[:, 0:EC], go_on[o][:, :], ones_e[:, :], 0.0, ALU.mult, ALU.add))
                    link(V.tensor_copy(tmp[:, 0:1], cnt[:, EC - 1:EC]))
                    if o == 0:
                        link(V.tensor_tensor_scan(wsum[:, 0:EC], go_on[0][:, :], weight[:, :], 0.0, ALU.mult, ALU.add))
                        V.tensor_copy(tmp[:, 1:2], wsum[:, EC - 1:EC]).then_inc(s_tails, 1)
                    else:
                        V.tensor_copy(tmp[:, 1:2], cnt[:, EC - 1:EC]).then_inc(s_tails, 1)
                    dve.wait_ge(s_st0, o + 1)
                    link(V.tensor_copy(start[:, :], psc[:, 0:2]))
                    link(V.tensor_tensor_scan(cnt[:, 0:EC], whole[o][:, :], ones_e[:, :], start[:, 0:1], ALU.mult, ALU.add))
                    link(V.tensor_tensor(tmp[:, 0:EC], cnt[:, 0:EC], leadend[o][:, :], ALU.mult))
                    link(V.tensor_reduce(cnt[:, EC:EC + 1], tmp[:, 0:EC], AX_X, ALU.add))
                    if o == 0:
                        link(V.tensor_tensor_scan(wsum[:, 0:EC], whole[0][:, :], weight[:, :], start[:, 1:2], ALU.mult, ALU.add))
                        link(V.tensor_tensor(tmp[:, 0:EC], wsum[:, 0:EC], leadend[0][:, :], ALU.mult))
                        link(V.tensor_reduce(wsum[:, EC:EC + 1], tmp[:, 0:EC], AX_X, ALU.add))
                    link(V.tensor_scalar(cnt[:, :], cnt[:, :], 1.0, None, ALU.add))
                    if o == 0:
                        V.reciprocal(scale[0][:, :], cnt[:, :]).then_inc(s_deg, 1)
                        dve.wait_ge(s_deg, 1)
                        V.tensor_copy(start[:, 0:1], cnt[:, 0:1]).then_inc(s_cnt1, 1)
                    else:
                        link(V.reciprocal(inv_deg_dst[:, :], cnt[:, :]))
                        V.tensor_copy(start[:, 0:1], cnt[:, 0:1]).then_inc(s_cnt1, 1)
                        dve.wait_ge(s_sq, 1)
                        V.reciprocal(scale[1][:, :], scale[1][:, :]).then_inc(s_deg, 1)
                dve.wait_ge(s_w3, 48)
                for k, to in ((0, Was), (1, Wad)):
                    for b in range(KB):
                        link(V.tensor_tensor(prod[:, :, :], W3[:, b, :].rearrange("p (h d) -> p h d", d=HD),
                                             att[:, k, :, :], ALU.mult))
                        link(V.tensor_reduce(to[:, b, :], prod[:, :, :], AX_X, ALU.add))

        x1e = dram("x1e", [P, TOTAL * D])
        x2e = dram("x2e", [P, TOTAL * D])
        x3e = dram("x3e", [P, TOTAL * D])
        agg2 = dram("agg2", [P, TOTAL * D])
        h3 = dram("h3", [P, TOTAL * D])

        msg = sb("msg", [P, 2, GT, D])
        own = sb("own", [P, 2, GT, D])
        pk = sb("pk", [P, 2, GT, 3], I32)
        lr = sb("lr", [P, D])
        tot = sb("tot", [P, 2, GT, D])
        tT = sb("tT", [P, 2, 2, KB, QT, P])
        o4 = sb("o4", [P, 2, QT, D])
        est = sb("est", [P, 2, 4, QT, 6])
        emv = sb("emv", [P, 2, 4, QT, 2])
        esm = sb("esm", [P, 2, 4, 3, QT])
        wslot = sb("wslot", [P, 2, GT])
        V, A, T = nc.vector, nc.scalar, nc.tensor

        def gather(pool, table, to, h, u, f, s):
            pool.indirect_dma_start(out=to, out_offset=None, in_=table[:, :],
                                    in_offset=bass.IndirectOffsetOnAxis(ap=pk[:, h, u, f:f + 1], axis=0),
                                    bounds_check=N - 1, oob_is_err=False).then_inc(s, 16)

        def scatter_rows(pool, table, h, n, s):
            for u in range(n):
                pool.indirect_dma_start(out=table[:, :], out_offset=bass.IndirectOffsetOnAxis(ap=pk[:, h, u, 2:3], axis=0),
                                        in_=own[:, h, u, :], in_offset=None, bounds_check=N - 1,
                                        oob_is_err=False).then_inc(s, 16)

        def indices(pool, o, g, s_pk, s_go):
            i, c, _ = g
            t = c * GT if i is None else i * (2 * GT) + c * GT
            n = group_tiles(g)
            pool.tensor_copy(pk[:, slot(g), 0:n, :], pack[o][:, bass.ds(t, n), :]).then_inc(s_pk, 1)
            pool.wait_ge(s_pk, ev(g, 1, 1))
            pool.sem_inc(s_go, 1)

        def transposed(q, k, of, to, s):
            for j in range(ntiles(q)):
                for b in range(KB):
                    last = T.transpose(to[:, b, j, :], of[:, half(q), q[1] % 2 * 4 + j, b * P:(b + 1) * P], ident[:, :])
            last.then_inc(s, 1)

        def product(q, k, weights, to, s):
            for j in range(ntiles(q)):
                for b in range(KB):
                    last = T.matmul(to[:, j, :], tT[:, q[1] % 2, k, b, j, :], weights[:, b, :],
                                    start=(b == 0), stop=(b == KB - 1))
            last.then_inc(s, 1)

        def accumulate(q, o, s_ready, ready, s_acc, s_lr, s_fix):
            n, h, j0, t0 = ntiles(q), half(q), q[1] % 2 * 4, tile0(q)
            if q[0] is None and q[1] >= FIX:
                V.wait_ge(s_fix, 1)
                V.wait_ge(s_lr, EC)
                V.tensor_tensor(msg[:, 0, 0, :], psF, lr[:, :], ALU.add).then_inc(s_acc, 1)
                return
            V.wait_ge(s_ready, ready)
            for j in range(n):
                if q[0] is None and t0 + j == 0:
                    continue
                before_it = msg[:, h, j0 + j - 1, :] if j0 + j else msg[:, 1 - h, GT - 1, :]
                wait(V, s_acc, t0 + (j - 1))
                V.scalar_tensor_tensor(out=msg[:, h, j0 + j, :], in0=before_it, scalar=go_on[o][:, bass.ds(t0 + j, 1)],
                                       in1=msg[:, h, j0 + j, :], op0=ALU.mult, op1=ALU.add).then_inc(s_acc, 1)
            V.wait_ge(s_acc, t0 + (n - 1))
            for j in range(n):
                V.wait_ge(s_lr, t0 + (j + 1))
                V.scalar_tensor_tensor(out=lr[:, :], in0=msg[:, h, j0 + j, :], scalar=leadend[o][:, bass.ds(t0 + j, 1)],
                                       in1=lr[:, :], op0=ALU.mult, op1=ALU.add).then_inc(s_lr, 1)

        def statistics(l, q, of, s_sum, s_bn, s_go, s_mv):
            n, k = ntiles(q), slot(q)
            V.wait_ge(s_sum, ev(q, 1, 1))
            for j in range(n):
                last = V.bn_stats(est[:, l, k, j, :], of(q, j))
            last.then_inc(s_bn, 1)
            V.wait_ge(s_bn, ev(q, 1, 1))
            V.sem_inc(s_go, 1)
            for j in range(n):
                last = V.bn_aggr(emv[:, l, k, j, :], est[:, l, k, j, :])
            last.then_inc(s_mv, 1)

        def deviation(l, q, s_mv, s_sd):
            n, k = ntiles(q), slot(q)
            A.wait_ge(s_mv, ev(q, 1, 1))
            A.activation(esm[:, l, k, 0, 0:n], emv[:, l, k, 0:n, 1], ACT.Sqrt, bias=eps[:, :]).then_inc(s_sd, 1)

        def reciprocals(l, q, s_sd, s_rs, s_nm):
            n, k = ntiles(q), slot(q)
            V.wait_ge(s_sd, ev(q, 1, 1))
            V.reciprocal(esm[:, l, k, 1, 0:n], esm[:, l, k, 0, 0:n]).then_inc(s_rs, 1)
            V.wait_ge(s_rs, ev(q, 1, 1))
            V.scalar_tensor_tensor(out=esm[:, l, k, 2, 0:n], in0=emv[:, l, k, 0:n, 0], scalar=-1.0,
                                   in1=esm[:, l, k, 1, 0:n], op0=ALU.mult, op1=ALU.mult).then_inc(s_nm, 1)

        def normalise(l, q, of, s_nm, s_norm):
            k = slot(q)
            A.wait_ge(s_nm, ev(q, 1, 1))
            for j in range(ntiles(q)):
                last = A.activation(of(q, j), of(q, j), ACT.Identity, bias=esm[:, l, k, 2, j:j + 1],
                                    scale=esm[:, l, k, 1, j:j + 1])
            last.then_inc(s_norm, 1)

        def own_row(q, j):
            return own[:, half(q), q[1] % 2 * 4 + j, :]

        def o4_row(q, j):
            return o4[:, q[1] % 2, j, :]

        def chunk_of(a, q):
            j0 = q[1] % 2 * 4
            return a[:, half(q), j0:j0 + ntiles(q), :]

        def tiles_of(table, q, n=None):
            t = tile0(q)
            n = n or ntiles(q)
            return table[:, bass.ds(t * D, n * D)]

        def store(sp, table, of, q, s_from, s_go, s_to):
            sp.wait_ge(s_from, ev(q, 1, 1))
            sp.sem_inc(s_go, 1)
            sp.dma_start(tiles_of(table, q), chunk_of(of, q).rearrange("p n d -> p (n d)")).then_inc(s_to, 16)

        def stored(q):
            return 32 * (q[1] // 4) if q[0] is None else q[0] * 32 + q[1] // 4 * 32

        def over(v, n):
            return v.unsqueeze(1).broadcast_to([P, n, D])

        with phase() as scope:
            psT = pb("psT", [P, KB, QT, P], F32, scope)
            psY = pb("psY", [P, QT, D], F32, scope)
            psF = psT[:, 0, 0:2, :].rearrange("p a b -> p (a b)")
            (s_pk, s_go, s_vgo, s_spgo, s_scaled, s_acc, s_lr, s_fix, s_tot, s_t, s_tc, s_y, s_add, s_bn, s_mv, s_sd, s_rs,
             s_nm, s_norm) = (sem(f"e0_{n}") for n in (
                "pk", "go", "vgo", "spgo", "scaled", "acc", "lr", "fix", "tot", "t", "tc", "y", "add", "bn", "mv", "sd",
                "rs", "nm", "norm"))
            s_g = [sem(f"e0_g{k}") for k in range(2)]
            s_sc = [sem(f"e0_sc{k}") for k in range(2)]
            s_lin = [sem(f"e0_lin{k}") for k in range(2)]
            block = scope.enter_context(nc.Block())

            @block.gpsimd
            def _(pool):
                def step(g):
                    n, h = group_tiles(g), slot(g)
                    if inside(g, 0, 2 * GI):
                        wait(pool, s_sc[h], nth(g, 16 * GT))
                        wait(pool, s_lin[h], nth(g, 32))
                        wait(pool, s_acc, ev(g, GT, 1 - GT))
                        indices(pool, 0, g, s_pk, s_go)
                        for u in range(n):
                            if n == GT:
                                gather(pool, x, msg[:, h, u, :], h, u, 0, s_g[h])
                                gather(pool, inv_deg_src, wslot[:, h, u:u + 1], h, u, 0, s_g[h])
                            gather(pool, x, own[:, h, u, :], h, u, 1, s_g[h])
                    b = sh(g, -1)
                    if inside(b, 0, 2 * GI):
                        pool.wait_ge(s_norm, FIX + 1 if group_tiles(b) == 1 else ev(b, 2, 2))
                        pool.sem_inc(s_go, 1)
                        scatter_rows(pool, x1, slot(b), group_tiles(b), s_sc[slot(b)])

                groups(pool, step, 2 * GI + 1)
                pool.wait_ge(s_sc[0], 16 * (GI * GT + 1))
                pool.wait_ge(s_sc[1], 16 * GI * GT)

            def arrived(q):
                return 16 * 3 * GI * GT + 16 if q[0] is None and q[1] >= FIX else landed(q, 3)

            @block.scalar
            def _(act):
                def step(q):
                    if inside(q, 0, FIX - 1):
                        act.wait_ge(s_g[half(q)], arrived(q))
                        for j in range(ntiles(q)):
                            jj = q[1] % 2 * 4 + j
                            last = A.activation(msg[:, half(q), jj, :], msg[:, half(q), jj, :], ACT.Copy,
                                                scale=wslot[:, half(q), jj:jj + 1])
                        last.then_inc(s_scaled, 1)
                    if inside(q, 0, FIX):
                        n = ntiles(q)
                        act.wait_ge(s_t, ev(q, 1, 1))
                        wait(act, s_y, ev(q, 1, -1))
                        A.activation(tT[:, q[1] % 2, 0, :, 0:n, :], psT[:, :, 0:n, :], ACT.Copy).then_inc(s_tc, 1)
                    b = sh(q, -1)
                    if inside(b, 0, FIX):
                        deviation(0, b, s_mv, s_sd)
                        normalise(0, b, own_row, s_nm, s_norm)

                chunks(act, step, FIX + 1)

            @block.tensor
            def _(pe):
                def step(q):
                    if q[0] is None and q[1] == FIX:
                        pe.wait_ge(s_acc, EC - 1)
                        pe.wait_ge(s_tc, FIX)
                        T.matmul(psF, feeds[0][:, :], msg[:, 1, GT - 1, :], start=True, stop=True).then_inc(s_fix, 1)
                    pe.wait_ge(s_tot, ev(q, 1, 1))
                    wait(pe, s_tc, ev(q))
                    transposed(q, 0, tot, psT, s_t)
                    pe.wait_ge(s_tc, ev(q, 1, 1))
                    wait(pe, s_add, ev(q))
                    product(q, 0, W0, psY, s_y)

                chunks(pe, step, FIX)

            @block.vector
            def _(dve):
                def step(q):
                    if inside(q, 0, FIX):
                        n, h, j0, t0 = ntiles(q), half(q), q[1] % 2 * 4, tile0(q)
                        accumulate(q, 0, s_scaled, ev(q, 1, 1), s_acc, s_lr, s_fix)
                        if n == 1:
                            dve.wait_ge(s_g[0], arrived(q))
                        wait(dve, s_acc, t0 + (n - 1))
                        wait(dve, s_t, ev(q, 1, -3))
                        for j in range(n):
                            last = V.scalar_tensor_tensor(out=tot[:, h, j0 + j, :], in0=own[:, h, j0 + j, :],
                                                          scalar=scale[0][:, bass.ds(t0 + j, 1)], in1=msg[:, h, j0 + j, :],
                                                          op0=ALU.mult, op1=ALU.add)
                        last.then_inc(s_tot, 1)
                    b = sh(q, -1)
                    if inside(b, 0, FIX):
                        n = ntiles(b)
                        dve.wait_ge(s_y, ev(b, 1, 1))
                        V.tensor_tensor(chunk_of(own, b), psY[:, 0:n, :], chunk_of(own, b), ALU.add).then_inc(s_add, 1)
                        statistics(0, b, own_row, s_add, s_bn, s_vgo, s_mv)
                        reciprocals(0, b, s_sd, s_rs, s_nm)

                V.memset(lr[:, :], 0.0).then_inc(s_lr, 1)
                chunks(dve, step, FIX + 1)

            @block.sync
            def _(sp):
                chunks(sp, lambda q: store(sp, x1e, own, q, s_norm, s_spgo, s_lin[half(q)]), FIX)
                sp.wait_ge(s_lin[0], 32 * GI + 16)
                sp.wait_ge(s_lin[1], 32 * GI)

        with phase() as scope:
            psT = [pb(f"psT{k}", [P, KB, QT, P], F32, scope) for k in "AB"]
            psY = [pb(f"psY{k}", [P, QT, D], F32, scope) for k in "AB"]
            psF = psT[0][:, 0, 0:2, :].rearrange("p a b -> p (a b)")
            (s_pk, s_go, s_vgo, s_spgo, s_scaled, s_acc, s_lr, s_fix, s_t, s_tc, s_y, s_oa, s_take, s_sum, s_plus) = (
                sem(f"e1_{n}") for n in ("pk", "go", "vgo", "spgo", "scaled", "acc", "lr", "fix", "t", "tc", "y", "oa",
                                         "take", "sum", "plus"))
            s_gb = [sem(f"e1_gb{k}") for k in range(3)]
            s_bn, s_mv, s_sd, s_rs, s_nm, s_norm = ([sem(f"e1_{n}{l}") for l in range(2)] for n in (
                "bn", "mv", "sd", "rs", "nm", "norm"))
            s_g = [sem(f"e1_g{k}") for k in range(2)]
            s_own = [sem(f"e1_own{k}") for k in range(2)]
            s_sc = [sem(f"e1_sc{k}") for k in range(2)]
            block = scope.enter_context(nc.Block())

            @block.sync
            def _(sp):
                def step(g):
                    n, h = group_tiles(g), slot(g)
                    i, c, _ = g
                    t = c * GT if i is None else i * (2 * GT) + c * GT
                    wait(sp, s_sc[h], nth(g, 16 * GT))
                    sp.sem_inc(s_spgo, 1)
                    sp.dma_start(own[:, h, 0:n, :].rearrange("p n d -> p (n d)"),
                                 x1e[:, bass.ds(t * D, n * D)]).then_inc(s_own[h], 16)

                groups(sp, step, 2 * GI)

            @block.gpsimd
            def _(pool):
                def step(g):
                    n, h = group_tiles(g), slot(g)
                    if inside(g, 0, 2 * GI):
                        wait(pool, s_sc[h], nth(g, 16 * GT))
                        wait(pool, s_acc, ev(g, GT, 1 - GT))
                        wait(pool, s_t, ev(g, 2, -2))
                        indices(pool, 0, g, s_pk, s_go)
                        if n == GT:
                            for u in range(n):
                                gather(pool, x1, msg[:, h, u, :], h, u, 0, s_g[h])
                    b = sh(g, -1)
                    if inside(b, 0, 2 * GI):
                        pool.wait_ge(s_norm[1], FIX + 1 if group_tiles(b) == 1 else ev(b, 2, 2))
                        pool.sem_inc(s_go, 1)
                        scatter_rows(pool, x2, slot(b), group_tiles(b), s_sc[slot(b)])

                groups(pool, step, 2 * GI + 1)
                pool.wait_ge(s_sc[0], 16 * (GI * GT + 1))
                pool.wait_ge(s_sc[1], 16 * GI * GT)

            @block.scalar
            def _(act):
                def step(q):
                    if inside(q, 0, FIX - 1):
                        act.wait_ge(s_g[half(q)], landed(q, 1))
                        t0 = tile0(q)
                        for j in range(ntiles(q)):
                            jj = q[1] % 2 * 4 + j
                            last = A.activation(msg[:, half(q), jj, :], msg[:, half(q), jj, :], ACT.Copy,
                                                scale=weight[:, bass.ds(t0 + j, 1)])
                        last.then_inc(s_scaled, 1)
                    if inside(q, 0, FIX):
                        n = ntiles(q)
                        act.wait_ge(s_t, ev(q, 1, 1))
                        wait(act, s_y, ev(q, 1, -1))
                        for k in range(2):
                            last = A.activation(tT[:, q[1] % 2, k, :, 0:n, :], psT[k][:, :, 0:n, :], ACT.Copy)
                        last.then_inc(s_tc, 1)
                    b, c = sh(q, -1), sh(q, -2)
                    if inside(b, 0, FIX):
                        deviation(0, b, s_mv[0], s_sd[0])
                        normalise(0, b, o4_row, s_nm[0], s_norm[0])
                    if inside(c, 0, FIX):
                        deviation(1, c, s_mv[1], s_sd[1])
                        normalise(1, c, own_row, s_nm[1], s_norm[1])

                chunks(act, step, FIX + 2)

            @block.tensor
            def _(pe):
                def step(q):
                    if q[0] is None and q[1] == FIX:
                        pe.wait_ge(s_acc, EC - 1)
                        pe.wait_ge(s_tc, FIX)
                        T.matmul(psF, feeds[0][:, :], msg[:, 1, GT - 1, :], start=True, stop=True).then_inc(s_fix, 1)
                    pe.wait_ge(s_acc, tile0(q) + (ntiles(q) - 1))
                    pe.wait_ge(s_own[half(q)], loads(q))
                    wait(pe, s_tc, ev(q))
                    transposed(q, 0, msg, psT[0], s_gb[0])
                    transposed(q, 1, own, psT[1], s_t)
                    pe.wait_ge(s_tc, ev(q, 1, 1))
                    wait(pe, s_take, ev(q))
                    product(q, 0, W1T, psY[0], s_gb[1])
                    product(q, 1, WrI, psY[1], s_y)

                chunks(pe, step, FIX)

            @block.vector
            def _(dve):
                def step(q):
                    if inside(q, 0, FIX):
                        accumulate(q, 0, s_scaled, ev(q, 1, 1), s_acc, s_lr, s_fix)
                    b, c = sh(q, -1), sh(q, -2)
                    if inside(b, 0, FIX):
                        n, t0 = ntiles(b), tile0(b)
                        dve.wait_ge(s_y, ev(b, 1, 1))
                        wait(dve, s_sum, ev(b, 1, -1))
                        for j in range(n):
                            last = V.scalar_tensor_tensor(out=o4[:, b[1] % 2, j, :], in0=B1, scalar=wsum[:, bass.ds(t0 + j, 1)],
                                                          in1=psY[0][:, j, :], op0=ALU.mult, op1=ALU.add)
                        last.then_inc(s_oa, 1)
                        V.tensor_tensor(chunk_of(own, b), psY[1][:, 0:n, :], over(BR, n), ALU.add).then_inc(s_take, 1)
                        statistics(0, b, o4_row, s_oa, s_bn[0], s_vgo, s_mv[0])
                    if inside(c, 0, FIX):
                        n = ntiles(c)
                        oc = o4[:, c[1] % 2, 0:n, :]
                        dve.wait_ge(s_norm[0], ev(c, 1, 1))
                        V.tensor_tensor(oc, oc, over(G1, n), ALU.mult).then_inc(s_plus, 1)
                        dve.wait_ge(s_plus, ev(c, 2, 1))
                        V.tensor_tensor(oc, oc, over(BE1, n), ALU.add).then_inc(s_plus, 1)
                        dve.wait_ge(s_plus, ev(c, 2, 2))
                        V.scalar_tensor_tensor(out=chunk_of(own, c), in0=oc, scalar=0.0, in1=chunk_of(own, c), op0=ALU.max,
                                               op1=ALU.add).then_inc(s_sum, 1)
                        statistics(1, c, own_row, s_sum, s_bn[1], s_vgo, s_mv[1])
                    if inside(b, 0, FIX):
                        reciprocals(0, b, s_sd[0], s_rs[0], s_nm[0])
                    if inside(c, 0, FIX):
                        reciprocals(1, c, s_sd[1], s_rs[1], s_nm[1])

                V.memset(lr[:, :], 0.0).then_inc(s_lr, 1)
                chunks(dve, step, FIX + 2)

        DG = D + 4
        gram_scope = ctx.enter_context(ExitStack())
        psG = pb("psG", [P, KB, 512], F32, gram_scope)

        with phase() as scope:
            xg = sb("xg", [P, RING, QT, DG], F32, scope)
            xm = sb("xm", [P, RING, QT, D], F32, scope)
            free = sb("free", [P, NPP + QT], F32, scope)
            s_fr, s_one2, s_mask, s_mul, s_gram, s_pgo = (sem(f"g_{n}") for n in ("fr", "one", "mask", "mul", "gram", "pgo"))
            s_x = [sem(f"g_x{k}") for k in range(RING)]
            block = scope.enter_context(nc.Block())

            @block.sync
            def _(sp):
                sp.dma_start(free[:, 0:NPP], dinv_dst[0:P * NPP, 0].rearrange("(p c) -> p c", p=P)).then_inc(s_fr, 16)
                sp.dma_start(free[0:TAIL, NPP:NPP + QT], dinv_dst[P * NPP:N, 0].rearrange("(p c) -> p c", p=TAIL)).then_inc(s_fr, 16)

                def step(q):
                    wait(sp, s_gram, ev(q, 1, 1 - RING))
                    sp.sem_inc(s_pgo, 1)
                    sp.dma_start(xg[0:rows(q), slot(q), :, 0:D],
                                 quad_of(x2, q).rearrange("p (j d) -> p j d", d=D)).then_inc(s_x[slot(q)], 16)

                steps(sp, step, 0, NQ)

            @block.vector
            def _(dve):
                V.memset(xg[:, :, :, D:DG], 1.0).then_inc(s_one2, 1)
                dve.wait_ge(s_fr, 32)
                V.tensor_scalar(free[:, 0:NPP], free[:, 0:NPP], 1.0, None, ALU.is_equal).then_inc(s_mask, 1)
                V.tensor_scalar(free[0:TAIL, NPP:NPP + QT], free[0:TAIL, NPP:NPP + QT], 1.0, None, ALU.is_equal).then_inc(s_mask, 1)
                dve.wait_ge(s_mask, 2)

                def step(q):
                    r, s = rows(q), slot(q)
                    dve.wait_ge(s_x[s], nth(q, 16, 16))
                    wait(dve, s_gram, ev(q, 1, 1 - RING))
                    V.tensor_tensor(xm[0:r, s, :, :], xg[0:r, s, :, 0:D],
                                    free[0:r, bass.ds(ev(q, QT), QT)].unsqueeze(2).broadcast_to([r, QT, D]),
                                    ALU.mult).then_inc(s_mul, 1)

                steps(dve, step, 0, NQ)

            @block.tensor
            def _(pe):
                pe.wait_ge(s_one2, 1)

                def step(q):
                    r, s = rows(q), slot(q)
                    pe.wait_ge(s_mul, ev(q, 1, 1))
                    for j in range(QT):
                        for b in range(KB):
                            last = T.matmul(psG[:, b, 0:D + 1], xm[0:r, s, j, b * P:(b + 1) * P], xg[0:r, s, j, 0:D + 1],
                                            start=q[0] is None and q[1] == 0 and j == 0, stop=False)
                    last.then_inc(s_gram, 1)

                steps(pe, step, 0, NQ)

        with phase() as scope:
            tw = sb("tw", [P, 2, GT, D], F32, scope)
            tot1 = sb("tot1", [P, 2, GT, DG], F32, scope)
            psF = pb("psF2", [P, D], F32, scope)[:, :]
            s_pk, s_go, s_spgo, s_scaled, s_acc, s_lr, s_fix, s_one2, s_part, s_tot, s_val, s_gram, s_own, s_agg = (
                sem(f"e2_{n}") for n in ("pk", "go", "spgo", "scaled", "acc", "lr", "fix", "one", "part", "tot", "val", "gram",
                                         "own", "agg"))
            s_g = [sem(f"e2_g{k}") for k in range(2)]
            s_lin = [sem(f"e2_lin{k}") for k in range(2)]
            block = scope.enter_context(nc.Block())

            def stored_pair(q):
                return 64 * (q[1] // 4) if q[0] is None else q[0] * 64 + q[1] // 4 * 64

            def arrived2(q):
                return 16 * 3 * GI * GT + 16 if q[0] is None and q[1] >= FIX else landed(q, 3)

            @block.gpsimd
            def _(pool):
                def step(g):
                    n, h = group_tiles(g), slot(g)
                    wait(pool, s_lin[h], nth(g, 64))
                    wait(pool, s_acc, ev(g, GT, 1 - GT))
                    wait(pool, s_tot, ev(g, 2, -2))
                    indices(pool, 1, g, s_pk, s_go)
                    for u in range(n):
                        if n == GT:
                            gather(pool, x2, msg[:, h, u, :], h, u, 0, s_g[h])
                            gather(pool, dinv_dst, wslot[:, h, u:u + 1], h, u, 0, s_g[h])
                        gather(pool, x2, own[:, h, u, :], h, u, 1, s_g[h])

                groups(pool, step, 2 * GI)

            @block.scalar
            def _(act):
                def step(q):
                    n, h, j0, t0 = ntiles(q), half(q), q[1] % 2 * 4, tile0(q)
                    if inside(q, 0, FIX):
                        act.wait_ge(s_g[h], arrived2(q))
                        if not (q[0] is None and q[1] == FIX):
                            for j in range(n):
                                last = A.activation(msg[:, h, j0 + j, :], msg[:, h, j0 + j, :], ACT.Copy,
                                                    scale=wslot[:, h, j0 + j:j0 + j + 1])
                            last.then_inc(s_scaled, 1)
                        wait(act, s_val, ev(q, 1, -3))
                        wait(act, s_gram, ev(q, 1, -3))
                        for j in range(n):
                            last = A.activation(tw[:, h, j0 + j, :], own[:, h, j0 + j, :], ACT.Copy,
                                                scale=inv_deg_dst[:, bass.ds(t0 + j, 1)])
                        last.then_inc(s_part, 1)
                    b = sh(q, -1)
                    if inside(b, 0, FIX):
                        n, h, j0, t0 = ntiles(b), half(b), b[1] % 2 * 4, tile0(b)
                        act.wait_ge(s_tot, ev(b, 1, 1))
                        for j in range(n):
                            last = A.activation(tw[:, h, j0 + j, :], tot1[:, h, j0 + j, 0:D], ACT.Copy,
                                                scale=valid[:, bass.ds(t0 + j, 1)])
                        last.then_inc(s_val, 1)

                chunks(act, step, FIX + 1)

            @block.vector
            def _(dve):
                def step(q):
                    n, h, j0, t0 = ntiles(q), half(q), q[1] % 2 * 4, tile0(q)
                    accumulate(q, 1, s_scaled, ev(q, 1, 1), s_acc, s_lr, s_fix)
                    wait(dve, s_acc, t0 + (n - 1))
                    dve.wait_ge(s_part, ev(q, 1, 1))
                    wait(dve, s_gram, ev(q, 1, -3))
                    wait(dve, s_lin[h], stored_pair(q))
                    for j in range(n):
                        last = V.scalar_tensor_tensor(out=tot1[:, h, j0 + j, 0:D], in0=msg[:, h, j0 + j, :],
                                                      scalar=scale[1][:, bass.ds(t0 + j, 1)], in1=tw[:, h, j0 + j, :],
                                                      op0=ALU.mult, op1=ALU.add)
                    last.then_inc(s_tot, 1)

                V.memset(tot1[:, :, :, D:DG], 1.0).then_inc(s_one2, 1)
                V.memset(lr[:, :], 0.0).then_inc(s_lr, 1)
                chunks(dve, step, FIX)

            @block.tensor
            def _(pe):
                pe.wait_ge(s_one2, 1)

                def step(q):
                    n, h, j0 = ntiles(q), half(q), q[1] % 2 * 4
                    fix = q[0] is None and q[1] == FIX
                    if fix:
                        pe.wait_ge(s_acc, EC - 1)
                        T.matmul(psF, feeds[1][:, :], msg[:, 1, GT - 1, :], start=True, stop=True).then_inc(s_fix, 1)
                    pe.wait_ge(s_val, ev(q, 1, 1))
                    for j in range(n):
                        for b in range(KB):
                            last = T.matmul(psG[:, b, 0:D + 1], tw[:, h, j0 + j, b * P:(b + 1) * P],
                                            tot1[:, h, j0 + j, 0:D + 1], start=False, stop=fix)
                    last.then_inc(s_gram, 1)

                chunks(pe, step, FIX)

            @block.sync
            def _(sp):
                def step(q):
                    n, h, j0 = ntiles(q), half(q), q[1] % 2 * 4
                    sp.wait_ge(s_tot, ev(q, 1, 1))
                    sp.sem_inc(s_spgo, 1)
                    sp.dma_start(tiles_of(agg2, q).rearrange("p (n d) -> p n d", d=D), tot1[:, h, j0:j0 + n, 0:D]).then_inc(s_lin[h], 16)
                    sp.dma_start(tiles_of(x2e, q), chunk_of(own, q).rearrange("p n d -> p (n d)")).then_inc(s_lin[h], 16)

                chunks(sp, step, FIX)
                sp.wait_ge(s_lin[0], 64 * GI + 32)
                sp.wait_ge(s_lin[1], 64 * GI)

        W2s = sb("W2s", [P, KB, D])
        shift = sb("shift", [P, D])
        with phase() as scope:
            gram = sb("gram", [P, KB, D + 1], F32, scope)
            wv = sb("wv", [P, KB, D], F32, scope)
            ws = sb("ws", [P, KB, D], F32, scope)
            mean = sb("mean", [P, D], F32, scope)
            var = sb("var", [P, D], F32, scope)
            tmp2 = sb("tmp2", [P, D], F32, scope)
            psV = pb("psV", [P, KB, D], F32, scope)
            psM = pb("psM", [P, 2, D], F32, scope)
            s_c, s_gr, s_v1, s_wv, s_mo, s_sd2, s_vr = (sem(f"s2_{n}") for n in ("c", "gr", "v", "wv", "mo", "sd", "vr"))
            block = scope.enter_context(nc.Block())

            @block.tensor
            def _(pe):
                pe.wait_ge(s_gr, 1)
                for b in range(KB):
                    for a in range(KB):
                        last = T.matmul(psV[:, b, :], gram[:, a, b * P:(b + 1) * P], W2[:, a, :], start=(a == 0), stop=(a == KB - 1))
                last.then_inc(s_v1, 1)
                pe.wait_ge(s_wv, 1)
                for k, of in enumerate((wv, ws)):
                    for b in range(KB):
                        last = T.matmul(psM[:, k, :], ones[:, :], of[:, b, :], start=(b == 0), stop=(b == KB - 1))
                last.then_inc(s_mo, 1)

            @block.scalar
            def _(act):
                act.wait_ge(s_vr, 1)
                A.activation(var[:, :], var[:, :], ACT.Sqrt, bias=eps[:, :]).then_inc(s_sd2, 1)

            @block.vector
            def _(dve):
                chain = [0]

                def link(ins):
                    chain[0] += 1
                    ins.then_inc(s_c, 1)
                    dve.wait_ge(s_c, chain[0])

                V.tensor_copy(gram[:, :, :], psG[:, :, 0:D + 1]).then_inc(s_gr, 1)
                dve.wait_ge(s_gr, 1)
                for b in range(KB):
                    link(V.tensor_scalar(ws[:, b, :], W2[:, b, :], gram[:, b, D:D + 1], None, ALU.mult))
                dve.wait_ge(s_v1, 1)
                V.tensor_tensor(wv[:, :, :], psV[:, :, :], W2[:, :, :], ALU.mult).then_inc(s_wv, 1)
                dve.wait_ge(s_mo, 1)
                link(V.tensor_scalar(mean[:, :], psM[:, 1, :], 1.0 / N, None, ALU.mult))
                link(V.tensor_tensor(tmp2[:, :], mean[:, :], mean[:, :], ALU.mult))
                V.scalar_tensor_tensor(out=var[:, :], in0=psM[:, 0, :], scalar=1.0 / N, in1=tmp2[:, :],
                                       op0=ALU.mult, op1=ALU.subtract).then_inc(s_vr, 1)
                link(V.tensor_tensor(mean[:, :], mean[:, :], B2, ALU.add))
                dve.wait_ge(s_sd2, 1)
                link(V.reciprocal(var[:, :], var[:, :]))
                link(V.tensor_tensor(var[:, :], var[:, :], G2, ALU.mult))
                link(V.tensor_tensor(tmp2[:, :], B2, mean[:, :], ALU.subtract))
                link(V.tensor_tensor(tmp2[:, :], tmp2[:, :], var[:, :], ALU.mult))
                link(V.tensor_tensor(shift[:, :], tmp2[:, :], BE2, ALU.add))
                link(V.tensor_tensor(W2s[:, :, :], W2[:, :, :], over(var[:, :], KB), ALU.mult))
        gram_scope.close()

        half_neg = sb("half_neg", [P, QT])
        R3 = 5
        with phase() as scope:
            xin = sb("p3_xin", [P, R3, QT, D], F32, scope)
            xT = sb("p3_xT", [P, 2, KB, QT, P], F32, scope)
            yo = sb("p3_yo", [P, R3, QT, D], F32, scope)
            y3 = sb("p3_y3", [P, R3, QT, D], F32, scope)
            small = sb("p3_small", [P, 2, R3, 3, QT], F32, scope)
            st = sb("p3_st", [P, 2, R3, QT, 6], F32, scope)
            mv = sb("p3_mv", [P, 2, R3, QT, 2], F32, scope)
            psT = [pb(f"p3_psT{k}", [P, KB, QT, P], F32, scope) for k in range(2)]
            psY = [pb(f"p3_psY{k}", [P, QT, D], F32, scope) for k in range(2)]
            s_t, s_tc, s_y, s_o, s_th, s_half, s_dp, s_spg = (sem(f"p3_{n}") for n in ("t", "tc", "y", "o", "th", "half", "dp", "sp"))
            s_add, s_bn, s_mv, s_ve, s_rs, s_nm, s_norm = ([sem(f"p3_{n}{l}") for l in range(2)] for n in (
                "add", "bn", "mv", "ve", "rs", "nm", "norm"))
            s_x = [sem(f"p3_x{k}") for k in range(R3)]
            s_st3 = [sem(f"p3_st3{k}") for k in range(R3)]
            s_st4 = [sem(f"p3_st4{k}") for k in range(R3)]
            block = scope.enter_context(nc.Block())
            LAST3 = NQ + 2
            buf3 = (xin, y3)

            @block.sync
            def _(sp):
                def load(q):
                    wait(sp, s_st3[slot(q)], nth(q, 16))
                    wait(sp, s_add[1], ev(q, 1, 1 - R3))
                    sp.sem_inc(s_spg, 1)
                    sp.dma_start(xin[0:rows(q), slot(q), :, :].rearrange("p j d -> p (j d)"),
                                 quad_of(x2, q)).then_inc(s_x[slot(q)], 16)

                def store_quad(l, table, q, s_st):
                    sp.wait_ge(s_norm[l], ev(q, 1, 1))
                    sp.sem_inc(s_spg, 1)
                    sp.dma_start(quad_of(table, q),
                                 buf3[l][0:rows(q), slot(q), :, :].rearrange("p j d -> p (j d)")).then_inc(s_st[slot(q)], 16)

                def step(q):
                    if inside(sh(q, 2), 0, NQ):
                        load(sh(q, 2))
                    if inside(sh(q, -2), 0, NQ):
                        store_quad(0, x3, sh(q, -2), s_st3)
                    if inside(sh(q, -3), 0, NQ):
                        store_quad(1, out, sh(q, -3), s_st4)

                load((None, 0, R3))
                load((None, 1, R3))
                steps(sp, step, 0, LAST3 + 1, ring=R3)
                for c in range(R3):
                    sp.wait_ge(s_st3[c], 16 * len(range(c, NQ + 1, R3)))
                    sp.wait_ge(s_st4[c], 16 * len(range(c, NQ + 1, R3)))

            @block.tensor
            def _(pe):
                def step(c):
                    q, k = sh(c, 1), 0
                    if inside(q, 0, NQ):
                        r, s = rows(q), slot(q)
                        pe.wait_ge(s_x[s], nth(q, 16, 16))
                        wait(pe, s_tc, ev(q))
                        for j in range(QT):
                            for b in range(KB):
                                last = T.transpose(psT[0][:, b, j, 0:r], xin[0:r, s, j, b * P:(b + 1) * P], ident[0:r, 0:r])
                        last.then_inc(s_t, 1)
                    q = c
                    if inside(q, 0, NQ):
                        r = rows(q)
                        pe.wait_ge(s_tc, ev(q, 1, 1))
                        wait(pe, s_o, ev(q))
                        for j in range(QT):
                            for b in range(KB):
                                last = T.matmul(psY[0][0:r, j, :], xT[:, 0, b, j, 0:r], W2s[:, b, :],
                                                start=(b == 0), stop=(b == KB - 1))
                        last.then_inc(s_y, 1)

                step((None, -1, R3))
                steps(pe, step, 0, NQ, ring=R3)

            @block.scalar
            def _(act):
                def norm(l, q):
                    r, s = rows(q), slot(q)
                    act.wait_ge(s_nm[l], ev(q, 1, 1))
                    for j in range(QT):
                        last = A.activation(buf3[l][0:r, s, j, :], buf3[l][0:r, s, j, :], ACT.Identity,
                                            bias=small[0:r, l, s, 2, j:j + 1], scale=small[0:r, l, s, 1, j:j + 1])
                    last.then_inc(s_norm[l], 1)

                def step(q):
                    nxt = sh(q, 1)
                    if inside(nxt, 0, NQ):
                        r = rows(nxt)
                        act.wait_ge(s_t, ev(nxt, 1, 1))
                        wait(act, s_y, ev(nxt))
                        A.activation(xT[:, 0, :, :, 0:r], psT[0][:, :, :, 0:r], ACT.Copy).then_inc(s_tc, 1)
                    if inside(q, 0, NQ):
                        r, s = rows(q), slot(q)
                        act.wait_ge(s_o, ev(q, 1, 1))
                        A.activation(yo[0:r, s, :, :], yo[0:r, s, :, :], ACT.Tanh).then_inc(s_th, 1)
                    if inside(sh(q, -1), 0, NQ):
                        norm(0, sh(q, -1))
                    if inside(sh(q, -2), 0, NQ):
                        norm(1, sh(q, -2))

                step((None, -1, R3))
                steps(act, step, 0, LAST3, ring=R3)

            @block.gpsimd
            def _(pool):
                def rsqrt(l, q):
                    r, s = rows(q), slot(q)
                    pool.wait_ge(s_ve[l], ev(q, 1, 1))
                    pool.sem_inc(s_dp, 1)
                    pool.tensor_tensor(small[0:r, l, s, 1, :], small[0:r, l, s, 0, :], half_neg[0:r, :],
                                       ALU.pow).then_inc(s_rs[l], 1)

                def step(q):
                    if inside(sh(q, -1), 0, NQ):
                        rsqrt(0, sh(q, -1))
                    if inside(sh(q, -2), 0, NQ):
                        rsqrt(1, sh(q, -2))

                pool.memset(half_neg[:, :], -0.5).then_inc(s_half, 1)
                pool.wait_ge(s_half, 1)
                steps(pool, step, 0, LAST3, ring=R3)

            @block.vector
            def _(dve):
                s_vp = sem("p3_vp")

                def stats(l, q):
                    r, s = rows(q), slot(q)
                    dve.wait_ge(s_add[l], ev(q, 1, 1))
                    for j in range(QT):
                        last = V.bn_stats(st[0:r, l, s, j, :], buf3[l][0:r, s, j, :])
                    last.then_inc(s_bn[l], 1)
                    dve.wait_ge(s_bn[l], ev(q, 1, 1))
                    dve.sem_inc(s_vp, 1)
                    for j in range(QT):
                        last = V.bn_aggr(mv[0:r, l, s, j, :], st[0:r, l, s, j, :])
                    last.then_inc(s_mv[l], 1)
                    dve.wait_ge(s_mv[l], ev(q, 1, 1))
                    V.tensor_scalar(small[0:r, l, s, 0, :], mv[0:r, l, s, :, 1], EPS, None, ALU.add).then_inc(s_ve[l], 1)

                def neg_mean(l, q):
                    r, s = rows(q), slot(q)
                    dve.wait_ge(s_rs[l], ev(q, 1, 1))
                    V.scalar_tensor_tensor(out=small[0:r, l, s, 2, :], in0=mv[0:r, l, s, :, 0], scalar=-1.0,
                                           in1=small[0:r, l, s, 1, :], op0=ALU.mult, op1=ALU.mult).then_inc(s_nm[l], 1)

                def step(q):
                    b, c = sh(q, -1), sh(q, -2)
                    if inside(q, 0, NQ):
                        r, s = rows(q), slot(q)
                        dve.wait_ge(s_y, ev(q, 1, 1))
                        V.tensor_tensor(yo[0:r, s, :, :], psY[0][0:r, :, :],
                                        shift[0:r, :].unsqueeze(1).broadcast_to([r, QT, D]), ALU.add).then_inc(s_o, 1)
                    if inside(b, 0, NQ):
                        r, s = rows(b), slot(b)
                        dve.wait_ge(s_th, ev(b, 1, 1))
                        V.tensor_tensor(xin[0:r, s, :, :], xin[0:r, s, :, :], yo[0:r, s, :, :], ALU.add).then_inc(s_add[0], 1)
                        stats(0, b)
                    if inside(c, 0, NQ):
                        r, s = rows(c), slot(c)
                        dve.wait_ge(s_norm[0], ev(c, 1, 1))
                        wait(dve, s_st4[s], nth(c, 16))
                        V.tensor_tensor(y3[0:r, s, :, :], xin[0:r, s, :, :],
                                        c3[0:r, :].unsqueeze(1).broadcast_to([r, QT, D]), ALU.add).then_inc(s_add[1], 1)
                        stats(1, c)
                    if inside(b, 0, NQ):
                        neg_mean(0, b)
                    if inside(c, 0, NQ):
                        neg_mean(1, c)

                steps(dve, step, 0, LAST3, ring=R3)

        def store_of(table_rows, q, of):
            return chunk_of(of, q).rearrange("p n d -> p (n d)")

        def load_group(sp, g, pairs, s_to, s_go, frees):
            n, h = group_tiles(g), slot(g)
            i, c, _ = g
            t = c * GT if i is None else i * (2 * GT) + c * GT
            for s, v in frees:
                wait(sp, s, v)
                sp.sem_inc(s_go, 1)
            for table, to in pairs:
                sp.dma_start(to[:, h, 0:n, :].rearrange("p n d -> p (n d)"),
                             table[:, bass.ds(t * D, n * D)]).then_inc(s_to[h], 16)

        with phase() as scope:
            psT = pb("e2b_psT", [P, KB, QT, P], F32, scope)
            psY = pb("e2b_psY", [P, QT, D], F32, scope)
            (s_pk, s_go, s_vgo, s_spgo, s_t, s_tc, s_y, s_o, s_th, s_add, s_bn, s_mv, s_sd, s_rs, s_nm, s_norm) = (
                sem(f"e2b_{n}") for n in ("pk", "go", "vgo", "spgo", "t", "tc", "y", "o", "th", "add", "bn", "mv", "sd",
                                          "rs", "nm", "norm"))
            s_in2 = [sem(f"e2b_in{k}") for k in range(2)]
            s_sc = [sem(f"e2b_sc{k}") for k in range(2)]
            s_lin = [sem(f"e2b_lin{k}") for k in range(2)]
            block = scope.enter_context(nc.Block())

            @block.sync
            def _(sp):
                def step(g):
                    if inside(g, 0, 2 * GI):
                        h = slot(g)
                        load_group(sp, g, ((agg2, msg), (x2e, own)), s_in2, s_spgo,
                                   ((s_sc[h], nth(g, 16 * GT)), (s_t, ev(g, 2, -2)), (s_lin[h], nth(g, 32))))
                    b = sh(g, -1)
                    if inside(b, 0, 2 * GI):
                        i, c, _ = b
                        for k in range(2 if group_tiles(b) == GT else 1):
                            store(sp, x3e, own, (i, 2 * c + k, 4), s_norm, s_spgo, s_lin[slot(b)])

                groups(sp, step, 2 * GI + 1)
                sp.wait_ge(s_lin[0], 32 * GI + 16)
                sp.wait_ge(s_lin[1], 32 * GI)

            @block.gpsimd
            def _(pool):
                def step(g):
                    wait(pool, s_sc[slot(g)], nth(g, 16 * GT))
                    indices(pool, 1, g, s_pk, s_go)
                    pool.wait_ge(s_norm, FIX + 1 if group_tiles(g) == 1 else ev(g, 2, 2))
                    pool.sem_inc(s_go, 1)
                    scatter_rows(pool, x3, slot(g), group_tiles(g), s_sc[slot(g)])

                groups(pool, step, 2 * GI)
                pool.wait_ge(s_sc[0], 16 * (GI * GT + 1))
                pool.wait_ge(s_sc[1], 16 * GI * GT)

            @block.tensor
            def _(pe):
                def step(q):
                    pe.wait_ge(s_in2[half(q)], two_loads(q))
                    wait(pe, s_tc, ev(q))
                    transposed(q, 0, msg, psT, s_t)
                    pe.wait_ge(s_tc, ev(q, 1, 1))
                    wait(pe, s_o, ev(q))
                    product(q, 0, W2s, psY, s_y)

                def two_loads(q):
                    c = 32 * (q[1] // 4 + 1)
                    return c if q[0] is None else q[0] * 32 + c

                chunks(pe, step, FIX)

            @block.scalar
            def _(act):
                def step(q):
                    if inside(q, 0, FIX):
                        n = ntiles(q)
                        act.wait_ge(s_t, ev(q, 1, 1))
                        wait(act, s_y, ev(q, 1, -1))
                        A.activation(tT[:, q[1] % 2, 0, :, 0:n, :], psT[:, :, 0:n, :], ACT.Copy).then_inc(s_tc, 1)
                        act.wait_ge(s_o, ev(q, 1, 1))
                        A.activation(o4[:, q[1] % 2, 0:n, :], o4[:, q[1] % 2, 0:n, :], ACT.Tanh).then_inc(s_th, 1)
                    b = sh(q, -1)
                    if inside(b, 0, FIX):
                        deviation(0, b, s_mv, s_sd)
                        normalise(0, b, own_row, s_nm, s_norm)

                chunks(act, step, FIX + 1)

            @block.vector
            def _(dve):
                def step(q):
                    if inside(q, 0, FIX):
                        n = ntiles(q)
                        dve.wait_ge(s_y, ev(q, 1, 1))
                        wait(dve, s_add, ev(q, 1, -1))
                        V.tensor_tensor(o4[:, q[1] % 2, 0:n, :], psY[:, 0:n, :], over(shift[:, :], n), ALU.add).then_inc(s_o, 1)
                    b = sh(q, -1)
                    if inside(b, 0, FIX):
                        n = ntiles(b)
                        dve.wait_ge(s_th, ev(b, 1, 1))
                        V.tensor_tensor(chunk_of(own, b), o4[:, b[1] % 2, 0:n, :], chunk_of(own, b), ALU.add).then_inc(s_add, 1)
                        statistics(0, b, own_row, s_add, s_bn, s_vgo, s_mv)
                        reciprocals(0, b, s_sd, s_rs, s_nm)

                chunks(dve, step, FIX + 1)

        score = sb("score", [P, EC, HEADS])
        with phase() as scope:
            psT = [pb(f"e3_psT{k}", [P, KB, QT, P], F32, scope) for k in "AB"]
            psY = pb("e3_psY", [P, QT, D], F32, scope)
            psE = pb("e3_psE", [P, QT, HEADS], F32, scope)
            s_pk, s_go, s_spgo, s_ta, s_t, s_tc, s_ya, s_y, s_h = (sem(f"e3_{n}") for n in (
                "pk", "go", "spgo", "ta", "t", "tc", "ya", "y", "h"))
            s_g = [sem(f"e3_g{k}") for k in range(2)]
            s_lin = [sem(f"e3_lin{k}") for k in range(2)]
            block = scope.enter_context(nc.Block())

            @block.gpsimd
            def _(pool):
                def step(g):
                    wait(pool, s_t, ev(g, 2, -2))
                    indices(pool, 1, g, s_pk, s_go)
                    for u in range(GT):
                        gather(pool, x3, msg[:, slot(g), u, :], slot(g), u, 0, s_g[slot(g)])
                        gather(pool, x3, own[:, slot(g), u, :], slot(g), u, 1, s_g[slot(g)])

                groups(pool, step, 2 * GI - 1)

            @block.tensor
            def _(pe):
                def step(q):
                    pe.wait_ge(s_g[half(q)], landed(q, 2))
                    wait(pe, s_tc, ev(q))
                    transposed(q, 0, msg, psT[0], s_ta)
                    transposed(q, 1, own, psT[1], s_t)
                    pe.wait_ge(s_tc, ev(q, 1, 1))
                    wait(pe, s_h, ev(q))
                    product(q, 0, W3, psY, s_ya)
                    for j in range(ntiles(q)):
                        for k, weights in enumerate((Was, Wad)):
                            for b in range(KB):
                                last = T.matmul(psE[:, j, :], tT[:, q[1] % 2, k, b, j, :], weights[:, b, :],
                                                start=(k == 0 and b == 0), stop=(k == 1 and b == KB - 1))
                    last.then_inc(s_y, 1)

                chunks(pe, step, FIX - 1)

            @block.scalar
            def _(act):
                def step(q):
                    n = ntiles(q)
                    act.wait_ge(s_t, ev(q, 1, 1))
                    wait(act, s_y, ev(q, 1, -1))
                    for k in range(2):
                        last = A.activation(tT[:, q[1] % 2, k, :, 0:n, :], psT[k][:, :, 0:n, :], ACT.Copy)
                    last.then_inc(s_tc, 1)

                chunks(act, step, FIX - 1)

            @block.vector
            def _(dve):
                def step(q):
                    n, h, j0 = ntiles(q), half(q), q[1] % 2 * 4
                    dve.wait_ge(s_y, ev(q, 1, 1))
                    wait(dve, s_lin[h], stored(q))
                    V.tensor_copy(tot[:, h, j0:j0 + n, :], psY[:, 0:n, :])
                    V.tensor_copy(score[:, bass.ds(tile0(q), n), :], psE[:, 0:n, :]).then_inc(s_h, 1)

                chunks(dve, step, FIX - 1)

            @block.sync
            def _(sp):
                chunks(sp, lambda q: store(sp, h3, tot, q, s_h, s_spgo, s_lin[half(q)]), FIX - 1)
                sp.wait_ge(s_lin[0], 32 * GI)
                sp.wait_ge(s_lin[1], 32 * GI)

        attend = sb("attend", [P, EC, HEADS])
        rden = sb("rden", [P, TOTAL, HEADS])
        with phase() as scope:
            eh = sb("eh", [P, HEADS, EC], F32, scope)
            fwd = sb("fwd", [P, HEADS, TOTAL], F32, scope)
            bwd = sb("bwd", [P, HEADS, EC], F32, scope)
            pf = sb("pf", [P, 2, EC], F32, scope)
            pbk = sb("pbk", [P, 2, EC], F32, scope)
            dg = sb("dg", [P, 2, HEADS, P], F32, scope)
            cr = sb("cr", [P, 2, HEADS, P], F32, scope)
            edge_in = sb("edge_in", [P, 2, HEADS], F32, scope)
            ends = sb("ends", [P, HEADS], F32, scope)
            psC = [pb(f"s3_psC{k}", [P, HEADS, P], F32, scope) for k in range(2)]
            psD = pb("s3_psD", [P, HEADS], F32, scope)
            s_c, s_dg3, s_cr, s_sub, s_ex, s_tl, s_dn = (sem(f"s3_{n}") for n in ("c", "dg", "cr", "sub", "ex", "tl", "dn"))
            block = scope.enter_context(nc.Block())

            @block.tensor
            def _(pe):
                pe.wait_ge(s_dg3, 1)
                for k in range(2):
                    for a in range(2):
                        last = T.matmul(psC[k][:, 4 * a:4 * a + 4, :], ones[:, :], dg[:, k, 4 * a:4 * a + 4, :], start=True, stop=True)
                last.then_inc(s_cr, 1)
                pe.wait_ge(s_tl, 1)
                T.matmul(psD[:, :], feeds[1][:, :], ends[:, :], start=True, stop=True).then_inc(s_dn, 1)

            @block.scalar
            def _(act):
                act.wait_ge(s_sub, 1)
                A.activation(eh[:, :, :], eh[:, :, :], ACT.Exp).then_inc(s_ex, 1)

            @block.vector
            def _(dve):
                chain = [0]

                def link(ins):
                    chain[0] += 1
                    ins.then_inc(s_c, 1)
                    dve.wait_ge(s_c, chain[0])

                link(V.scalar_tensor_tensor(out=eh[:, :, :], in0=score[:, :, :].rearrange("p t h -> p h t"), scalar=0.2,
                                            in1=score[:, :, :].rearrange("p t h -> p h t"), op0=ALU.mult, op1=ALU.max))
                for k, of in ((0, go_on[1]), (1, whole[1])):
                    link(V.tensor_scalar(pf[:, k, :], of[:, :], 1.0, 1e30, ALU.subtract, ALU.mult))
                link(V.tensor_scalar(pbk[:, 1, :], on_next[:, :], 1.0, 1e30, ALU.subtract, ALU.mult))
                link(V.tensor_copy(pbk[:, 0, :], pbk[:, 1, :]))
                link(V.memset(pbk[:, 0, EC - 1:EC], -1e30))
                for hd in range(HEADS):
                    V.tensor_tensor_scan(fwd[:, hd, 0:EC], pf[:, 0, :], eh[:, hd, :], -1e30, ALU.add, ALU.max)
                    last = V.tensor_tensor_scan(bwd[:, hd, ::-1], pbk[:, 0, ::-1], eh[:, hd, ::-1], -1e30, ALU.add, ALU.max)
                link(last)
                for hd in range(HEADS):
                    V.tensor_scalar(dg[:, 0, hd, :], ident[:, :], fwd[:, hd, EC - 1:EC], None, ALU.mult)
                    last = V.tensor_scalar(dg[:, 1, hd, :], ident[:, :], bwd[:, hd, 0:1], None, ALU.mult)
                last.then_inc(s_dg3, 1)
                dve.wait_ge(s_cr, 1)
                for k, pen in ((0, pen_f), (1, pen_b)):
                    link(V.tensor_tensor(cr[:, k, :, :], psC[k][:, :, :], pen[:, :].unsqueeze(1).broadcast_to([P, HEADS, P]), ALU.add))
                    link(V.tensor_reduce(edge_in[:, k, :], cr[:, k, :, :], AX_X, ALU.max))
                for hd in range(HEADS):
                    V.tensor_tensor_scan(fwd[:, hd, 0:EC], pf[:, 1, :], eh[:, hd, :], edge_in[:, 0, hd:hd + 1], ALU.add, ALU.max)
                    last = V.tensor_tensor_scan(bwd[:, hd, ::-1], pbk[:, 1, ::-1], eh[:, hd, ::-1], edge_in[:, 1, hd:hd + 1],
                                                ALU.add, ALU.max)
                link(last)
                link(V.tensor_tensor(bwd[:, :, :], fwd[:, :, 0:EC], bwd[:, :, :], ALU.max))
                V.tensor_tensor(eh[:, :, :], eh[:, :, :], bwd[:, :, :], ALU.subtract).then_inc(s_sub, 1)
                dve.wait_ge(s_ex, 1)
                link(V.tensor_copy(attend[:, :, :], eh[:, :, :].rearrange("p h t -> p t h")))
                for hd in range(HEADS):
                    last = V.tensor_tensor_scan(fwd[:, hd, 0:EC], go_on[1][:, :], eh[:, hd, :], 0.0, ALU.mult, ALU.add)
                link(last)
                V.tensor_copy(ends[:, :], fwd[:, :, EC - 1]).then_inc(s_tl, 1)
                dve.wait_ge(s_dn, 1)
                link(V.tensor_copy(edge_in[:, 0, :], psD[:, :]))
                for hd in range(HEADS):
                    last = V.tensor_tensor_scan(fwd[:, hd, 0:EC], whole[1][:, :], eh[:, hd, :], edge_in[:, 0, hd:hd + 1],
                                                ALU.mult, ALU.add)
                link(last)
                link(V.tensor_tensor(bwd[:, :, :], fwd[:, :, 0:EC], leadend[1][:, :].unsqueeze(1).broadcast_to([P, HEADS, EC]), ALU.mult))
                link(V.tensor_reduce(fwd[:, :, EC], bwd[:, :, :], AX_X, ALU.add))
                link(V.tensor_scalar(ends[:, :], valid[:, EC:EC + 1].broadcast_to([P, HEADS]), -1.0, 1.0, ALU.mult, ALU.add))
                link(V.tensor_tensor(fwd[:, :, EC], fwd[:, :, EC], ends[:, :], ALU.add))
                link(V.tensor_scalar(fwd[:, :, :], fwd[:, :, :], 1e-16, None, ALU.add))
                link(V.reciprocal(fwd[:, :, :], fwd[:, :, :]))
                link(V.tensor_copy(rden[:, :, :], fwd[:, :, :].rearrange("p h t -> p t h")))

        with phase() as scope:
            psF = pb("e3b_psF", [P, D], F32, scope)[:, :]
            (s_pk, s_go, s_vgo, s_spgo, s_scaled, s_acc, s_lr, s_fix, s_o, s_add, s_bn, s_mv, s_sd, s_rs, s_nm, s_norm) = (
                sem(f"e3b_{n}") for n in ("pk", "go", "vgo", "spgo", "scaled", "acc", "lr", "fix", "o", "add", "bn", "mv",
                                          "sd", "rs", "nm", "norm"))
            s_hin = [sem(f"e3b_h{k}") for k in range(2)]
            s_own = [sem(f"e3b_own{k}") for k in range(2)]
            s_sc = [sem(f"e3b_sc{k}") for k in range(2)]
            block = scope.enter_context(nc.Block())

            @block.sync
            def _(sp):
                def step(g):
                    h = slot(g)
                    frees = ((s_sc[h], nth(g, 16 * GT)), (s_acc, ev(g, GT, 1 - GT)), (s_o, ev(g, 4, -4)))
                    if group_tiles(g) == GT:
                        load_group(sp, g, ((h3, msg),), s_hin, s_spgo, frees)
                    load_group(sp, g, ((x3e, own),), s_own, s_spgo, frees)

                groups(sp, step, 2 * GI)

            @block.gpsimd
            def _(pool):
                def step(g):
                    wait(pool, s_sc[slot(g)], nth(g, 16 * GT))
                    indices(pool, 1, g, s_pk, s_go)
                    pool.wait_ge(s_norm, FIX + 1 if group_tiles(g) == 1 else ev(g, 2, 2))
                    pool.sem_inc(s_go, 1)
                    scatter_rows(pool, out, slot(g), group_tiles(g), s_sc[slot(g)])

                groups(pool, step, 2 * GI)
                pool.wait_ge(s_sc[0], 16 * (GI * GT + 1))
                pool.wait_ge(s_sc[1], 16 * GI * GT)

            @block.tensor
            def _(pe):
                pe.wait_ge(s_acc, EC - 1)
                T.matmul(psF, feeds[1][:, :], msg[:, 1, GT - 1, :], start=True, stop=True).then_inc(s_fix, 1)

            @block.scalar
            def _(act):
                def step(q):
                    deviation(0, q, s_mv, s_sd)
                    normalise(0, q, own_row, s_nm, s_norm)

                chunks(act, step, FIX)

            @block.vector
            def _(dve):
                def by_head(a):
                    return a.rearrange("p n (h d) -> p n h d", d=HD)

                def step(q):
                    if inside(q, 0, FIX):
                        n, h, t0 = ntiles(q), half(q), tile0(q)
                        if not (q[0] is None and q[1] == FIX):
                            dve.wait_ge(s_hin[h], loads(q))
                            m = by_head(chunk_of(msg, q))
                            V.tensor_tensor(m, m, attend[:, bass.ds(t0, n), :].unsqueeze(3).broadcast_to([P, n, HEADS, HD]),
                                            ALU.mult).then_inc(s_scaled, 1)
                        accumulate(q, 1, s_scaled, ev(q, 1, 1), s_acc, s_lr, s_fix)
                        wait(dve, s_acc, t0 + (n - 1))
                        oq = o4[:, q[1] % 2, 0:n, :]
                        V.tensor_tensor(by_head(oq), by_head(chunk_of(msg, q)),
                                        rden[:, bass.ds(t0, n), :].unsqueeze(3).broadcast_to([P, n, HEADS, HD]),
                                        ALU.mult).then_inc(s_o, 1)
                        dve.wait_ge(s_o, ev(q, 2, 1))
                        V.tensor_tensor(oq, oq, over(B3, n), ALU.add).then_inc(s_o, 1)
                        dve.wait_ge(s_o, ev(q, 2, 2))
                        dve.wait_ge(s_own[h], loads(q))
                        V.scalar_tensor_tensor(out=chunk_of(own, q), in0=oq, scalar=0.0, in1=chunk_of(own, q),
                                               op0=ALU.max, op1=ALU.add).then_inc(s_add, 1)
                        statistics(0, q, own_row, s_add, s_bn, s_vgo, s_mv)
                    b = sh(q, -1)
                    if inside(b, 0, FIX):
                        reciprocals(0, b, s_sd, s_rs, s_nm)

                V.memset(lr[:, :], 0.0).then_inc(s_lr, 1)
                chunks(dve, step, FIX + 1)


_INS = ["x", "src", "dst", "edge_weight", "L0_gnn_W", "L1_gnn_W", "L1_gnn_b", "L1_gnn_ln_gamma", "L1_gnn_ln_beta",
        "L1_gnn_res_W", "L1_gnn_res_b", "L2_gnn_W", "L2_gnn_b", "L2_gnn_gamma", "L2_gnn_beta", "L3_gnn_W",
        "L3_gnn_att_src", "L3_gnn_att_dst", "L3_gnn_bias"]


def kernel(**inputs):
    import numpy as np
    import concourse.bacc as bacc
    from concourse.bass_utils import run_bass_kernel_spmd

    nc = bacc.Bacc("TRN2", target_bir_lowering=False, num_devices=1)
    arrays, args = {}, []
    for name in _INS:
        a = np.ascontiguousarray(inputs[name])
        arrays[f"in_{name}"] = a
        args.append(nc.dram_tensor(f"in_{name}", a.shape, mybir.dt.from_np(a.dtype), kind="ExternalInput").ap())
    args.append(nc.dram_tensor("out_0", (N, D), F32, kind="ExternalOutput").ap())
    build(nc, *args)
    r = run_bass_kernel_spmd(nc, [arrays], core_ids=[0])
    return r.results[0]["out_0"]
```

```python
from contextlib import ExitStack, contextmanager

import concourse.bass as bass
from concourse import mybir

F32 = mybir.dt.float32
BF16 = mybir.dt.bfloat16
I32 = mybir.dt.int32
ALU = mybir.AluOpType
ACT = mybir.ActivationFunctionType
AX_X = mybir.AxisListType.X

P = 128
D = 256
KB = D // P
EPS = 1e-5

N = 100000
QT = 4
NPP = N // (P * QT) * QT
NQ = NPP // QT
TAIL = (N - P * NPP) // QT
RING = 3
ITERS = NQ // RING

E = 25000
EC = -(-E // P)
EP = P * EC
GT = 7
SI = EC // (2 * GT)
NH = 4
GI = EC // (NH * GT)
NG = NH * GI
PADKEY = (1 << 17) - 1
SKIP = 1 << 18
DIGITS = ((0, 5), (5, 4), (9, 4), (13, 4))
ND = max(1 << bits for _, bits in DIGITS)


def ev(q, mul=1, add=0):
    i, c, u = q
    return c * mul + add if i is None else i * (u * mul) + (c * mul + add)


def sh(q, k):
    return (q[0], q[1] + k, q[2])


def slot(q):
    return q[1] % q[2]


def nth(q, mul=1, add=0):
    i, c, u = q
    return c // u * mul + add if i is None else i * mul + (c // u * mul + add)


def inside(q, lo, hi):
    return q[0] is not None or lo <= q[1] <= hi


def wait(eng, sem, value):
    if type(value) is not int or value > 0:
        eng.wait_ge(sem, value)


def rows(q):
    return TAIL if q[0] is None and q[1] == NQ else P


def value(eng, v):
    return v if type(v) is int else eng.snap(v)


def quad_of(table, q, at=None):
    if rows(q) == TAIL:
        return table[P * NPP:N, :].rearrange("(p j) d -> p (j d)", j=QT)
    return table[0:P * NPP, :].rearrange("(p n) d -> p (n d)", n=NPP)[:, bass.ds(ev(q, QT * D) if at is None else at, QT * D)]


def steps(eng, step, first, last, cuts=(), at_cut=None, ring=RING):
    iters = NQ // ring
    for c in range(first, 2 * ring):
        step((None, c, ring))
    edges = [2] + list(cuts) + [iters - 1]
    for n in range(len(edges) - 1):
        if n >= 1:
            at_cut(n - 1, edges[n])
        with eng.Fori(edges[n], edges[n + 1]) as i:
            for u in range(ring):
                step((i, u, ring))
    for c in range(ring * (iters - 1), last + 1):
        step((None, c, ring))


FIX = 2 * NG
CB = 2 * NH


def is_fix(q):
    return q[0] is None and q[1] >= FIX


def tile0(q):
    i, c, _ = q
    at = c // 2 * GT + c % 2 * 4
    return at if i is None else i * (NH * GT) + at


def ntiles(q):
    return 1 if is_fix(q) else 4 - q[1] % 2


def half(q):
    return q[1] // 2 % NH


def filled(q, per_group):
    c = per_group * (q[1] // CB + 1)
    return c if q[0] is None else q[0] * per_group + c


def landed(q, per):
    return 16 * per * (GI * GT + 1) if is_fix(q) else filled(q, 16 * per * GT)


def loads(q):
    return filled(q, 16)


def chunks(eng, step, last):
    for c in range(CB):
        step((None, c, CB))
    with eng.Fori(1, GI) as i:
        for u in range(CB):
            step((i, u, CB))
    for c in range(FIX, last + 1):
        step((None, c, CB))


def chunks_ahead(eng, step, last):
    for c in range(CB):
        step((None, c, CB))
    with eng.Fori(1, GI - 1) as i:
        for u in range(CB):
            step((i, u, CB))
    for c in range(FIX - CB, last + 1):
        step((None, c, CB))


def groups(eng, step, last):
    for g in range(NH):
        step((None, g, NH))
    with eng.Fori(1, GI) as i:
        for u in range(NH):
            step((i, u, NH))
    for g in range(NG, last + 1):
        step((None, g, NH))


def group_tile0(g):
    return ev(g, GT)


def group_tiles(g):
    return 1 if g[0] is None and g[1] >= NG else GT



def build(nc, x, src, dst, ew, w0, w1, b1, g1, be1, wr, br, w2, b2, g2, be2, w3, as3, ad3, b3, out):
    ctx = ExitStack()
    with ctx:
        def sb(name, shape, dt=F32, scope=ctx):
            return scope.enter_context(nc.sbuf_tensor(name, shape, dt))

        def pb(name, shape, dt=F32, scope=ctx):
            return scope.enter_context(nc.psum_tensor(name, shape, dt))

        taken = []

        def sem(name):
            taken.append(nc.alloc_semaphore(name=name))
            return taken[-1]

        @contextmanager
        def phase():
            with ExitStack() as scope:
                yield scope
            nc.clear_and_free_semaphores(list(taken))
            nc.all_engine_barrier()
            taken.clear()

        def dram(name, shape, dt=F32):
            return nc.dram_tensor(name, shape, dt, kind="Internal").ap()

        x1 = dram("x1", [N, D])
        x2 = dram("x2", [N, D])
        x3 = dram("x3", [N, D])
        sorted_src = dram("sorted_src", [EP + 2, 4], I32)
        sorted_dst = dram("sorted_dst", [EP + 2, 4], I32)
        rec_dram = (sorted_src, sorted_dst)

        ident = sb("ident", [P, P])
        ones = sb("ones", [P, P])
        before = sb("before", [P, P])
        eps = sb("eps", [P, 1])
        W0 = sb("W0", [P, KB, D])
        WrI = sb("WrI", [P, KB, D])
        WZ = sb("WZ", [P, KB, 2 * D])
        W1T = sb("W1T", [P, KB, D])
        W2 = sb("W2", [P, KB, D])
        c1 = sb("c1", [P, D])
        vec = sb("vec", [P, 8, D])
        B1, G1, BE1, BR, B2, G2, BE2, B3 = (vec[:, k, :] for k in range(8))
        c3 = sb("c3", [P, D])
        rec = [sb(f"rec{k}", [P, EC, 4], I32) for k in range(2)]

        with phase() as scope:
            raw = sb("raw", [P, 2, KB, D], F32, scope)
            srow = sb("srow", [1, 2, 4], I32, scope)
            cols = sb("cols", [P, 3, EC], I32, scope)
            psw = [pb(f"psw{k}", [P, KB, D], F32, scope) for k in range(4)]
            AC = sb("AC", [P, KB, D], F32, scope)
            ACT_T = sb("ACT_T", [P, KB, D], F32, scope)
            row_mean = sb("row_mean", [P, KB], F32, scope)
            s_const, s_ld, s_raw, s_fill, s_tw, s_sent, s_cols, s_id, s_link, s_ac, s_w0 = map(sem, (
                "s_const", "s_ld", "s_raw", "s_fill", "s_tw", "s_sent", "s_cols", "s_id", "s_link", "s_ac", "s_w0"))
            block = scope.enter_context(nc.Block())

            @block.sync
            def _(sp):
                sp.dma_start(raw[:, 0, :, :], wr.rearrange("(k p) d -> p k d", p=P)).then_inc(s_raw, 16)
                sp.dma_start(raw[:, 1, :, :], w1.rearrange("(k p) d -> p k d", p=P)).then_inc(s_raw, 16)
                sp.dma_start(W0[:, :, :], w0.rearrange("(k p) d -> p k d", p=P)).then_inc(s_w0, 16)
                sp.dma_start(W2[:, :, :], w2.rearrange("(k p) d -> p k d", p=P)).then_inc(s_ld, 16)
                sp.wait_ge(s_fill, 3)
                for k, a in enumerate((src, dst, ew.bitcast(I32))):
                    full = E // EC
                    sp.dma_start(cols[0:full, k, :], a[0:full * EC].rearrange("(p c) -> p c", c=EC)).then_inc(s_cols, 16)
                    sp.dma_start(cols[full:full + 1, k, 0:E - full * EC],
                                 a[full * EC:E].rearrange("(p c) -> p c", p=1)).then_inc(s_cols, 16)
                for k, a in enumerate((b1, g1, be1, br, b2, g2, be2, b3)):
                    sp.dma_start(vec[:, k, :], a.partition_broadcast(P)).then_inc(s_ld, 16)
                sp.wait_ge(s_fill, 5)
                for table in rec_dram:
                    for end in (0, 1):
                        at = end * (EP + 1)
                        sp.dma_start(table[at:at + 1, :], srow[0:1, end, :]).then_inc(s_sent, 16)
                sp.wait_ge(s_sent, 64)
                sp.wait_ge(s_ld, 144)

            @block.gpsimd
            def _(pool):
                for k, fill in ((0, PADKEY), (1, PADKEY), (2, 0)):
                    pool.memset(cols[:, k, :], fill).then_inc(s_fill, 1)
                pool.memset(srow[:, 0, :], -1).then_inc(s_fill, 1)
                pool.memset(srow[:, 1, :], -2).then_inc(s_fill, 1)
                pool.memset(ident[:, :], 0.0).then_inc(s_id, 1)
                pool.memset(before[:, :], 0.0).then_inc(s_id, 1)
                pool.memset(ones[:, :], 1.0).then_inc(s_const, 1)
                pool.memset(eps[:, :], EPS).then_inc(s_const, 1)
                pool.wait_ge(s_id, 2)
                pool.affine_select(out=ident[:, :], in_=ident[:, :], compare_op=ALU.not_equal, fill=1.0, base=0,
                                   pattern=[[-1, P]], channel_multiplier=1).then_inc(s_id, 1)
                pool.affine_select(out=before[:, :], in_=before[:, :], compare_op=ALU.is_ge, fill=1.0, base=0,
                                   pattern=[[-1, P]], channel_multiplier=1).then_inc(s_id, 1)
                pool.wait_ge(s_id, 4)

            @block.tensor
            def _(pe):
                pe.wait_ge(s_raw, 32)
                pe.wait_ge(s_id, 4)
                for m in range(2):
                    for a in range(KB):
                        for b in range(KB):
                            last = nc.tensor.transpose(psw[m][:, b, a * P:(a + 1) * P],
                                                       raw[:, m, a, b * P:(b + 1) * P], ident[:, :])
                    last.then_inc(s_tw, 1)
                pe.wait_ge(s_ac, 1)
                for a in range(KB):
                    for b in range(KB):
                        last = nc.tensor.transpose(psw[2][:, a, b * P:(b + 1) * P], AC[:, b, a * P:(a + 1) * P], ident[:, :])
                last.then_inc(s_tw, 1)
                pe.wait_ge(s_ac, 2)
                for b in range(KB):
                    for a in range(KB):
                        last = nc.tensor.matmul(psw[3][:, b, :], ACT_T[:, a, b * P:(b + 1) * P], WrI[:, a, :],
                                                start=(a == 0), stop=(a == KB - 1))
                last.then_inc(s_tw, 1)

            @block.vector
            def _(dve):
                chain = [0]

                def link(ins):
                    chain[0] += 1
                    ins.then_inc(s_link, 1)
                    dve.wait_ge(s_link, chain[0])

                dve.wait_ge(s_w0, 16)
                dve.wait_ge(s_id, 4)
                link(nc.vector.tensor_copy(AC[:, :, :], W0[:, :, :]))
                for b in range(KB):
                    at = AC[:, b, b * P:(b + 1) * P]
                    link(nc.vector.tensor_tensor(at, at, ident[:, :], ALU.add))
                link(nc.vector.tensor_reduce(row_mean[:, :], AC[:, :, :], AX_X, ALU.add))
                link(nc.vector.tensor_scalar(row_mean[:, :], row_mean[:, :], 1.0 / D, None, ALU.mult))
                for b in range(KB):
                    last = nc.vector.tensor_scalar(AC[:, b, :], AC[:, b, :], row_mean[:, b:b + 1], None, ALU.subtract)
                last.then_inc(s_ac, 1)
                dve.wait_ge(s_ac, 1)
                nc.vector.tensor_copy(WZ[:, :, 0:D], AC[:, :, :])
                for m, to in ((0, WrI), (1, W1T)):
                    dve.wait_ge(s_tw, m + 1)
                    link(nc.vector.tensor_copy(to[:, :, :], psw[m][:, :, :]))
                for b in range(KB):
                    at = WrI[:, b, b * P:(b + 1) * P]
                    link(nc.vector.tensor_tensor(at, at, ident[:, :], ALU.add))
                dve.wait_ge(s_tw, 3)
                nc.vector.tensor_copy(ACT_T[:, :, :], psw[2][:, :, :]).then_inc(s_ac, 1)
                dve.wait_ge(s_tw, 4)
                nc.vector.tensor_copy(WZ[:, :, D:2 * D], psw[3][:, :, :])
                dve.wait_ge(s_ld, 144)
                nc.vector.scalar_tensor_tensor(out=c1[:, :], in0=BE1, scalar=0.0, in1=BR, op0=ALU.max, op1=ALU.add)
                nc.vector.tensor_scalar(c3[:, :], B3, 0.0, None, ALU.max)
                dve.wait_ge(s_cols, 96)
                for k, order in ((0, (0, 1, 2)), (1, (1, 0, 2))):
                    for f in range(3):
                        nc.vector.tensor_copy(rec[k][:, :, f], cols[:, order[f], :])
                for k in range(2):
                    nc.vector.memset(rec[k][:, :, 3], 0)

        with phase() as scope:
            xin = sb("xin", [P, RING, QT, D], F32, scope)
            xT = sb("xT", [P, RING, KB, QT, P], F32, scope)
            y1 = sb("y1", [P, RING, QT, D], F32, scope)
            y2 = sb("y2", [P, RING, QT, D], F32, scope)
            small = sb("small", [P, 2, RING, 3, QT], F32, scope)
            st = sb("st", [P, 2, RING, QT, 6], F32, scope)
            mv = sb("mv", [P, 2, RING, QT, 2], F32, scope)
            digit = sb("digit", [P, EC], I32, scope)
            digit_f = sb("digit_f", [P, EC], BF16, scope)
            iota_i = sb("iota_i", [P, ND], I32, scope)
            iota_d = sb("iota_d", [P, ND], BF16, scope)
            hot = sb("hot", [P, ND, EC], BF16, scope)
            cum = sb("cum", [P, ND, EC], F32, scope)
            below = sb("below", [P, ND], F32, scope)
            count = sb("count", [P, ND], F32, scope)
            offset = sb("offset", [P, ND], F32, scope)
            rank_f = sb("rank_f", [P, EC], F32, scope)
            rank = [sb(f"rank{k}", [P, EC], I32, scope) for k in range(2)]
            rank_slot = sb("rank_slot", [P, 2, GT], I32, scope)
            rec_slot = sb("rec_slot", [P, 2, GT, 4], I32, scope)
            psT = pb("p1_psT", [P, KB, QT, P], F32, scope)
            psZ = [pb(f"psZ{k}", [P, 2, 2, D], F32, scope) for k in range(3)]

            s_x = [sem(f"s_x{k}") for k in range(RING)]
            s_st1 = [sem(f"s_st1{k}") for k in range(RING)]
            s_st2 = [sem(f"s_st2{k}") for k in range(RING)]
            s_t = sem("s_t")
            s_tc = sem("s_tc")
            s_z = sem("s_z")
            s_bn0 = sem("s_bn0")
            s_mv0 = sem("s_mv0")
            s_sd0 = sem("s_sd0")
            s_rs0 = sem("s_rs0")
            s_rows1 = sem("s_rows1")
            s_y2 = sem("s_y2")
            s_bn1, s_mv1, s_sd1, s_rs1, s_nm1 = map(sem, ("s_bn1", "s_mv1", "s_sd1", "s_rs1", "s_nm1"))
            s_rows2 = sem("s_rows2")
            s_dpass = sem("s_dpass")
            s_spass = sem("s_spass")
            s_rec = [sem(f"s_rec{k}") for k in range(2)]
            s_iota, s_chain, s_cnt, s_off, s_offr, s_rank, s_slotc, s_pass = map(sem, (
                "s_iota", "s_chain", "s_cnt", "s_off", "s_offr", "s_rank", "s_slotc", "s_pass"))
            s_scat = [sem(f"s_scat{k}") for k in range(2)]
            block = scope.enter_context(nc.Block())
            CUTS = [4, 11, 18, 26, 33, 40, 48]
            LAST = NQ + 3

            def psz(q, k):
                return psZ[(2 * q[1] + k) % 3]

            def tiles(k):
                return range(2 * k, 2 * k + 2)

            @block.sync
            def _(sp):
                def load(q):
                    at, used = value(sp, ev(q, QT * D)), value(sp, ev(q, 1, 1 - RING))
                    wait(sp, s_t, used)
                    sp.sem_inc(s_spass, 1)
                    sp.dma_start(xin[0:rows(q), slot(q), :, :].rearrange("p j d -> p (j d)"),
                                 quad_of(x, q, at)).then_inc(s_x[slot(q)], 16)

                def store(of, table, q, s_from, done, s_st):
                    at, done = value(sp, ev(q, QT * D)), value(sp, done)
                    sp.wait_ge(s_from, done)
                    sp.sem_inc(s_spass, 1)
                    sp.dma_start(quad_of(table, q, at),
                                 of[0:rows(q), slot(q), :, :].rearrange("p j d -> p (j d)")).then_inc(s_st[slot(q)], 16)

                def step(q):
                    if inside(sh(q, 2), 0, NQ):
                        load(sh(q, 2))
                    b, d = sh(q, -1), sh(q, -3)
                    if inside(b, 0, NQ):
                        store(y1, x1, b, s_rows1, ev(b, 2, 2), s_st1)
                    if inside(d, 0, NQ):
                        store(y2, x2, d, s_rows2, ev(d, 1, 1), s_st2)

                load((None, 0, RING))
                load((None, 1, RING))
                steps(sp, step, 0, LAST)
                for c in range(RING):
                    sp.wait_ge(s_st1[c], 16 * len(range(c, NQ + 1, RING)))
                    sp.wait_ge(s_st2[c], 16 * len(range(c, NQ + 1, RING)))

            @block.tensor
            def _(pe):
                def transposes(q):
                    pe.wait_ge(s_x[slot(q)], nth(q, 16, 16))
                    wait(pe, s_tc, ev(q))
                    for j in range(QT):
                        for k in range(KB):
                            last = nc.tensor.transpose(psT[:, k, j, 0:rows(q)], xin[0:rows(q), slot(q), j, k * P:(k + 1) * P],
                                                       ident[0:rows(q), 0:rows(q)])
                    last.then_inc(s_t, 1)

                def products(q, k):
                    wait(pe, s_rows1, ev(q, 2, k - 2))
                    wait(pe, s_y2, ev(q, 2, k - 2))
                    for j in tiles(k):
                        for l in range(2):
                            for b in range(KB):
                                last = nc.tensor.matmul(psz(q, k)[0:rows(q), l, j % 2, :], xT[:, slot(q), b, j, 0:rows(q)],
                                                        WZ[:, b, l * D:(l + 1) * D], start=(b == 0), stop=(b == KB - 1))
                    last.then_inc(s_z, 1)

                def step(q):
                    if inside(sh(q, 1), 0, NQ):
                        transposes(sh(q, 1))
                    if inside(q, 0, NQ):
                        pe.wait_ge(s_tc, ev(q, 1, 1))
                        products(q, 0)
                        products(q, 1)

                def sort_offsets(k, i):
                    wait(pe, s_rows1, 2 * RING * i - 2)
                    wait(pe, s_y2, 2 * RING * i - 2)
                    pe.wait_ge(s_cnt, k + 1)
                    nc.tensor.matmul(psZ[0][:, 0, 0, 0:ND], ones[:, :], below[:, :], start=True, stop=False)
                    nc.tensor.matmul(psZ[0][:, 0, 0, 0:ND], before[:, :], count[:, :], start=False, stop=True).then_inc(s_off, 1)
                    pe.wait_ge(s_offr, k + 1)

                step((None, -1, RING))
                sort_offsets(0, 0)
                steps(pe, step, 0, NQ, CUTS, lambda n, i: sort_offsets(n + 1, i))

            @block.scalar
            def _(act):
                def copy_transposed(q):
                    act.wait_ge(s_t, ev(q, 1, 1))
                    wait(act, s_z, ev(q, 2, 2 - 2 * RING))
                    nc.scalar.activation(xT[:, slot(q), :, :, 0:rows(q)], psT[:, :, :, 0:rows(q)], ACT.Copy).then_inc(s_tc, 1)

                def deviation(l, q, lo, hi, s_mv, s_sd, count):
                    act.wait_ge(s_mv, count)
                    r, s = rows(q), slot(q)
                    nc.scalar.activation(small[0:r, l, s, 0, lo:hi], mv[0:r, l, s, lo:hi, 1], ACT.Sqrt,
                                         bias=eps[0:r, :]).then_inc(s_sd, 1)

                def scale_x1(q, k):
                    r, s = rows(q), slot(q)
                    act.wait_ge(s_rs0, ev(q, 2, k + 1))
                    wait(act, s_st1[s], nth(q, 16))
                    for j in tiles(k):
                        last = nc.scalar.activation(y1[0:r, s, j, :], psz(q, k)[0:r, 0, j % 2, :], ACT.Copy,
                                                    scale=small[0:r, 0, s, 1, j:j + 1])
                    last.then_inc(s_rows1, 1)

                def normalise_x2(q):
                    r, s = rows(q), slot(q)
                    act.wait_ge(s_nm1, ev(q, 1, 1))
                    for j in range(QT):
                        last = nc.scalar.activation(y2[0:r, s, j, :], y2[0:r, s, j, :], ACT.Identity,
                                                    bias=small[0:r, 1, s, 2, j:j + 1], scale=small[0:r, 1, s, 1, j:j + 1])
                    last.then_inc(s_rows2, 1)

                def step(q):
                    nxt, b, c = sh(q, 1), sh(q, -1), sh(q, -2)
                    here = inside(q, 0, NQ)
                    if inside(nxt, 0, NQ):
                        copy_transposed(nxt)
                    if here:
                        deviation(0, q, 0, 2, s_mv0, s_sd0, ev(q, 2, 1))
                    if inside(c, 0, NQ):
                        normalise_x2(c)
                    if here:
                        scale_x1(q, 0)
                        deviation(0, q, 2, 4, s_mv0, s_sd0, ev(q, 2, 2))
                    if inside(b, 0, NQ):
                        deviation(1, b, 0, QT, s_mv1, s_sd1, ev(b, 1, 1))
                    if here:
                        scale_x1(q, 1)

                step((None, -1, RING))
                steps(act, step, 0, NQ + 2)

            @block.vector
            def _(dve):
                def partial0(q, k):
                    r, s = rows(q), slot(q)
                    dve.wait_ge(s_z, ev(q, 2, k + 1))
                    for j in tiles(k):
                        last = nc.vector.bn_stats(st[0:r, 0, s, j, :], psz(q, k)[0:r, 0, j % 2, :])
                    last.then_inc(s_bn0, 1)

                def total0(q, k):
                    r, s = rows(q), slot(q)
                    dve.wait_ge(s_bn0, ev(q, 2, k + 1))
                    dve.sem_inc(s_dpass, 1)
                    for j in tiles(k):
                        last = nc.vector.bn_aggr(mv[0:r, 0, s, j, :], st[0:r, 0, s, j, :])
                    last.then_inc(s_mv0, 1)

                def reciprocal0(q, k):
                    r, s = rows(q), slot(q)
                    dve.wait_ge(s_sd0, ev(q, 2, k + 1))
                    nc.vector.reciprocal(small[0:r, 0, s, 1, 2 * k:2 * k + 2], small[0:r, 0, s, 0, 2 * k:2 * k + 2]).then_inc(s_rs0, 1)

                def layer1(q, k):
                    r, s = rows(q), slot(q)
                    dve.wait_ge(s_rs0, ev(q, 2, k + 1))
                    wait(dve, s_st2[s], nth(q, 16))
                    for j in tiles(k):
                        last = nc.vector.scalar_tensor_tensor(out=y2[0:r, s, j, :], in0=psz(q, k)[0:r, 1, j % 2, :],
                                                              scalar=small[0:r, 0, s, 1, j:j + 1], in1=c1[0:r, :],
                                                              op0=ALU.mult, op1=ALU.add)
                    last.then_inc(s_y2, 1)

                def partial1(q):
                    r, s = rows(q), slot(q)
                    dve.wait_ge(s_y2, ev(q, 2, 2))
                    for j in range(QT):
                        last = nc.vector.bn_stats(st[0:r, 1, s, j, :], y2[0:r, s, j, :])
                    last.then_inc(s_bn1, 1)

                def total1(q):
                    r, s = rows(q), slot(q)
                    dve.wait_ge(s_bn1, ev(q, 1, 1))
                    dve.sem_inc(s_dpass, 1)
                    for j in range(QT):
                        last = nc.vector.bn_aggr(mv[0:r, 1, s, j, :], st[0:r, 1, s, j, :])
                    last.then_inc(s_mv1, 1)

                def reciprocal1(q):
                    r, s = rows(q), slot(q)
                    dve.wait_ge(s_sd1, ev(q, 1, 1))
                    nc.vector.reciprocal(small[0:r, 1, s, 1, :], small[0:r, 1, s, 0, :]).then_inc(s_rs1, 1)

                def neg_mean1(q):
                    r, s = rows(q), slot(q)
                    dve.wait_ge(s_rs1, ev(q, 1, 1))
                    nc.vector.scalar_tensor_tensor(out=small[0:r, 1, s, 2, :], in0=mv[0:r, 1, s, :, 0], scalar=-1.0,
                                                   in1=small[0:r, 1, s, 1, :], op0=ALU.mult, op1=ALU.mult).then_inc(s_nm1, 1)

                def step(q):
                    b = sh(q, -1)
                    here, behind = inside(q, 0, NQ), inside(b, 0, NQ)
                    if here:
                        partial0(q, 0)
                    if behind:
                        layer1(b, 1)
                    if here:
                        total0(q, 0)
                    if behind:
                        partial1(b)
                    if here:
                        reciprocal0(q, 0)
                        partial0(q, 1)
                    if behind:
                        total1(b)
                    if here:
                        total0(q, 1)
                        layer1(q, 0)
                        reciprocal0(q, 1)
                    if behind:
                        reciprocal1(b)
                        neg_mean1(b)

                chain = [0]

                def link(ins):
                    chain[0] += 1
                    ins.then_inc(s_chain, 1)
                    dve.wait_ge(s_chain, chain[0])

                def rank_pass(k):
                    o, r = k % 2, k // 2
                    shift, bits = DIGITS[r]
                    nd = 1 << bits
                    if r:
                        dve.wait_ge(s_rec[o], 16 * r)
                    link(nc.vector.tensor_scalar(digit[:, :], rec[o][:, :, 0], shift, nd - 1,
                                                 ALU.logical_shift_right, ALU.bitwise_and))
                    link(nc.vector.tensor_copy(digit_f[:, :], digit[:, :]))
                    link(nc.vector.tensor_tensor(hot[:, 0:nd, :], digit_f[:, :].unsqueeze(1).broadcast_to([P, nd, EC]),
                                                 iota_d[:, 0:nd].unsqueeze(2).broadcast_to([P, nd, EC]), ALU.is_equal))
                    hot_v = hot[:, 0:nd, :].rearrange("p d c -> p (d c)")
                    cum_v = cum[:, 0:nd, :].rearrange("p d c -> p (d c)")
                    link(nc.vector.tensor_tensor_scan(cum_v, hot_v, hot_v, 0.0, ALU.add, ALU.max))
                    link(nc.vector.memset(below[:, :], 0.0))
                    link(nc.vector.memset(count[:, :], 0.0))
                    link(nc.vector.tensor_copy(below[:, 1:nd], cum[:, 0:nd - 1, EC - 1]))
                    nc.vector.tensor_tensor(count[:, 0:nd], cum[:, 0:nd, EC - 1], below[:, 0:nd],
                                            ALU.subtract).then_inc(s_cnt, 1)
                    dve.wait_ge(s_off, k + 1)
                    nc.vector.tensor_tensor(offset[:, :], psZ[0][:, 0, 0, 0:ND], below[:, :], ALU.subtract).then_inc(s_offr, 1)
                    dve.wait_ge(s_offr, k + 1)
                    link(nc.vector.tensor_tensor(cum[:, 0:nd, :], cum[:, 0:nd, :],
                                                 offset[:, 0:nd].unsqueeze(2).broadcast_to([P, nd, EC]), ALU.add))
                    link(nc.vector.tensor_tensor(cum[:, 0:nd, :], cum[:, 0:nd, :], hot[:, 0:nd, :], ALU.mult))
                    link(nc.vector.tensor_reduce(rank_f[:, :], cum[:, 0:nd, :].rearrange("p d c -> p c d"), AX_X, ALU.add))
                    nc.vector.tensor_copy(rank[o][:, :], rank_f[:, :]).then_inc(s_rank, 1)

                dve.wait_ge(s_iota, 1)
                link(nc.vector.tensor_copy(iota_d[:, :], iota_i[:, :]))
                rank_pass(0)
                steps(dve, step, 0, NQ + 1, CUTS, lambda n, i: rank_pass(n + 1))

            @block.gpsimd
            def _(pool):
                pool.iota(iota_i[:, :], pattern=[[1, ND]], base=0, channel_multiplier=0).then_inc(s_iota, 1)
                copies = 0
                for k in range(2 * len(DIGITS)):
                    o, r = k % 2, k // 2

                    def body(i, first):
                        for h in range(2):
                            if not (first and k == 0):
                                pool.wait_ge(s_scat[h], i * (16 * GT) + k * SI * 16 * GT)
                            pool.tensor_copy(rank_slot[:, h, :], rank[o][:, bass.ds(i * (2 * GT) + h * GT, GT)])
                            pool.tensor_copy(rec_slot[:, h, :, :], rec[o][:, bass.ds(i * (2 * GT) + h * GT, GT), :]).then_inc(s_slotc, 1)
                            pool.wait_ge(s_slotc, i * 2 + (k * SI * 2 + h + 1))
                            pool.sem_inc(s_pass, 1)
                            for u in range(GT):
                                pool.indirect_dma_start(
                                    out=rec_dram[o][:, :], out_offset=bass.IndirectOffsetOnAxis(ap=rank_slot[:, h, u:u + 1], axis=0),
                                    in_=rec_slot[:, h, u, :], in_offset=None, bounds_check=EP + 1,
                                    oob_is_err=False).then_inc(s_scat[h], 16)

                    pool.wait_ge(s_rank, k + 1)
                    body(0, True)
                    with pool.Fori(1, SI) as i:
                        body(i, False)
                    for h in range(2):
                        pool.wait_ge(s_scat[h], (k + 1) * SI * 16 * GT)
                    pool.dma_start(rec[o][:, :, :].rearrange("p c w -> p (c w)"),
                                   rec_dram[o][1:EP + 1, :].rearrange("(p c) w -> p (c w)", c=EC)).then_inc(s_rec[o], 16)
                for o in range(2):
                    pool.wait_ge(s_rec[o], 16 * len(DIGITS))

        inv_deg_src = dram("inv_deg_src", [N, 1])
        dinv_dst = dram("dinv_dst", [N, 1])
        deg_table = (inv_deg_src, dinv_dst)
        go_on = [sb(f"go_on{o}", [P, EC]) for o in range(2)]
        whole = [sb(f"whole{o}", [P, EC]) for o in range(2)]
        leadend = [sb(f"leadend{o}", [P, EC]) for o in range(2)]
        pack = [sb(f"pack{o}", [P, EC + 1, 3], I32) for o in range(2)]
        scale = [sb(f"scale{o}", [P, EC + 1]) for o in range(2)]
        feeds = [sb(f"feeds{o}", [P, P]) for o in range(2)]
        inv_deg_dst = sb("inv_deg_dst", [P, EC + 1])
        weight = sb("weight", [P, EC])
        wsum = sb("wsum", [P, EC + 1])
        valid = sb("valid", [P, EC + 1])
        on_next = sb("on_next", [P, EC])
        pen_f = sb("pen_f", [P, P])
        pen_b = sb("pen_b", [P, P])
        TOTAL = EC + 1
        W3 = sb("W3", [P, KB, D])
        Was = sb("Was", [P, KB, 8])
        Wad = sb("Wad", [P, KB, 8])
        HEADS, HD = as3.shape

        with phase() as scope:
            recp = [sb(f"recp{o}", [P, EC, 4], I32, scope) for o in range(2)]
            recn = [sb(f"recn{o}", [P, EC, 4], I32, scope) for o in range(2)]
            att = sb("att", [P, 2, HEADS, HD], F32, scope)
            prod = sb("prod", [P, HEADS, HD], F32, scope)
            keyf = sb("keyf", [P, EC], F32, scope)
            keyp = sb("keyp", [P, EC], F32, scope)
            keyn = sb("keyn", [P, EC], F32, scope)
            last_e = sb("last_e", [P, EC], F32, scope)
            lead = sb("lead", [P, EC], F32, scope)
            fin = sb("fin", [P, EC + 1], F32, scope)
            idxf = sb("idxf", [P, EC + 1], F32, scope)
            ones_e = sb("ones_e", [P, EC], F32, scope)
            cnt = sb("cnt", [P, EC + 1], F32, scope)
            tmp = sb("tmp", [P, EC + 1], F32, scope)
            start = sb("start", [P, 2], F32, scope)
            diag = sb("diag", [P, 2, P], F32, scope)
            after = sb("after", [P, P], F32, scope)
            before_t = sb("before_t", [P, P], F32, scope)
            full1 = sb("full1", [P, N // P], F32, scope)
            idx_slot = sb("idx_slot", [P, 2, GT], I32, scope)
            val_slot = sb("val_slot", [P, 2, GT], F32, scope)
            ps = pb("ps", [P, 2, P], F32, scope)
            psc = pb("psc", [P, 512], F32, scope)
            (s_in, s_w3, s_one, s_init, s_v, s_dg, s_row, s_tails, s_st0, s_cnt1, s_sq, s_deg, s_slot, s_pass2, s_m) = map(sem, (
                "s_in", "s_w3", "s_one", "s_init", "s_v", "s_dg", "s_row", "s_tails", "s_st0", "s_cnt1", "s_sq", "s_deg",
                "s_slot", "s_pass2", "s_m"))
            s_dsc = [sem(f"s_dsc{k}") for k in range(2)]
            block = scope.enter_context(nc.Block())

            @block.sync
            def _(sp):
                for o in range(2):
                    for t, at in ((recp[o], 0), (recn[o], 2)):
                        sp.dma_start(t[:, :, :].rearrange("p c w -> p (c w)"),
                                     rec_dram[o][at:at + EP, :].rearrange("(p c) w -> p (c w)", c=EC)).then_inc(s_in, 16)
                sp.dma_start(W3[:, :, :], w3.rearrange("(k p) h d -> p k (h d)", p=P)).then_inc(s_w3, 16)
                for k, a in enumerate((as3, ad3)):
                    sp.dma_start(att[:, k, :, :], a.partition_broadcast(P)).then_inc(s_w3, 16)
                sp.wait_ge(s_one, 1)
                for table in deg_table:
                    sp.dma_start(table[0:P * (N // P), 0].rearrange("(p c) -> p c", p=P), full1[:, :]).then_inc(s_init, 16)
                    sp.dma_start(table[P * (N // P):N, 0].rearrange("(p c) -> p c", p=1),
                                 full1[0:1, 0:N % P]).then_inc(s_init, 16)

            @block.gpsimd
            def _(pool):
                pool.memset(full1[:, :], 1.0).then_inc(s_one, 1)
                pool.memset(ones_e[:, :], 1.0).then_inc(s_m, 1)
                pool.memset(after[:, :], 0.0).then_inc(s_m, 1)
                pool.wait_ge(s_m, 2)
                pool.affine_select(out=after[:, :], in_=after[:, :], compare_op=ALU.is_ge, fill=1.0, base=0,
                                   pattern=[[-1, P]], channel_multiplier=1).then_inc(s_m, 1)
                pool.memset(before_t[:, :], 0.0).then_inc(s_m, 1)
                pool.wait_ge(s_m, 4)
                pool.affine_select(out=before_t[:, :], in_=before_t[:, :], compare_op=ALU.is_ge, fill=1.0, base=0,
                                   pattern=[[1, P]], channel_multiplier=-1).then_inc(s_m, 1)
                pool.wait_ge(s_init, 64)
                pool.wait_ge(s_deg, 1)

                def body(i, first, n=GT, halves=2):
                    for h in range(halves):
                        if not first:
                            pool.wait_ge(s_dsc[h], i * (16 * GT))
                        t = i * (2 * GT) + h * GT
                        pool.tensor_copy(idx_slot[:, h, 0:n], pack[0][:, bass.ds(t, n), 2])
                        pool.tensor_copy(val_slot[:, h, 0:n], scale[0][:, bass.ds(t, n)]).then_inc(s_slot, 1)
                        pool.wait_ge(s_slot, i * 2 + (h + 1))
                        pool.sem_inc(s_pass2, 1)
                        for u in range(n):
                            pool.indirect_dma_start(
                                out=inv_deg_src[:, :], out_offset=bass.IndirectOffsetOnAxis(ap=idx_slot[:, h, u:u + 1], axis=0),
                                in_=val_slot[:, h, u:u + 1], in_offset=None, bounds_check=N - 1,
                                oob_is_err=False).then_inc(s_dsc[h], 16)

                body(0, True)
                with pool.Fori(1, SI) as i:
                    body(i, False)
                body(SI, False, 1, 1)
                pool.wait_ge(s_dsc[0], (SI * GT + 1) * 16)
                pool.wait_ge(s_dsc[1], SI * GT * 16)

            @block.tensor
            def _(pe):
                for o in range(2):
                    pe.wait_ge(s_dg, o + 1)
                    for k in range(2):
                        last = nc.tensor.matmul(ps[:, k, :], ones[:, :], diag[:, k, :], start=True, stop=True)
                    last.then_inc(s_row, 1)
                    pe.wait_ge(s_tails, o + 1)
                    nc.tensor.matmul(psc[:, 0:2], feeds[o][:, :], tmp[:, 0:2], start=True, stop=True).then_inc(s_st0, 1)

            @block.scalar
            def _(act):
                act.wait_ge(s_cnt1, 2)
                nc.scalar.activation(scale[1][:, :], cnt[:, :], ACT.Sqrt).then_inc(s_sq, 1)

            @block.vector
            def _(dve):
                chain = [0]

                def link(ins):
                    chain[0] += 1
                    ins.then_inc(s_v, 1)
                    dve.wait_ge(s_v, chain[0])

                V = nc.vector
                dve.wait_ge(s_in, 64)
                dve.wait_ge(s_m, 5)
                for o in range(2):
                    link(V.tensor_copy(keyf[:, :], rec[o][:, :, 0]))
                    link(V.tensor_copy(keyp[:, :], recp[o][:, :, 0]))
                    link(V.tensor_copy(keyn[:, :], recn[o][:, :, 0]))
                    link(V.tensor_tensor(whole[o][:, :], keyf[:, :], keyp[:, :], ALU.is_equal))
                    link(V.tensor_copy(go_on[o][:, :], whole[o][:, :]))
                    link(V.memset(go_on[o][:, 0:1], 0.0))
                    link(V.tensor_tensor(last_e[:, :], keyf[:, :], keyn[:, :], ALU.not_equal))
                    if o == 1:
                        link(V.tensor_tensor(on_next[:, :], keyf[:, :], keyn[:, :], ALU.is_equal))
                    link(V.tensor_scalar(lead[:, :], keyf[:, :], keyf[:, 0:1], whole[o][:, 0:1], ALU.is_equal, ALU.mult))
                    link(V.tensor_tensor(leadend[o][:, :], last_e[:, :], lead[:, :], ALU.mult))
                    link(V.tensor_tensor(fin[:, 0:EC], last_e[:, :], leadend[o][:, :], ALU.subtract))
                    link(V.tensor_reduce(fin[:, EC:EC + 1], leadend[o][:, :], AX_X, ALU.add))
                    link(V.tensor_scalar(idxf[:, :], fin[:, :], -float(SKIP), float(SKIP), ALU.mult, ALU.add))
                    link(V.tensor_tensor(idxf[:, 0:EC], idxf[:, 0:EC], keyf[:, :], ALU.add))
                    link(V.tensor_tensor(idxf[:, EC:EC + 1], idxf[:, EC:EC + 1], keyf[:, 0:1], ALU.add))
                    link(V.tensor_copy(pack[o][:, :, 2], idxf[:, :]))
                    if o == 1:
                        link(V.tensor_scalar(valid[:, :], idxf[:, :], float(N), None, ALU.is_lt))
                    link(V.tensor_scalar(pack[o][:, 0:EC, 1], keyf[:, :], float(N - 1), None, ALU.min))
                    link(V.tensor_scalar(pack[o][:, EC:EC + 1, 1], keyf[:, 0:1], float(N - 1), None, ALU.min))
                    link(V.tensor_copy(keyp[:, :], rec[o][:, :, 1]))
                    link(V.tensor_scalar(pack[o][:, 0:EC, 0], keyp[:, :], float(N - 1), None, ALU.min))
                    link(V.memset(pack[o][:, EC:EC + 1, 0], 0))
                    link(V.tensor_scalar(diag[:, 0, :], ident[:, :], keyf[:, 0:1], None, ALU.mult))
                    V.tensor_scalar(diag[:, 1, :], ident[:, :], keyf[:, EC - 1:EC], None, ALU.mult).then_inc(s_dg, 1)
                    dve.wait_ge(s_row, o + 1)
                    link(V.scalar_tensor_tensor(out=feeds[o][:, :], in0=ps[:, 0, :], scalar=keyf[:, EC - 1:EC],
                                                in1=before[:, :], op0=ALU.is_equal, op1=ALU.mult))
                    if o == 1:
                        for pen, k, key, where in ((pen_f, 1, keyf[:, 0:1], before_t), (pen_b, 0, keyf[:, EC - 1:EC], after)):
                            link(V.scalar_tensor_tensor(out=pen[:, :], in0=ps[:, k, :], scalar=key, in1=where[:, :],
                                                        op0=ALU.is_equal, op1=ALU.mult))
                            link(V.tensor_scalar(pen[:, :], pen[:, :], 1.0, 1e30, ALU.subtract, ALU.mult))
                    else:
                        link(V.tensor_copy(weight[:, :], rec[0][:, :, 2].bitcast(F32)))
                    link(V.tensor_tensor_scan(cnt[:, 0:EC], go_on[o][:, :], ones_e[:, :], 0.0, ALU.mult, ALU.add))
                    link(V.tensor_copy(tmp[:, 0:1], cnt[:, EC - 1:EC]))
                    if o == 0:
                        link(V.tensor_tensor_scan(wsum[:, 0:EC], go_on[0][:, :], weight[:, :], 0.0, ALU.mult, ALU.add))
                        V.tensor_copy(tmp[:, 1:2], wsum[:, EC - 1:EC]).then_inc(s_tails, 1)
                    else:
                        V.tensor_copy(tmp[:, 1:2], cnt[:, EC - 1:EC]).then_inc(s_tails, 1)
                    dve.wait_ge(s_st0, o + 1)
                    link(V.tensor_copy(start[:, :], psc[:, 0:2]))
                    link(V.tensor_tensor_scan(cnt[:, 0:EC], whole[o][:, :], ones_e[:, :], start[:, 0:1], ALU.mult, ALU.add))
                    link(V.tensor_tensor(tmp[:, 0:EC], cnt[:, 0:EC], leadend[o][:, :], ALU.mult))
                    link(V.tensor_reduce(cnt[:, EC:EC + 1], tmp[:, 0:EC], AX_X, ALU.add))
                    if o == 0:
                        link(V.tensor_tensor_scan(wsum[:, 0:EC], whole[0][:, :], weight[:, :], start[:, 1:2], ALU.mult, ALU.add))
                        link(V.tensor_tensor(tmp[:, 0:EC], wsum[:, 0:EC], leadend[0][:, :], ALU.mult))
                        link(V.tensor_reduce(wsum[:, EC:EC + 1], tmp[:, 0:EC], AX_X, ALU.add))
                    link(V.tensor_scalar(cnt[:, :], cnt[:, :], 1.0, None, ALU.add))
                    if o == 0:
                        V.reciprocal(scale[0][:, :], cnt[:, :]).then_inc(s_deg, 1)
                        dve.wait_ge(s_deg, 1)
                        V.tensor_copy(start[:, 0:1], cnt[:, 0:1]).then_inc(s_cnt1, 1)
                    else:
                        link(V.reciprocal(inv_deg_dst[:, :], cnt[:, :]))
                        V.tensor_copy(start[:, 0:1], cnt[:, 0:1]).then_inc(s_cnt1, 1)
                        dve.wait_ge(s_sq, 1)
                        V.reciprocal(scale[1][:, :], scale[1][:, :]).then_inc(s_deg, 1)
                dve.wait_ge(s_w3, 48)
                for k, to in ((0, Was), (1, Wad)):
                    for b in range(KB):
                        link(V.tensor_tensor(prod[:, :, :], W3[:, b, :].rearrange("p (h d) -> p h d", d=HD),
                                             att[:, k, :, :], ALU.mult))
                        link(V.tensor_reduce(to[:, b, :], prod[:, :, :], AX_X, ALU.add))

        x1e = dram("x1e", [P, TOTAL * D])
        x2e = dram("x2e", [P, TOTAL * D])
        x3e = dram("x3e", [P, TOTAL * D])
        agg2 = dram("agg2", [P, TOTAL * D])
        h3 = dram("h3", [P, TOTAL * D])

        def edge_buffers(scope, tag, count=5):
            return [sb(f"{name}_{tag}", shape, F32, scope) for name, shape in (
                ("msg", [P, NH, GT, D]), ("own", [P, NH, GT, D]), ("tot", [P, NH, GT, D]), ("tT", [P, 2, 2, KB, QT, P]),
                ("o4", [P, 2, QT, D]))[:count]]

        edge_scope = ctx.enter_context(ExitStack())
        pk = sb("pk", [P, NH, GT, 3], I32)
        lr = sb("lr", [P, D])
        est = sb("est", [P, 2, 4, QT, 6])
        emv = sb("emv", [P, 2, 4, QT, 2])
        esm = sb("esm", [P, 2, 4, 3, QT])
        wslot = sb("wslot", [P, NH, GT])
        W2s = sb("W2s", [P, KB, D])
        shift = sb("shift", [P, D])
        half_neg = sb("half_neg", [P, QT])
        shift_parts = sb("shift_parts", [P, 2, D], BF16)
        ones16 = sb("ones16", [P, P], BF16)
        msg, own, tot, tT, o4 = edge_buffers(edge_scope, "a")
        V, A, T = nc.vector, nc.scalar, nc.tensor

        def gather(pool, table, to, h, u, f, s):
            pool.indirect_dma_start(out=to, out_offset=None, in_=table[:, :],
                                    in_offset=bass.IndirectOffsetOnAxis(ap=pk[:, h, u, f:f + 1], axis=0),
                                    bounds_check=N - 1, oob_is_err=False).then_inc(s, 16)

        def scatter_rows(pool, table, h, n, s):
            for u in range(n):
                pool.indirect_dma_start(out=table[:, :], out_offset=bass.IndirectOffsetOnAxis(ap=pk[:, h, u, 2:3], axis=0),
                                        in_=own[:, h, u, :], in_offset=None, bounds_check=N - 1,
                                        oob_is_err=False).then_inc(s, 16)

        def indices(pool, o, g, s_pk, s_go):
            n = group_tiles(g)
            pool.tensor_copy(pk[:, slot(g), 0:n, :], pack[o][:, bass.ds(group_tile0(g), n), :]).then_inc(s_pk, 1)
            pool.wait_ge(s_pk, ev(g, 1, 1))
            pool.sem_inc(s_go, 1)

        def transposed(q, k, of, to, s):
            for j in range(ntiles(q)):
                for b in range(KB):
                    last = T.transpose(to[:, b, j, :], of[:, half(q), q[1] % 2 * 4 + j, b * P:(b + 1) * P], ident[:, :])
            last.then_inc(s, 1)

        def product(q, k, weights, to, s):
            for j in range(ntiles(q)):
                for b in range(KB):
                    last = T.matmul(to[:, j, :], tT[:, q[1] % 2, k, b, j, :], weights[:, b, :],
                                    start=(b == 0), stop=(b == KB - 1))
            last.then_inc(s, 1)

        def accumulate(q, o, carried, s_ready, ready, s_acc, s_lr, s_fix):
            n, h, j0, t0 = ntiles(q), half(q), q[1] % 2 * 4, tile0(q)
            if is_fix(q):
                V.wait_ge(s_fix, 1)
                if s_lr is None:
                    V.tensor_copy(msg[:, 0, 0, :], carried).then_inc(s_acc, 1)
                    return
                V.wait_ge(s_lr, EC)
                V.tensor_tensor(msg[:, 0, 0, :], carried, lr[:, :], ALU.add).then_inc(s_acc, 1)
                return
            V.wait_ge(s_ready, ready)
            for j in range(n + 1):
                if j < n and not (q[0] is None and t0 + j == 0):
                    before_it = msg[:, h, j0 + j - 1, :] if j0 + j else msg[:, (h - 1) % NH, GT - 1, :]
                    wait(V, s_acc, t0 + (j - 1))
                    V.scalar_tensor_tensor(out=msg[:, h, j0 + j, :], in0=before_it, scalar=go_on[o][:, bass.ds(t0 + j, 1)],
                                           in1=msg[:, h, j0 + j, :], op0=ALU.mult, op1=ALU.add).then_inc(s_acc, 1)
                if j and s_lr is not None:
                    if j == n:
                        V.wait_ge(s_acc, t0 + (n - 1))
                    V.wait_ge(s_lr, t0 + j)
                    V.scalar_tensor_tensor(out=lr[:, :], in0=msg[:, h, j0 + j - 1, :], scalar=leadend[o][:, bass.ds(t0 + (j - 1), 1)],
                                           in1=lr[:, :], op0=ALU.mult, op1=ALU.add).then_inc(s_lr, 1)

        def statistics(l, q, of, s_sum, s_bn, s_go, s_mv):
            n, k = ntiles(q), q[1] % 4
            V.wait_ge(s_sum, ev(q, 1, 1))
            for j in range(n):
                last = V.bn_stats(est[:, l, k, j, :], of(q, j))
            last.then_inc(s_bn, 1)
            V.wait_ge(s_bn, ev(q, 1, 1))
            V.sem_inc(s_go, 1)
            for j in range(n):
                last = V.bn_aggr(emv[:, l, k, j, :], est[:, l, k, j, :])
            last.then_inc(s_mv, 1)

        def deviation(l, q, s_mv, s_sd):
            n, k = ntiles(q), q[1] % 4
            A.wait_ge(s_mv, ev(q, 1, 1))
            A.activation(esm[:, l, k, 0, 0:n], emv[:, l, k, 0:n, 1], ACT.Sqrt, bias=eps[:, :]).then_inc(s_sd, 1)

        def reciprocals(l, q, s_sd, s_rs, s_nm):
            n, k = ntiles(q), q[1] % 4
            V.wait_ge(s_sd, ev(q, 1, 1))
            V.reciprocal(esm[:, l, k, 1, 0:n], esm[:, l, k, 0, 0:n]).then_inc(s_rs, 1)
            V.wait_ge(s_rs, ev(q, 1, 1))
            V.scalar_tensor_tensor(out=esm[:, l, k, 2, 0:n], in0=emv[:, l, k, 0:n, 0], scalar=-1.0,
                                   in1=esm[:, l, k, 1, 0:n], op0=ALU.mult, op1=ALU.mult).then_inc(s_nm, 1)

        def normalise(l, q, of, s_nm, s_norm):
            k = q[1] % 4
            A.wait_ge(s_nm, ev(q, 1, 1))
            for j in range(ntiles(q)):
                last = A.activation(of(q, j), of(q, j), ACT.Identity, bias=esm[:, l, k, 2, j:j + 1],
                                    scale=esm[:, l, k, 1, j:j + 1])
            last.then_inc(s_norm, 1)

        def own_row(q, j):
            return own[:, half(q), q[1] % 2 * 4 + j, :]

        def o4_row(q, j):
            return o4[:, q[1] % 2, j, :]

        def chunk_of(a, q):
            j0 = q[1] % 2 * 4
            return a[:, half(q), j0:j0 + ntiles(q), :]

        def tiles_of(table, q, n=None):
            t = tile0(q)
            n = n or ntiles(q)
            return table[:, bass.ds(t * D, n * D)]

        def store(sp, table, of, q, s_from, s_go, s_to):
            sp.wait_ge(s_from, ev(q, 1, 1))
            sp.sem_inc(s_go, 1)
            sp.dma_start(tiles_of(table, q), chunk_of(of, q).rearrange("p n d -> p (n d)")).then_inc(s_to, 16)

        def stored(q, per_group=32):
            c = per_group * (q[1] // CB)
            return c if q[0] is None else q[0] * per_group + c

        def over(v, n):
            return v.unsqueeze(1).broadcast_to([P, n, D])

        with phase() as scope:
            psT = [pb(f"psT{k}", [P, KB, QT, P], F32, scope) for k in "AB"]
            psY = [pb(f"psY{k}", [P, QT, D], F32, scope) for k in "AB"]
            psF = psT[0][:, 0, 0:2, :].rearrange("p a b -> p (a b)")
            (s_pk, s_go, s_vgo, s_spgo, s_scaled, s_acc, s_lr, s_fix, s_tot, s_t, s_tc, s_y, s_add, s_bn, s_mv, s_sd, s_rs,
             s_nm, s_norm) = (sem(f"e0_{n}") for n in (
                "pk", "go", "vgo", "spgo", "scaled", "acc", "lr", "fix", "tot", "t", "tc", "y", "add", "bn", "mv", "sd",
                "rs", "nm", "norm"))
            s_g = [sem(f"e0_g{k}") for k in range(NH)]
            s_sc = [sem(f"e0_sc{k}") for k in range(NH)]
            s_lin = [sem(f"e0_lin{k}") for k in range(NH)]
            block = scope.enter_context(nc.Block())

            @block.gpsimd
            def _(pool):
                def step(g):
                    n, h = group_tiles(g), slot(g)
                    if inside(g, 0, NG):
                        wait(pool, s_sc[h], nth(g, 16 * GT))
                        wait(pool, s_lin[h], nth(g, 32))
                        wait(pool, s_acc, ev(g, GT, 1 - (NH - 1) * GT))
                        indices(pool, 0, g, s_pk, s_go)
                        for u in range(n):
                            if n == GT:
                                gather(pool, x, msg[:, h, u, :], h, u, 0, s_g[h])
                                gather(pool, inv_deg_src, wslot[:, h, u:u + 1], h, u, 0, s_g[h])
                            gather(pool, x, own[:, h, u, :], h, u, 1, s_g[h])
                    b = sh(g, -3)
                    if inside(b, 0, NG):
                        pool.wait_ge(s_norm, FIX + 1 if group_tiles(b) == 1 else ev(b, 2, 2))
                        pool.sem_inc(s_go, 1)
                        scatter_rows(pool, x1, slot(b), group_tiles(b), s_sc[slot(b)])

                groups(pool, step, NG + 3)
                for k in range(NH):
                    pool.wait_ge(s_sc[k], 16 * (GI * GT + (k == 0)))

            def arrived(q):
                return 16 * 3 * GI * GT + 16 if is_fix(q) else landed(q, 3)

            @block.scalar
            def _(act):
                def scale_rows(q):
                    act.wait_ge(s_g[half(q)], arrived(q))
                    for j in range(ntiles(q)):
                        jj = q[1] % 2 * 4 + j
                        last = A.activation(msg[:, half(q), jj, :], msg[:, half(q), jj, :], ACT.Copy,
                                            scale=wslot[:, half(q), jj:jj + 1])
                    last.then_inc(s_scaled, 1)

                def step(q):
                    if inside(sh(q, 1), 0, FIX - 1):
                        scale_rows(sh(q, 1))
                    if inside(q, 0, FIX):
                        n = ntiles(q)
                        act.wait_ge(s_t, ev(q, 1, 1))
                        wait(act, s_y, ev(q, 1, -1))
                        A.activation(tT[:, q[1] % 2, 0, :, 0:n, :], psT[q[1] % 2][:, :, 0:n, :], ACT.Copy).then_inc(s_tc, 1)
                    b, c = sh(q, -2), sh(q, -3)
                    if inside(b, 0, FIX):
                        deviation(0, b, s_mv, s_sd)
                    if inside(c, 0, FIX):
                        normalise(0, c, own_row, s_nm, s_norm)

                scale_rows((None, 0, CB))
                chunks_ahead(act, step, FIX + 3)

            @block.tensor
            def _(pe):
                def step(q):
                    if inside(q, 0, FIX):
                        if is_fix(q):
                            pe.wait_ge(s_acc, EC - 1)
                            pe.wait_ge(s_tc, FIX - 1)
                            T.matmul(psF, feeds[0][:, :], msg[:, NH - 1, GT - 1, :], start=True, stop=True).then_inc(s_fix, 1)
                        pe.wait_ge(s_tot, ev(q, 1, 1))
                        wait(pe, s_tc, ev(q, 1, -1))
                        transposed(q, 0, tot, psT[q[1] % 2], s_t)
                    b = sh(q, -1)
                    if inside(b, 0, FIX):
                        pe.wait_ge(s_tc, ev(b, 1, 1))
                        wait(pe, s_add, ev(b, 1, -1))
                        product(b, 0, W0, psY[b[1] % 2], s_y)

                chunks(pe, step, FIX + 1)

            @block.vector
            def _(dve):
                def step(q):
                    if inside(q, 0, FIX):
                        n, h, j0, t0 = ntiles(q), half(q), q[1] % 2 * 4, tile0(q)
                        accumulate(q, 0, psF, s_scaled, ev(q, 1, 1), s_acc, s_lr, s_fix)
                        if n == 1:
                            dve.wait_ge(s_g[0], arrived(q))
                        wait(dve, s_acc, t0 + (n - 1))
                        wait(dve, s_t, ev(q, 1, 1 - CB))
                        for j in range(n):
                            last = V.scalar_tensor_tensor(out=tot[:, h, j0 + j, :], in0=own[:, h, j0 + j, :],
                                                          scalar=scale[0][:, bass.ds(t0 + j, 1)], in1=msg[:, h, j0 + j, :],
                                                          op0=ALU.mult, op1=ALU.add)
                        last.then_inc(s_tot, 1)
                    b, c = sh(q, -2), sh(q, -3)
                    if inside(c, 0, FIX):
                        reciprocals(0, c, s_sd, s_rs, s_nm)
                    if inside(b, 0, FIX):
                        n = ntiles(b)
                        dve.wait_ge(s_y, ev(b, 1, 1))
                        V.tensor_tensor(chunk_of(own, b), psY[b[1] % 2][:, 0:n, :], chunk_of(own, b), ALU.add).then_inc(s_add, 1)
                        statistics(0, b, own_row, s_add, s_bn, s_vgo, s_mv)

                V.memset(lr[:, :], 0.0).then_inc(s_lr, 1)
                chunks(dve, step, FIX + 3)

            @block.sync
            def _(sp):
                chunks(sp, lambda q: store(sp, x1e, own, q, s_norm, s_spgo, s_lin[half(q)]), FIX)
                for k in range(NH):
                    sp.wait_ge(s_lin[k], 32 * GI + 16 * (k == 0))

        with phase() as scope:
            psT = [pb(f"e1_psT{k}", [P, KB, QT, P], F32, scope) for k in "AB"]
            psY = [pb(f"e1_psY{k}", [P, QT, D], F32, scope) for k in "AB"]
            psF = psT[0][:, 0, 0:2, :].rearrange("p a b -> p (a b)")
            (s_pk, s_go, s_vgo, s_spgo, s_scaled, s_acc, s_lr, s_fix, s_t, s_tc, s_y, s_oa, s_take, s_sum, s_plus) = (
                sem(f"e1_{n}") for n in ("pk", "go", "vgo", "spgo", "scaled", "acc", "lr", "fix", "t", "tc", "y", "oa",
                                         "take", "sum", "plus"))
            s_gb = [sem(f"e1_gb{k}") for k in range(3)]
            s_bn, s_mv, s_sd, s_rs, s_nm, s_norm = ([sem(f"e1_{n}{l}") for l in range(2)] for n in (
                "bn", "mv", "sd", "rs", "nm", "norm"))
            s_g = [sem(f"e1_g{k}") for k in range(NH)]
            s_dslot = sem("e1_dslot")
            s_dg = [sem(f"e1_dg{k}") for k in range(NH)]
            dst_slot = sb("dst_slot", [P, NH, GT], I32, scope)
            s_own = [sem(f"e1_own{k}") for k in range(NH)]
            s_sc = [sem(f"e1_sc{k}") for k in range(NH)]
            block = scope.enter_context(nc.Block())

            @block.sync
            def _(sp):
                def step(g):
                    n, h = group_tiles(g), slot(g)
                    wait(sp, s_sc[h], nth(g, 16 * GT))
                    sp.sem_inc(s_spgo, 1)
                    sp.dma_start(own[:, h, 0:n, :].rearrange("p n d -> p (n d)"),
                                 x1e[:, bass.ds(ev(g, GT * D), n * D)]).then_inc(s_own[h], 16)

                groups(sp, step, NG)

            @block.gpsimd
            def _(pool):
                def step(g):
                    n, h = group_tiles(g), slot(g)
                    if inside(g, 0, NG):
                        wait(pool, s_sc[h], nth(g, 16 * GT))
                        wait(pool, s_acc, ev(g, GT, 1 - (NH - 1) * GT))
                        wait(pool, s_t, ev(g, 2, 2 - CB))
                        indices(pool, 0, g, s_pk, s_go)
                        wait(pool, s_dg[h], nth(g, 16 * GT))
                        pool.tensor_copy(dst_slot[:, h, 0:n], pack[1][:, bass.ds(group_tile0(g), n), 2])
                        pool.tensor_copy(wslot[:, h, 0:n], scale[1][:, bass.ds(group_tile0(g), n)]).then_inc(s_dslot, 1)
                        if n == GT:
                            for u in range(n):
                                gather(pool, x1, msg[:, h, u, :], h, u, 0, s_g[h])
                        pool.wait_ge(s_dslot, ev(g, 1, 1))
                        pool.sem_inc(s_go, 1)
                        for u in range(n):
                            pool.indirect_dma_start(
                                out=dinv_dst[:, :], out_offset=bass.IndirectOffsetOnAxis(ap=dst_slot[:, h, u:u + 1], axis=0),
                                in_=wslot[:, h, u:u + 1], in_offset=None, bounds_check=N - 1,
                                oob_is_err=False).then_inc(s_dg[h], 16)
                    b = sh(g, -3)
                    if inside(b, 0, NG):
                        pool.wait_ge(s_norm[1], FIX + 1 if group_tiles(b) == 1 else ev(b, 2, 2))
                        pool.sem_inc(s_go, 1)
                        scatter_rows(pool, x2, slot(b), group_tiles(b), s_sc[slot(b)])

                groups(pool, step, NG + 3)
                for k in range(NH):
                    pool.wait_ge(s_sc[k], 16 * (GI * GT + (k == 0)))
                    pool.wait_ge(s_dg[k], 16 * (GI * GT + (k == 0)))

            @block.scalar
            def _(act):
                def scale_rows(q):
                    act.wait_ge(s_g[half(q)], landed(q, 1))
                    t0 = tile0(q)
                    for j in range(ntiles(q)):
                        jj = q[1] % 2 * 4 + j
                        last = A.activation(msg[:, half(q), jj, :], msg[:, half(q), jj, :], ACT.Copy,
                                            scale=weight[:, bass.ds(t0 + j, 1)])
                    last.then_inc(s_scaled, 1)

                def step(q):
                    b, c, d = sh(q, -2), sh(q, -3), sh(q, -4)
                    if inside(sh(q, 1), 0, FIX - 1):
                        scale_rows(sh(q, 1))
                    if inside(c, 0, FIX):
                        normalise(0, c, o4_row, s_nm[0], s_norm[0])
                    if inside(d, 0, FIX):
                        normalise(1, d, own_row, s_nm[1], s_norm[1])
                    if inside(q, 0, FIX):
                        n = ntiles(q)
                        act.wait_ge(s_t, ev(q, 1, 1))
                        wait(act, s_y, ev(q, 1, -1))
                        for k in range(2):
                            last = A.activation(tT[:, q[1] % 2, k, :, 0:n, :], psT[k][:, :, 0:n, :], ACT.Copy)
                        last.then_inc(s_tc, 1)
                    if inside(b, 0, FIX):
                        deviation(0, b, s_mv[0], s_sd[0])
                    if inside(c, 0, FIX):
                        deviation(1, c, s_mv[1], s_sd[1])

                scale_rows((None, 0, CB))
                chunks_ahead(act, step, FIX + 4)

            @block.tensor
            def _(pe):
                def step(q):
                    if inside(q, 0, FIX):
                        if is_fix(q):
                            pe.wait_ge(s_acc, EC - 1)
                            pe.wait_ge(s_tc, FIX)
                            T.matmul(psF, feeds[0][:, :], msg[:, NH - 1, GT - 1, :], start=True, stop=True).then_inc(s_fix, 1)
                        pe.wait_ge(s_acc, tile0(q) + (ntiles(q) - 1))
                        pe.wait_ge(s_own[half(q)], loads(q))
                        wait(pe, s_tc, ev(q))
                        transposed(q, 0, msg, psT[0], s_gb[0])
                        transposed(q, 1, own, psT[1], s_t)
                    b = sh(q, -1)
                    if inside(b, 0, FIX):
                        pe.wait_ge(s_tc, ev(b, 1, 1))
                        wait(pe, s_take, ev(b))
                        product(b, 0, W1T, psY[0], s_gb[1])
                        product(b, 1, WrI, psY[1], s_y)

                chunks(pe, step, FIX + 1)

            @block.vector
            def _(dve):
                def step(q):
                    b, c, d = sh(q, -2), sh(q, -3), sh(q, -4)
                    if inside(q, 0, FIX):
                        accumulate(q, 0, psF, s_scaled, ev(q, 1, 1), s_acc, s_lr, s_fix)
                    if inside(c, 0, FIX):
                        reciprocals(0, c, s_sd[0], s_rs[0], s_nm[0])
                    if inside(d, 0, FIX):
                        reciprocals(1, d, s_sd[1], s_rs[1], s_nm[1])
                    if inside(b, 0, FIX):
                        n, t0 = ntiles(b), tile0(b)
                        dve.wait_ge(s_y, ev(b, 1, 1))
                        wait(dve, s_sum, ev(b, 1, -1))
                        for j in range(n):
                            last = V.scalar_tensor_tensor(out=o4[:, b[1] % 2, j, :], in0=B1, scalar=wsum[:, bass.ds(t0 + j, 1)],
                                                          in1=psY[0][:, j, :], op0=ALU.mult, op1=ALU.add)
                        last.then_inc(s_oa, 1)
                        V.tensor_tensor(chunk_of(own, b), psY[1][:, 0:n, :], over(BR, n), ALU.add).then_inc(s_take, 1)
                        statistics(0, b, o4_row, s_oa, s_bn[0], s_vgo, s_mv[0])
                    if inside(c, 0, FIX):
                        n = ntiles(c)
                        oc = o4[:, c[1] % 2, 0:n, :]
                        dve.wait_ge(s_norm[0], ev(c, 1, 1))
                        V.tensor_tensor(oc, oc, over(G1, n), ALU.mult).then_inc(s_plus, 1)
                        dve.wait_ge(s_plus, ev(c, 2, 1))
                        V.tensor_tensor(oc, oc, over(BE1, n), ALU.add).then_inc(s_plus, 1)
                        dve.wait_ge(s_plus, ev(c, 2, 2))
                        V.scalar_tensor_tensor(out=chunk_of(own, c), in0=oc, scalar=0.0, in1=chunk_of(own, c), op0=ALU.max,
                                               op1=ALU.add).then_inc(s_sum, 1)
                        statistics(1, c, own_row, s_sum, s_bn[1], s_vgo, s_mv[1])

                V.memset(lr[:, :], 0.0).then_inc(s_lr, 1)
                chunks(dve, step, FIX + 4)

        DG = D + 4
        gram_scope = ctx.enter_context(ExitStack())
        psG = pb("psG", [P, KB, 512], F32, gram_scope)

        edge_scope.close()
        edge_scope = ctx.enter_context(ExitStack())
        msg, own, tot = edge_buffers(edge_scope, "b", 3)
        QR = 4

        def qslot(q, j):
            return (q[1] % CB // 2 * GT + q[1] % 2 * 4 + j) % QR

        def qloads(q, j):
            i, c, _ = q
            t = c // 2 * GT + c % 2 * 4 + j
            n = t // QR + (1 if t % QR else 0)
            return 16 * n if i is None else i * (16 * NH * GT // QR) + 16 * n

        def quad_rows(q):
            return TAIL if is_fix(q) else P

        def quads(q):
            return [j for j in range(ntiles(q)) if not (q[0] is None and tile0(q) + j == 0)]

        def gram(of, by, **flags):
            T.matmul(psG[:, 0, 0:D + 1], of[:, 0:P], by[:, 0:D + 1], **flags)
            return T.matmul(psG[:, 1, P:D + 1], of[:, P:D], by[:, P:D + 1], **flags)

        with phase() as scope:
            xg = sb("xg", [P, QR, QT, DG], F32, scope)
            xm = sb("xm", [P, QR, QT, D], F32, scope)
            free = sb("free", [P, NPP + QT], F32, scope)
            s_fr, s_mask, s_mul, s_qgram = (sem(f"g_{n}") for n in ("fr", "mask", "mul", "gram"))
            s_x = [sem(f"g_x{k}") for k in range(QR)]
            tw = tot
            tot1 = sb("tot1", [P, NH, GT, DG], F32, scope)
            psF = pb("psF2", [P, D], F32, scope)[:, :]
            s_pk, s_go, s_spgo, s_scaled, s_acc, s_lr, s_fix, s_one2, s_part, s_tot, s_val, s_gram = (
                sem(f"e2_{n}") for n in ("pk", "go", "spgo", "scaled", "acc", "lr", "fix", "one", "part", "tot", "val", "gram"))
            s_g = [sem(f"e2_g{k}") for k in range(NH)]
            s_lin = [sem(f"e2_lin{k}") for k in range(NH)]
            block = scope.enter_context(nc.Block())

            def arrived2(q):
                return 16 * 3 * GI * GT + 16 if is_fix(q) else landed(q, 3)

            @block.gpsimd
            def _(pool):
                def step(g):
                    n, h = group_tiles(g), slot(g)
                    wait(pool, s_lin[h], nth(g, 64))
                    wait(pool, s_acc, ev(g, GT, 1 - (NH - 1) * GT))
                    wait(pool, s_tot, ev(g, 2, 2 - CB))
                    indices(pool, 1, g, s_pk, s_go)
                    for u in range(n):
                        if n == GT:
                            gather(pool, x2, msg[:, h, u, :], h, u, 0, s_g[h])
                            gather(pool, dinv_dst, wslot[:, h, u:u + 1], h, u, 0, s_g[h])
                        gather(pool, x2, own[:, h, u, :], h, u, 1, s_g[h])

                groups(pool, step, NG)

            @block.scalar
            def _(act):
                def scale_rows(q):
                    n, h, j0, t0 = ntiles(q), half(q), q[1] % 2 * 4, tile0(q)
                    act.wait_ge(s_g[h], arrived2(q))
                    if not is_fix(q):
                        for j in range(n):
                            last = A.activation(msg[:, h, j0 + j, :], msg[:, h, j0 + j, :], ACT.Copy,
                                                scale=wslot[:, h, j0 + j:j0 + j + 1])
                        last.then_inc(s_scaled, 1)
                    wait(act, s_gram, ev(q, 1, 1 - CB))
                    for j in range(n):
                        last = A.activation(tw[:, h, j0 + j, :], own[:, h, j0 + j, :], ACT.Copy,
                                            scale=inv_deg_dst[:, bass.ds(t0 + j, 1)])
                    last.then_inc(s_part, 1)

                def step(q):
                    if inside(sh(q, 1), 0, FIX):
                        scale_rows(sh(q, 1))
                    if inside(q, 0, FIX):
                        n, h, j0, t0 = ntiles(q), half(q), q[1] % 2 * 4, tile0(q)
                        act.wait_ge(s_tot, ev(q, 1, 1))
                        for j in range(n):
                            last = A.activation(tw[:, h, j0 + j, :], tot1[:, h, j0 + j, 0:D], ACT.Copy,
                                                scale=valid[:, bass.ds(t0 + j, 1)])
                        last.then_inc(s_val, 1)

                scale_rows((None, 0, CB))
                chunks_ahead(act, step, FIX)

            @block.vector
            def _(dve):
                def step(q):
                    n, h, j0, t0 = ntiles(q), half(q), q[1] % 2 * 4, tile0(q)
                    r = quad_rows(q)
                    for j in quads(q):
                        s = qslot(q, j)
                        dve.wait_ge(s_x[s], qloads(q, j))
                        wait(dve, s_qgram, t0 + (j - QR))
                        V.tensor_tensor(xm[0:r, s, :, :], xg[0:r, s, :, 0:D],
                                        free[0:r, bass.ds((t0 + (j - 1)) * QT, QT)].unsqueeze(2).broadcast_to([r, QT, D]),
                                        ALU.mult).then_inc(s_mul, 1)
                    accumulate(q, 1, psF, s_scaled, ev(q, 1, 1), s_acc, s_lr, s_fix)
                    wait(dve, s_acc, t0 + (n - 1))
                    dve.wait_ge(s_part, ev(q, 1, 1))
                    wait(dve, s_gram, ev(q, 1, 1 - CB))
                    wait(dve, s_lin[h], stored(q, 64))
                    for j in range(n):
                        last = V.scalar_tensor_tensor(out=tot1[:, h, j0 + j, 0:D], in0=msg[:, h, j0 + j, :],
                                                      scalar=scale[1][:, bass.ds(t0 + j, 1)], in1=tw[:, h, j0 + j, :],
                                                      op0=ALU.mult, op1=ALU.add)
                    last.then_inc(s_tot, 1)

                V.memset(tot1[:, :, :, D:DG], 1.0).then_inc(s_one2, 1)
                V.memset(xg[:, :, :, D:DG], 1.0).then_inc(s_one2, 1)
                dve.wait_ge(s_fr, 32)
                V.tensor_scalar(free[:, 0:NPP], free[:, 0:NPP], 1.0, None, ALU.is_equal).then_inc(s_mask, 1)
                V.tensor_scalar(free[0:TAIL, NPP:NPP + QT], free[0:TAIL, NPP:NPP + QT], 1.0, None, ALU.is_equal).then_inc(s_mask, 1)
                dve.wait_ge(s_mask, 2)
                V.memset(lr[:, :], 0.0).then_inc(s_lr, 1)
                chunks(dve, step, FIX)

            @block.tensor
            def _(pe):
                pe.wait_ge(s_one2, 2)

                def step(q):
                    n, h, j0 = ntiles(q), half(q), q[1] % 2 * 4
                    fix = is_fix(q)
                    r = quad_rows(q)
                    for t in quads(q):
                        s = qslot(q, t)
                        pe.wait_ge(s_mul, tile0(q) + t)
                        for j in range(QT):
                            last = gram(xm[0:r, s, j, :], xg[0:r, s, j, :],
                                        start=q[0] is None and q[1] == 0 and t == 1 and j == 0, stop=False)
                        last.then_inc(s_qgram, 1)
                    if fix:
                        pe.wait_ge(s_acc, EC - 1)
                        T.matmul(psF, feeds[1][:, :], msg[:, NH - 1, GT - 1, :], start=True, stop=True).then_inc(s_fix, 1)
                    pe.wait_ge(s_val, ev(q, 1, 1))
                    for j in range(n):
                        last = gram(tw[:, h, j0 + j, :], tot1[:, h, j0 + j, :], start=False, stop=fix)
                    last.then_inc(s_gram, 1)

                chunks(pe, step, FIX)

            @block.sync
            def _(sp):
                def load_quads(q):
                    r = quad_rows(q)
                    for j in quads(q):
                        wait(sp, s_qgram, tile0(q) + (j - QR))
                        sp.sem_inc(s_spgo, 1)
                        table = (x2[P * NPP:N, :].rearrange("(p j) d -> p j d", j=QT) if is_fix(q) else
                                 x2[0:P * NPP, :].rearrange("(p n) d -> p n d", n=NPP)[:, bass.ds((tile0(q) + (j - 1)) * QT, QT), :])
                        sp.dma_start(xg[0:r, qslot(q, j), :, 0:D], table).then_inc(s_x[qslot(q, j)], 16)

                def step(q):
                    if inside(sh(q, 1), 0, FIX):
                        load_quads(sh(q, 1))
                    n, h, j0 = ntiles(q), half(q), q[1] % 2 * 4
                    sp.wait_ge(s_tot, ev(q, 1, 1))
                    sp.sem_inc(s_spgo, 1)
                    sp.dma_start(tiles_of(agg2, q).rearrange("p (n d) -> p n d", d=D), tot1[:, h, j0:j0 + n, 0:D]).then_inc(s_lin[h], 16)
                    sp.dma_start(tiles_of(x2e, q), chunk_of(own, q).rearrange("p n d -> p (n d)")).then_inc(s_lin[h], 16)

                sp.dma_start(free[:, 0:NPP], dinv_dst[0:P * NPP, 0].rearrange("(p c) -> p c", p=P)).then_inc(s_fr, 16)
                sp.dma_start(free[0:TAIL, NPP:NPP + QT], dinv_dst[P * NPP:N, 0].rearrange("(p c) -> p c", p=TAIL)).then_inc(s_fr, 16)
                load_quads((None, 0, CB))
                chunks_ahead(sp, step, FIX)
                for k in range(NH):
                    sp.wait_ge(s_lin[k], 64 * GI + 32 * (k == 0))

        edge_scope.close()

        with phase() as scope:
            part = [sb(f"part{k}", [P, D], BF16, scope) for k in range(3)]
            rest = sb("rest", [P, D], F32, scope)
            grams = sb("grams", [P, KB, D + 1], F32, scope)
            wv = sb("wv", [P, KB, D], F32, scope)
            ws = sb("ws", [P, KB, D], F32, scope)
            mean = sb("mean", [P, D], F32, scope)
            var = sb("var", [P, D], F32, scope)
            tmp2 = sb("tmp2", [P, D], F32, scope)
            psV = pb("psV", [P, KB, D], F32, scope)
            psX = pb("psX", [P, P], F32, scope)
            psM = pb("psM", [P, 2, D], F32, scope)
            s_c, s_gr, s_tr, s_v1, s_wv, s_mo, s_sd2, s_vr = (sem(f"s2_{n}") for n in ("c", "gr", "tr", "v", "wv", "mo", "sd", "vr"))
            block = scope.enter_context(nc.Block())

            @block.tensor
            def _(pe):
                pe.wait_ge(s_gr, 1)
                T.transpose(psX[:, :], grams[:, 0, P:D], ident[:, :]).then_inc(s_tr, 1)
                pe.wait_ge(s_gr, 2)
                for b in range(KB):
                    for a in range(KB):
                        last = T.matmul(psV[:, b, :], grams[:, a, b * P:(b + 1) * P], W2[:, a, :], start=(a == 0), stop=(a == KB - 1))
                last.then_inc(s_v1, 1)
                pe.wait_ge(s_wv, 1)
                for k, of in enumerate((wv, ws)):
                    for b in range(KB):
                        last = T.matmul(psM[:, k, :], ones[:, :], of[:, b, :], start=(b == 0), stop=(b == KB - 1))
                last.then_inc(s_mo, 1)

            @block.scalar
            def _(act):
                act.wait_ge(s_vr, 1)
                A.activation(var[:, :], var[:, :], ACT.Sqrt, bias=eps[:, :]).then_inc(s_sd2, 1)

            @block.vector
            def _(dve):
                chain = [0]

                def link(ins):
                    chain[0] += 1
                    ins.then_inc(s_c, 1)
                    dve.wait_ge(s_c, chain[0])

                V.tensor_copy(grams[:, 0, :], psG[:, 0, 0:D + 1])
                V.tensor_copy(grams[:, 1, P:D + 1], psG[:, 1, P:D + 1]).then_inc(s_gr, 1)
                dve.wait_ge(s_tr, 1)
                V.tensor_copy(grams[:, 1, 0:P], psX[:, :]).then_inc(s_gr, 1)
                dve.wait_ge(s_gr, 2)
                for b in range(KB):
                    link(V.tensor_scalar(ws[:, b, :], W2[:, b, :], grams[:, b, D:D + 1], None, ALU.mult))
                dve.wait_ge(s_v1, 1)
                V.tensor_tensor(wv[:, :, :], psV[:, :, :], W2[:, :, :], ALU.mult).then_inc(s_wv, 1)
                dve.wait_ge(s_mo, 1)
                link(V.tensor_scalar(mean[:, :], psM[:, 1, :], 1.0 / N, None, ALU.mult))
                link(V.tensor_tensor(tmp2[:, :], mean[:, :], mean[:, :], ALU.mult))
                V.scalar_tensor_tensor(out=var[:, :], in0=psM[:, 0, :], scalar=1.0 / N, in1=tmp2[:, :],
                                       op0=ALU.mult, op1=ALU.subtract).then_inc(s_vr, 1)
                link(V.tensor_tensor(mean[:, :], mean[:, :], B2, ALU.add))
                dve.wait_ge(s_sd2, 1)
                link(V.reciprocal(var[:, :], var[:, :]))
                link(V.tensor_tensor(var[:, :], var[:, :], G2, ALU.mult))
                link(V.tensor_tensor(tmp2[:, :], B2, mean[:, :], ALU.subtract))
                link(V.tensor_tensor(tmp2[:, :], tmp2[:, :], var[:, :], ALU.mult))
                link(V.tensor_tensor(shift[:, :], tmp2[:, :], BE2, ALU.add))
                link(V.tensor_tensor(W2s[:, :, :], W2[:, :, :], over(var[:, :], KB), ALU.mult))
                link(V.memset(ones16[:, :], 1.0))
                link(V.memset(half_neg[:, :], -0.5))
                link(V.memset(shift_parts[:, :, :], 0.0))
                of = shift
                for k in range(3):
                    link(V.tensor_copy(part[k][:, :], of[:, :]))
                    if k < 2:
                        link(V.tensor_tensor(rest[:, :], of[:, :], part[k][:, :], ALU.subtract))
                        of = rest
                    at = slice(32 * k, 32 * k + 1)
                    for a in range(2):
                        link(V.tensor_copy(shift_parts[at, a, :], part[k][at, :]))
        gram_scope.close()

        R3 = 5
        TURN = (0, 1, 0, 1, 2)
        with phase() as scope:
            xin = sb("p3_xin", [P, R3, QT, D], F32, scope)
            xT = sb("p3_xT", [P, 3, KB, QT, P], F32, scope)
            y2 = sb("p3_y2", [P, R3, QT, D], F32, scope)
            y3 = sb("p3_y3", [P, R3, QT, D], F32, scope)
            small = sb("p3_small", [P, 2, R3, 3, QT], F32, scope)
            st = sb("p3_st", [P, 2, R3, QT, 6], F32, scope)
            mv = sb("p3_mv", [P, 2, R3, QT, 2], F32, scope)
            psT = pb("p3_psT", [P, KB, QT, P], F32, scope)
            psY = [pb(f"p3_psY{k}", [P, QT, D], F32, scope) for k in range(3)]
            s_t, s_tc, s_y, s_th, s_vp, s_pp, s_spg = (sem(f"p3_{n}") for n in ("t", "tc", "y", "th", "vp", "pp", "sp"))
            s_add, s_bn, s_mv, s_ve, s_rs, s_nm, s_norm = ([sem(f"p3_{n}{l}") for l in range(2)] for n in (
                "add", "bn", "mv", "ve", "rs", "nm", "norm"))
            s_x = [sem(f"p3_x{k}") for k in range(R3)]
            s_st3 = [sem(f"p3_st3{k}") for k in range(R3)]
            s_st4 = [sem(f"p3_st4{k}") for k in range(R3)]
            block = scope.enter_context(nc.Block())
            buf3 = (y2, y3)

            @block.sync
            def _(sp):
                def load(q):
                    wait(sp, s_add[0], ev(q, 1, 1 - R3))
                    sp.sem_inc(s_spg, 1)
                    sp.dma_start(xin[0:rows(q), slot(q), :, :].rearrange("p j d -> p (j d)"),
                                 quad_of(x2, q)).then_inc(s_x[slot(q)], 16)

                def store_quad(l, table, q, s_st):
                    sp.wait_ge(s_norm[l], ev(q, 1, 1))
                    sp.sem_inc(s_spg, 1)
                    sp.dma_start(quad_of(table, q),
                                 buf3[l][0:rows(q), slot(q), :, :].rearrange("p j d -> p (j d)")).then_inc(s_st[slot(q)], 16)

                def step(q):
                    if inside(sh(q, 2), 0, NQ):
                        load(sh(q, 2))
                    if inside(sh(q, -4), 0, NQ):
                        store_quad(0, x3, sh(q, -4), s_st3)
                    if inside(sh(q, -6), 0, NQ):
                        store_quad(1, out, sh(q, -6), s_st4)

                load((None, 0, R3))
                load((None, 1, R3))
                steps(sp, step, 0, NQ + 6, ring=R3)
                for c in range(R3):
                    sp.wait_ge(s_st3[c], 16 * len(range(c, NQ + 1, R3)))
                    sp.wait_ge(s_st4[c], 16 * len(range(c, NQ + 1, R3)))

            @block.tensor
            def _(pe):
                def step(q):
                    nxt = sh(q, 1)
                    if inside(nxt, 0, NQ):
                        r, s = rows(nxt), slot(nxt)
                        pe.wait_ge(s_x[s], nth(nxt, 16, 16))
                        wait(pe, s_tc, ev(nxt))
                        for j in range(QT):
                            for b in range(KB):
                                last = T.transpose(psT[:, b, j, 0:r], xin[0:r, s, j, b * P:(b + 1) * P], ident[0:r, 0:r])
                        last.then_inc(s_t, 1)
                    if inside(q, 0, NQ):
                        r, k = rows(q), TURN[slot(q)]
                        pe.wait_ge(s_tc, ev(q, 1, 1))
                        wait(pe, s_th, ev(q, 1, -1))
                        for a in range(QT // 2):
                            T.matmul(psY[k][0:r, 2 * a:2 * a + 2, :], ones16[:, 0:r], shift_parts[:, :, :], start=True, stop=False)
                        for j in range(QT):
                            for b in range(KB):
                                last = T.matmul(psY[k][0:r, j, :], xT[:, k, b, j, 0:r], W2s[:, b, :],
                                                start=False, stop=(b == KB - 1 and j % 2 == 1))
                        last.then_inc(s_y, 1)

                step((None, -1, R3))
                steps(pe, step, 0, NQ, ring=R3)

            @block.scalar
            def _(act):
                def norm(l, q):
                    r, s = rows(q), slot(q)
                    act.wait_ge(s_nm[l], ev(q, 1, 1))
                    for j in range(QT):
                        last = A.activation(buf3[l][0:r, s, j, :], buf3[l][0:r, s, j, :], ACT.Identity,
                                            bias=small[0:r, l, s, 1, j:j + 1], scale=small[0:r, l, s, 0, j:j + 1])
                    last.then_inc(s_norm[l], 1)

                def step(q):
                    nxt, a = sh(q, 1), sh(q, -1)
                    if inside(nxt, 0, NQ):
                        r = rows(nxt)
                        act.wait_ge(s_t, ev(nxt, 1, 1))
                        wait(act, s_y, ev(nxt, 1, -1))
                        A.activation(xT[:, TURN[slot(nxt)], :, :, 0:r], psT[:, :, :, 0:r], ACT.Copy).then_inc(s_tc, 1)
                    if inside(a, 0, NQ):
                        r, s = rows(a), slot(a)
                        act.wait_ge(s_y, ev(a, 1, 1))
                        wait(act, s_st3[s], nth(a, 16))
                        wait(act, s_add[1], ev(a, 1, 1 - R3))
                        A.activation(y2[0:r, s, :, :], psY[TURN[s]][0:r, :, :], ACT.Tanh).then_inc(s_th, 1)
                    if inside(sh(q, -3), 0, NQ):
                        norm(0, sh(q, -3))
                    if inside(sh(q, -5), 0, NQ):
                        norm(1, sh(q, -5))

                step((None, -1, R3))
                steps(act, step, 0, NQ + 5, ring=R3)

            @block.gpsimd
            def _(pool):
                def rsqrt(l, q):
                    r, s = rows(q), slot(q)
                    pool.wait_ge(s_ve[l], ev(q, 1, 1))
                    pool.sem_inc(s_pp, 1)
                    pool.tensor_tensor(small[0:r, l, s, 0, :], small[0:r, l, s, 2, :], half_neg[0:r, :],
                                       ALU.pow).then_inc(s_rs[l], 1)

                def step(q):
                    b = sh(q, -3)
                    if inside(b, 0, NQ):
                        r, s = rows(b), slot(b)
                        at = y3[0:r, s, :, :]
                        wait(pool, s_st4[s], nth(b, 16))
                        pool.sem_inc(s_pp, 1)
                        pool.wait_ge(s_norm[0], ev(b, 1, 1))
                        pool.tensor_tensor(at, y2[0:r, s, :, :], c3[0:r, :].unsqueeze(1).broadcast_to([r, QT, D]),
                                           ALU.add).then_inc(s_add[1], 1)
                    for l, k in ((1, 4), (0, 2)):
                        if inside(sh(q, -k), 0, NQ):
                            rsqrt(l, sh(q, -k))

                steps(pool, step, 0, NQ + 4, ring=R3)

            @block.vector
            def _(dve):
                def partial(l, q):
                    r, s = rows(q), slot(q)
                    dve.wait_ge(s_add[l], ev(q, 1, 1))
                    for j in range(QT):
                        last = V.bn_stats(st[0:r, l, s, j, :], buf3[l][0:r, s, j, :])
                    last.then_inc(s_bn[l], 1)

                def total(l, q):
                    r, s = rows(q), slot(q)
                    dve.wait_ge(s_bn[l], ev(q, 1, 1))
                    dve.sem_inc(s_vp, 1)
                    for j in range(QT):
                        last = V.bn_aggr(mv[0:r, l, s, j, :], st[0:r, l, s, j, :])
                    last.then_inc(s_mv[l], 1)

                def guarded(l, q):
                    r, s = rows(q), slot(q)
                    dve.wait_ge(s_mv[l], ev(q, 1, 1))
                    V.tensor_scalar(small[0:r, l, s, 2, :], mv[0:r, l, s, :, 1], EPS, None, ALU.add).then_inc(s_ve[l], 1)

                def neg_mean(l, q):
                    r, s = rows(q), slot(q)
                    dve.wait_ge(s_rs[l], ev(q, 1, 1))
                    V.scalar_tensor_tensor(out=small[0:r, l, s, 1, :], in0=mv[0:r, l, s, :, 0], scalar=-1.0,
                                           in1=small[0:r, l, s, 0, :], op0=ALU.mult, op1=ALU.mult).then_inc(s_nm[l], 1)

                def step(q):
                    b, c, d, e = (sh(q, -k) for k in (2, 3, 4, 5))
                    if inside(b, 0, NQ):
                        r, s = rows(b), slot(b)
                        dve.wait_ge(s_th, ev(b, 1, 1))
                        V.tensor_tensor(y2[0:r, s, :, :], xin[0:r, s, :, :], y2[0:r, s, :, :], ALU.add).then_inc(s_add[0], 1)
                    if inside(d, 0, NQ):
                        partial(1, d)
                    if inside(c, 0, NQ):
                        neg_mean(0, c)
                    if inside(b, 0, NQ):
                        partial(0, b)
                    if inside(e, 0, NQ):
                        neg_mean(1, e)
                    for part in (total, guarded):
                        for l, which in ((1, d), (0, b)):
                            if inside(which, 0, NQ):
                                part(l, which)

                steps(dve, step, 0, NQ + 5, ring=R3)

        score = sb("score", [P, EC, HEADS])
        attend = sb("attend", [P, EC, HEADS])
        rden = sb("rden", [P, TOTAL, HEADS])
        edge_scope = ctx.enter_context(ExitStack())
        msg, own, tot, tT, o4 = edge_buffers(edge_scope, "c")

        def load_group(sp, g, pairs, s_to, s_go, frees):
            n, h = group_tiles(g), slot(g)
            for s, v in frees:
                wait(sp, s, v)
                sp.sem_inc(s_go, 1)
            for table, to in pairs:
                sp.dma_start(to[:, h, 0:n, :].rearrange("p n d -> p (n d)"),
                             table[:, bass.ds(ev(g, GT * D), n * D)]).then_inc(s_to[h], 16)

        with phase() as scope:
            psT = [pb(f"e2b_psT{k}", [P, KB, QT, P], F32, scope) for k in "AB"]
            psY = [pb(f"e2b_psY{k}", [P, QT, D], F32, scope) for k in "AB"]
            (s_pk, s_go, s_vgo, s_spgo, s_t, s_tc, s_y, s_o, s_th, s_add, s_bn, s_mv, s_sd, s_rs, s_nm, s_norm) = (
                sem(f"e2b_{n}") for n in ("pk", "go", "vgo", "spgo", "t", "tc", "y", "o", "th", "add", "bn", "mv", "sd",
                                          "rs", "nm", "norm"))
            s_in2 = [sem(f"e2b_in{k}") for k in range(NH)]
            s_sc = [sem(f"e2b_sc{k}") for k in range(NH)]
            s_lin = [sem(f"e2b_lin{k}") for k in range(NH)]
            block = scope.enter_context(nc.Block())

            @block.sync
            def _(sp):
                def step(g):
                    if inside(g, 0, NG):
                        h = slot(g)
                        load_group(sp, g, ((agg2, msg), (x2e, own)), s_in2, s_spgo,
                                   ((s_sc[h], nth(g, 16 * GT)), (s_t, ev(g, 2, 2 - CB)), (s_lin[h], nth(g, 32))))
                    b = sh(g, -3)
                    if inside(b, 0, NG):
                        i, c, _ = b
                        for k in range(2 if group_tiles(b) == GT else 1):
                            store(sp, x3e, own, (i, 2 * c + k, CB), s_norm, s_spgo, s_lin[slot(b)])

                groups(sp, step, NG + 3)
                for k in range(NH):
                    sp.wait_ge(s_lin[k], 32 * GI + 16 * (k == 0))

            @block.gpsimd
            def _(pool):
                def powers(q):
                    n, k = ntiles(q), q[1] % 4
                    pool.wait_ge(s_sd, ev(q, 1, 1))
                    pool.sem_inc(s_go, 1)
                    pool.tensor_tensor(esm[:, 0, k, 1, 0:n], esm[:, 0, k, 0, 0:n], half_neg[:, 0:n], ALU.pow).then_inc(s_rs, 1)

                def step(g):
                    if inside(g, 0, NG):
                        i, c, _ = g
                        for k in range(2 if group_tiles(g) == GT else 1):
                            powers((i, 2 * c + k, CB))
                    b = sh(g, -1)
                    if inside(b, 0, NG):
                        wait(pool, s_sc[slot(b)], nth(b, 16 * GT))
                        indices(pool, 1, b, s_pk, s_go)
                        pool.wait_ge(s_norm, FIX + 1 if group_tiles(b) == 1 else ev(b, 2, 2))
                        pool.sem_inc(s_go, 1)
                        scatter_rows(pool, x3, slot(b), group_tiles(b), s_sc[slot(b)])

                groups(pool, step, NG + 1)
                for k in range(NH):
                    pool.wait_ge(s_sc[k], 16 * (GI * GT + (k == 0)))

            @block.tensor
            def _(pe):
                def step(q):
                    if inside(q, 0, FIX):
                        pe.wait_ge(s_in2[half(q)], filled(q, 32))
                        wait(pe, s_tc, ev(q, 1, -1))
                        transposed(q, 0, msg, psT[q[1] % 2], s_t)
                    b = sh(q, -1)
                    if inside(b, 0, FIX):
                        pe.wait_ge(s_tc, ev(b, 1, 1))
                        wait(pe, s_o, ev(b, 1, -1))
                        product(b, 0, W2s, psY[b[1] % 2], s_y)

                chunks(pe, step, FIX + 1)

            @block.scalar
            def _(act):
                def step(q):
                    if inside(q, 0, FIX):
                        n = ntiles(q)
                        act.wait_ge(s_t, ev(q, 1, 1))
                        wait(act, s_y, ev(q, 1, -1))
                        A.activation(tT[:, q[1] % 2, 0, :, 0:n, :], psT[q[1] % 2][:, :, 0:n, :], ACT.Copy).then_inc(s_tc, 1)
                    a, b, c = sh(q, -1), sh(q, -2), sh(q, -3)
                    if inside(a, 0, FIX):
                        n = ntiles(a)
                        act.wait_ge(s_o, ev(a, 1, 1))
                        A.activation(o4[:, a[1] % 2, 0:n, :], o4[:, a[1] % 2, 0:n, :], ACT.Tanh).then_inc(s_th, 1)
                    if inside(c, 0, FIX):
                        normalise(0, c, own_row, s_nm, s_norm)

                chunks(act, step, FIX + 3)

            @block.vector
            def _(dve):
                def step(q):
                    a, b, c = sh(q, -1), sh(q, -2), sh(q, -3)
                    if inside(a, 0, FIX):
                        n = ntiles(a)
                        dve.wait_ge(s_y, ev(a, 1, 1))
                        wait(dve, s_add, ev(a, 1, -1))
                        V.tensor_tensor(o4[:, a[1] % 2, 0:n, :], psY[a[1] % 2][:, 0:n, :], over(shift[:, :], n), ALU.add).then_inc(s_o, 1)
                    if inside(c, 0, FIX):
                        n, k = ntiles(c), c[1] % 4
                        dve.wait_ge(s_rs, ev(c, 1, 1))
                        V.scalar_tensor_tensor(out=esm[:, 0, k, 2, 0:n], in0=emv[:, 0, k, 0:n, 0], scalar=-1.0,
                                               in1=esm[:, 0, k, 1, 0:n], op0=ALU.mult, op1=ALU.mult).then_inc(s_nm, 1)
                    if inside(b, 0, FIX):
                        n = ntiles(b)
                        dve.wait_ge(s_th, ev(b, 1, 1))
                        V.tensor_tensor(chunk_of(own, b), o4[:, b[1] % 2, 0:n, :], chunk_of(own, b), ALU.add).then_inc(s_add, 1)
                        statistics(0, b, own_row, s_add, s_bn, s_vgo, s_mv)
                        k = b[1] % 4
                        dve.wait_ge(s_mv, ev(b, 1, 1))
                        V.tensor_scalar(esm[:, 0, k, 0, 0:n], emv[:, 0, k, 0:n, 1], EPS, None, ALU.add).then_inc(s_sd, 1)

                chunks(dve, step, FIX + 3)

        with phase() as scope:
            psT = [pb(f"e3_psT{k}", [P, KB, QT, P], F32, scope) for k in "AB"]
            psY = pb("e3_psY", [P, QT, D], F32, scope)
            psE = pb("e3_psE", [P, QT, HEADS], F32, scope)
            s_pk, s_go, s_spgo, s_ta, s_t, s_tc, s_ya, s_y, s_h = (sem(f"e3_{n}") for n in (
                "pk", "go", "spgo", "ta", "t", "tc", "ya", "y", "h"))
            s_g = [sem(f"e3_g{k}") for k in range(NH)]
            s_lin = [sem(f"e3_lin{k}") for k in range(NH)]
            block = scope.enter_context(nc.Block())

            @block.gpsimd
            def _(pool):
                def step(g):
                    wait(pool, s_t, ev(g, 2, 2 - CB))
                    indices(pool, 1, g, s_pk, s_go)
                    for u in range(GT):
                        gather(pool, x3, msg[:, slot(g), u, :], slot(g), u, 0, s_g[slot(g)])
                        gather(pool, x3, own[:, slot(g), u, :], slot(g), u, 1, s_g[slot(g)])

                groups(pool, step, NG - 1)

            @block.tensor
            def _(pe):
                def step(q):
                    if inside(q, 0, FIX - 1):
                        pe.wait_ge(s_g[half(q)], landed(q, 2))
                        wait(pe, s_tc, ev(q))
                        transposed(q, 0, msg, psT[0], s_ta)
                        transposed(q, 1, own, psT[1], s_t)
                    b = sh(q, -1)
                    if inside(b, 0, FIX - 1):
                        pe.wait_ge(s_tc, ev(b, 1, 1))
                        wait(pe, s_h, ev(b))
                        product(b, 0, W3, psY, s_ya)
                        for j in range(ntiles(b)):
                            for k, weights in enumerate((Was, Wad)):
                                for a in range(KB):
                                    last = T.matmul(psE[:, j, :], tT[:, b[1] % 2, k, a, j, :], weights[:, a, :],
                                                    start=(k == 0 and a == 0), stop=(k == 1 and a == KB - 1))
                        last.then_inc(s_y, 1)

                chunks(pe, step, FIX)

            @block.scalar
            def _(act):
                def step(q):
                    n = ntiles(q)
                    act.wait_ge(s_t, ev(q, 1, 1))
                    wait(act, s_y, ev(q, 1, -1))
                    for k in range(2):
                        last = A.activation(tT[:, q[1] % 2, k, :, 0:n, :], psT[k][:, :, 0:n, :], ACT.Copy)
                    last.then_inc(s_tc, 1)

                chunks(act, step, FIX - 1)

            @block.vector
            def _(dve):
                def step(q):
                    n, h, j0 = ntiles(q), half(q), q[1] % 2 * 4
                    dve.wait_ge(s_y, ev(q, 1, 1))
                    wait(dve, s_lin[h], stored(q))
                    V.tensor_copy(tot[:, h, j0:j0 + n, :], psY[:, 0:n, :])
                    V.tensor_copy(score[:, bass.ds(tile0(q), n), :], psE[:, 0:n, :]).then_inc(s_h, 1)

                chunks(dve, step, FIX - 1)

            @block.sync
            def _(sp):
                chunks(sp, lambda q: store(sp, h3, tot, q, s_h, s_spgo, s_lin[half(q)]), FIX - 1)
                for k in range(NH):
                    sp.wait_ge(s_lin[k], 32 * GI)

        edge_scope.close()

        with phase() as scope:
            eh = sb("eh", [P, HEADS, EC], F32, scope)
            fwd = sb("fwd", [P, HEADS, TOTAL], F32, scope)
            bwd = sb("bwd", [P, HEADS, EC], F32, scope)
            pf = sb("pf", [P, 2, EC], F32, scope)
            pbk = sb("pbk", [P, 2, EC], F32, scope)
            dg = sb("dg", [P, 2, HEADS, P], F32, scope)
            cr = sb("cr", [P, 2, HEADS, P], F32, scope)
            edge_in = sb("edge_in", [P, 2, HEADS], F32, scope)
            ends = sb("ends", [P, HEADS], F32, scope)
            psC = [pb(f"s3_psC{k}", [P, HEADS, P], F32, scope) for k in range(2)]
            psD = pb("s3_psD", [P, HEADS], F32, scope)
            s_c, s_dg3, s_cr, s_sub, s_ex, s_tl, s_dn = (sem(f"s3_{n}") for n in ("c", "dg", "cr", "sub", "ex", "tl", "dn"))
            block = scope.enter_context(nc.Block())

            @block.tensor
            def _(pe):
                pe.wait_ge(s_dg3, 1)
                for k in range(2):
                    for a in range(2):
                        last = T.matmul(psC[k][:, 4 * a:4 * a + 4, :], ones[:, :], dg[:, k, 4 * a:4 * a + 4, :], start=True, stop=True)
                last.then_inc(s_cr, 1)
                pe.wait_ge(s_tl, 1)
                T.matmul(psD[:, :], feeds[1][:, :], ends[:, :], start=True, stop=True).then_inc(s_dn, 1)

            @block.scalar
            def _(act):
                act.wait_ge(s_sub, 1)
                A.activation(eh[:, :, :], eh[:, :, :], ACT.Exp).then_inc(s_ex, 1)

            @block.vector
            def _(dve):
                chain = [0]

                def link(ins):
                    chain[0] += 1
                    ins.then_inc(s_c, 1)
                    dve.wait_ge(s_c, chain[0])

                link(V.scalar_tensor_tensor(out=eh[:, :, :], in0=score[:, :, :].rearrange("p t h -> p h t"), scalar=0.2,
                                            in1=score[:, :, :].rearrange("p t h -> p h t"), op0=ALU.mult, op1=ALU.max))
                for k, of in ((0, go_on[1]), (1, whole[1])):
                    link(V.tensor_scalar(pf[:, k, :], of[:, :], 1.0, 1e30, ALU.subtract, ALU.mult))
                link(V.tensor_scalar(pbk[:, 1, :], on_next[:, :], 1.0, 1e30, ALU.subtract, ALU.mult))
                link(V.tensor_copy(pbk[:, 0, :], pbk[:, 1, :]))
                link(V.memset(pbk[:, 0, EC - 1:EC], -1e30))
                for hd in range(HEADS):
                    V.tensor_tensor_scan(fwd[:, hd, 0:EC], pf[:, 0, :], eh[:, hd, :], -1e30, ALU.add, ALU.max)
                    last = V.tensor_tensor_scan(bwd[:, hd, ::-1], pbk[:, 0, ::-1], eh[:, hd, ::-1], -1e30, ALU.add, ALU.max)
                link(last)
                for hd in range(HEADS):
                    V.tensor_scalar(dg[:, 0, hd, :], ident[:, :], fwd[:, hd, EC - 1:EC], None, ALU.mult)
                    last = V.tensor_scalar(dg[:, 1, hd, :], ident[:, :], bwd[:, hd, 0:1], None, ALU.mult)
                last.then_inc(s_dg3, 1)
                dve.wait_ge(s_cr, 1)
                for k, pen in ((0, pen_f), (1, pen_b)):
                    link(V.tensor_tensor(cr[:, k, :, :], psC[k][:, :, :], pen[:, :].unsqueeze(1).broadcast_to([P, HEADS, P]), ALU.add))
                    link(V.tensor_reduce(edge_in[:, k, :], cr[:, k, :, :], AX_X, ALU.max))
                for hd in range(HEADS):
                    V.tensor_tensor_scan(fwd[:, hd, 0:EC], pf[:, 1, :], eh[:, hd, :], edge_in[:, 0, hd:hd + 1], ALU.add, ALU.max)
                    last = V.tensor_tensor_scan(bwd[:, hd, ::-1], pbk[:, 1, ::-1], eh[:, hd, ::-1], edge_in[:, 1, hd:hd + 1],
                                                ALU.add, ALU.max)
                link(last)
                link(V.tensor_tensor(bwd[:, :, :], fwd[:, :, 0:EC], bwd[:, :, :], ALU.max))
                V.tensor_tensor(eh[:, :, :], eh[:, :, :], bwd[:, :, :], ALU.subtract).then_inc(s_sub, 1)
                dve.wait_ge(s_ex, 1)
                link(V.tensor_copy(attend[:, :, :], eh[:, :, :].rearrange("p h t -> p t h")))
                for hd in range(HEADS):
                    last = V.tensor_tensor_scan(fwd[:, hd, 0:EC], go_on[1][:, :], eh[:, hd, :], 0.0, ALU.mult, ALU.add)
                link(last)
                V.tensor_copy(ends[:, :], fwd[:, :, EC - 1]).then_inc(s_tl, 1)
                dve.wait_ge(s_dn, 1)
                link(V.tensor_copy(edge_in[:, 0, :], psD[:, :]))
                for hd in range(HEADS):
                    last = V.tensor_tensor_scan(fwd[:, hd, 0:EC], whole[1][:, :], eh[:, hd, :], edge_in[:, 0, hd:hd + 1],
                                                ALU.mult, ALU.add)
                link(last)
                link(V.tensor_tensor(bwd[:, :, :], fwd[:, :, 0:EC], leadend[1][:, :].unsqueeze(1).broadcast_to([P, HEADS, EC]), ALU.mult))
                link(V.tensor_reduce(fwd[:, :, EC], bwd[:, :, :], AX_X, ALU.add))
                link(V.tensor_scalar(ends[:, :], valid[:, EC:EC + 1].broadcast_to([P, HEADS]), -1.0, 1.0, ALU.mult, ALU.add))
                link(V.tensor_tensor(fwd[:, :, EC], fwd[:, :, EC], ends[:, :], ALU.add))
                link(V.tensor_scalar(fwd[:, :, :], fwd[:, :, :], 1e-16, None, ALU.add))
                link(V.reciprocal(fwd[:, :, :], fwd[:, :, :]))
                link(V.tensor_copy(rden[:, :, :], fwd[:, :, :].rearrange("p h t -> p t h")))

        msg, own, tot, tT, o4 = edge_buffers(ctx, "d")
        with phase() as scope:
            psF = pb("e3b_psF", [P, D], F32, scope)[:, :]
            (s_pk, s_go, s_vgo, s_spgo, s_scaled, s_acc, s_led, s_sum, s_fix, s_o, s_add, s_bn, s_mv, s_sd, s_rs, s_nm, s_norm) = (
                sem(f"e3b_{n}") for n in ("pk", "go", "vgo", "spgo", "scaled", "acc", "led", "sum", "fix", "o", "add", "bn", "mv",
                                          "sd", "rs", "nm", "norm"))
            s_hin = [sem(f"e3b_h{k}") for k in range(NH)]
            s_own = [sem(f"e3b_own{k}") for k in range(NH)]
            s_sc = [sem(f"e3b_sc{k}") for k in range(NH)]
            block = scope.enter_context(nc.Block())

            def by_head(a):
                return a.rearrange("p n (h d) -> p n h d", d=HD)

            @block.sync
            def _(sp):
                def step(g):
                    h = slot(g)
                    frees = ((s_sc[h], nth(g, 16 * GT)), (s_acc, ev(g, GT, 1 - (NH - 1) * GT)),
                             (s_led, ev(g, 2, 2 - CB)), (s_o, ev(g, 4, 4 - 2 * CB)))
                    if group_tiles(g) == GT:
                        load_group(sp, g, ((h3, msg),), s_hin, s_spgo, frees)
                    load_group(sp, g, ((x3e, own),), s_own, s_spgo, frees)

                groups(sp, step, NG)

            @block.gpsimd
            def _(pool):
                def weigh(q):
                    n, t0 = ntiles(q), tile0(q)
                    pool.wait_ge(s_hin[half(q)], loads(q))
                    pool.sem_inc(s_go, 1)
                    m = by_head(chunk_of(msg, q))
                    pool.tensor_tensor(m, m, attend[:, bass.ds(t0, n), :].unsqueeze(3).broadcast_to([P, n, HEADS, HD]),
                                       ALU.mult).then_inc(s_scaled, 1)

                def step(g):
                    if inside(g, 0, NG - 1):
                        for k in range(2):
                            weigh((g[0], 2 * g[1] + k, CB))
                    b = sh(g, -2)
                    if inside(b, 0, NG):
                        wait(pool, s_sc[slot(b)], nth(b, 16 * GT))
                        indices(pool, 1, b, s_pk, s_go)
                        pool.wait_ge(s_norm, FIX + 1 if group_tiles(b) == 1 else ev(b, 2, 2))
                        pool.sem_inc(s_go, 1)
                        scatter_rows(pool, out, slot(b), group_tiles(b), s_sc[slot(b)])

                groups(pool, step, NG + 2)
                for k in range(NH):
                    pool.wait_ge(s_sc[k], 16 * (GI * GT + (k == 0)))

            @block.tensor
            def _(pe):
                def step(q):
                    if is_fix(q):
                        pe.wait_ge(s_acc, EC - 1)
                        T.matmul(psF, feeds[1][:, :], msg[:, NH - 1, GT - 1, :], start=False, stop=True).then_inc(s_fix, 1)
                        return
                    pe.wait_ge(s_led, ev(q, 1, 1))
                    for j in range(ntiles(q)):
                        last = T.matmul(psF, ident[:, :], tot[:, half(q), q[1] % 2 * 4 + j, :],
                                        start=q[0] is None and q[1] == 0 and j == 0, stop=False)
                    last.then_inc(s_sum, 1)

                chunks(pe, step, FIX)

            @block.scalar
            def _(act):
                def step(q):
                    if inside(q, 0, FIX - 1):
                        n, h, j0, t0 = ntiles(q), half(q), q[1] % 2 * 4, tile0(q)
                        act.wait_ge(s_acc, t0 + (n - 1))
                        wait(act, s_sum, ev(q, 1, 1 - CB))
                        for j in range(n):
                            last = A.activation(tot[:, h, j0 + j, :], msg[:, h, j0 + j, :], ACT.Copy,
                                                scale=leadend[1][:, bass.ds(t0 + j, 1)])
                        last.then_inc(s_led, 1)
                    b = sh(q, -1)
                    if inside(b, 0, FIX):
                        deviation(0, b, s_mv, s_sd)
                    if inside(sh(q, -2), 0, FIX):
                        normalise(0, sh(q, -2), own_row, s_nm, s_norm)

                chunks(act, step, FIX + 2)

            @block.vector
            def _(dve):
                def step(q):
                    if inside(q, 0, FIX):
                        n, h, t0 = ntiles(q), half(q), tile0(q)
                        accumulate(q, 1, psF, s_scaled, ev(q, 1, 1), s_acc, None, s_fix)
                        wait(dve, s_acc, t0 + (n - 1))
                        b = sh(q, -2)
                        if inside(b, 0, FIX):
                            reciprocals(0, b, s_sd, s_rs, s_nm)
                        oq = o4[:, q[1] % 2, 0:n, :]
                        V.tensor_tensor(by_head(oq), by_head(chunk_of(msg, q)),
                                        rden[:, bass.ds(t0, n), :].unsqueeze(3).broadcast_to([P, n, HEADS, HD]),
                                        ALU.mult).then_inc(s_o, 1)
                        dve.wait_ge(s_o, ev(q, 2, 1))
                        V.tensor_tensor(oq, oq, over(B3, n), ALU.add).then_inc(s_o, 1)
                        dve.wait_ge(s_o, ev(q, 2, 2))
                        dve.wait_ge(s_own[h], loads(q))
                        V.scalar_tensor_tensor(out=chunk_of(own, q), in0=oq, scalar=0.0, in1=chunk_of(own, q),
                                               op0=ALU.max, op1=ALU.add).then_inc(s_add, 1)
                        statistics(0, q, own_row, s_add, s_bn, s_vgo, s_mv)
                    else:
                        reciprocals(0, sh(q, -2), s_sd, s_rs, s_nm)

                chunks(dve, step, FIX + 2)


_INS = ["x", "src", "dst", "edge_weight", "L0_gnn_W", "L1_gnn_W", "L1_gnn_b", "L1_gnn_ln_gamma", "L1_gnn_ln_beta",
        "L1_gnn_res_W", "L1_gnn_res_b", "L2_gnn_W", "L2_gnn_b", "L2_gnn_gamma", "L2_gnn_beta", "L3_gnn_W",
        "L3_gnn_att_src", "L3_gnn_att_dst", "L3_gnn_bias"]


def kernel(**inputs):
    import numpy as np
    import concourse.bacc as bacc
    from concourse.bass_utils import run_bass_kernel_spmd

    nc = bacc.Bacc("TRN2", target_bir_lowering=False, num_devices=1)
    arrays, args = {}, []
    for name in _INS:
        a = np.ascontiguousarray(inputs[name])
        arrays[f"in_{name}"] = a
        args.append(nc.dram_tensor(f"in_{name}", a.shape, mybir.dt.from_np(a.dtype), kind="ExternalInput").ap())
    args.append(nc.dram_tensor("out_0", (N, D), F32, kind="ExternalOutput").ap())
    build(nc, *args)
    r = run_bass_kernel_spmd(nc, [arrays], core_ids=[0])
    return r.results[0]["out_0"]
```
